# Optimizing a Trainium2 kernel written in Bass

```python
import numpy as np
import jax
import jax.numpy as jnp

def _softmax(x, axis=-1):
    return jax.nn.softmax(x, axis=axis)

def _gelu(x):
    return jax.nn.gelu(x, approximate=True)

def _silu(x):
    return jax.nn.silu(x)

def _sigmoid(x):
    return jax.nn.sigmoid(x)

def _layernorm(x, axis=-1, eps=1e-05):
    m = jnp.mean(x, axis=axis, keepdims=True)
    v = jnp.var(x, axis=axis, keepdims=True)
    return (x - m) / jnp.sqrt(v + eps)

def _scatter_add(tgt, idx, src, axis=0):
    return tgt.at[idx].add(src)

def _segment_sum(src, seg, n):
    return jax.ops.segment_sum(src, seg, n)
kernel_name = 'mk_gnn_resnorm_d4_gnn_r32_f600a6'

def setup_inputs(seed: int=0):
    np.random.seed(seed)
    _w = jnp.asarray

    def _rec_inputs():
        import jax
        import jax.numpy as jnp
        _gk = jax.random.key(seed)
        x = -0.000202 + 1 * jax.random.normal(jax.random.fold_in(_gk, 1), (3125, 64), jnp.float32)
        src = jax.random.randint(jax.random.fold_in(_gk, 2), (100000,), 0, 3125, jnp.int32)
        dst = jnp.minimum((3125 * jax.random.uniform(jax.random.fold_in(_gk, 3), (100000,)) ** 2.0).astype(jnp.int32), 99999)
        _o = jnp.argsort(dst, stable=True)
        src = src[_o]
        dst = dst[_o]
        edge_attr_64 = 1.36993e-05 + 0.999972 * jax.random.normal(jax.random.fold_in(_gk, 12), (100000, 64), jnp.float32)
        edge_attr_9 = 0.000739051 + 0.999958 * jax.random.normal(jax.random.fold_in(_gk, 13), (100000, 9), jnp.float32)
        edge_type_8 = jax.random.randint(jax.random.fold_in(_gk, 15), (100000,), 0, 8, jnp.int32)
        edge_weight = jax.random.uniform(jax.random.fold_in(_gk, 16), (100000,), jnp.float32, 0.0, 1)
        return (x, src, dst, edge_attr_64, edge_attr_9, edge_type_8, edge_weight)
    x, src, dst, edge_attr_64, edge_attr_9, edge_type_8, edge_weight = _rec_inputs()

    def _L0_gnn_setup():
        import jax, jax.numpy as jnp
        import numpy as np
        N_NODES = 3125
        N_EDGES = 100000
        N_RELS = 8
        F_IN = 64
        F_OUT = 64
        key = jax.random.key(seed)
        k1, k2, k3, k4, k5, k6 = jax.random.split(key, 6)
        X = jax.random.normal(k1, (N_NODES, F_IN), dtype=jnp.float32)
        W = jax.random.normal(k2, (N_RELS, F_IN, F_OUT), dtype=jnp.float32) * 0.1
        A = jax.random.uniform(k3, (N_EDGES,), dtype=jnp.float32)
        src = jax.random.randint(k4, (N_EDGES,), 0, N_NODES, dtype=jnp.int32)
        dst = jax.random.randint(k5, (N_EDGES,), 0, N_NODES, dtype=jnp.int32)
        etype = jax.random.randint(k6, (N_EDGES,), 0, N_RELS, dtype=jnp.int32)
        return {'X': X, 'W': W, 'A': A, 'src': src, 'dst': dst, 'etype': etype}
    _L0_gnn_all = _L0_gnn_setup()
    _L0_gnn_in = {k: v for k, v in _L0_gnn_all.items() if k in ('W',)}
    del _L0_gnn_all

    def _L1_gnn_setup():
        import jax, jax.numpy as jnp
        import numpy as np
        N, D, H, E = (50000, 64, 4, 25000)
        key = jax.random.key(seed)
        k1, k2, k3, k4, k5 = jax.random.split(key, 5)
        inputs = jax.random.normal(k1, (N, D), dtype=jnp.float32)
        Wh = jax.random.normal(k2, (H, D, D), dtype=jnp.float32) * (1.414 / np.sqrt(D))
        weight = jax.random.normal(k3, (H * D, D), dtype=jnp.float32) * (1.414 / np.sqrt(H * D))
        src = jax.random.randint(k4, (E,), 0, N, dtype=jnp.int64)
        dst = jax.random.randint(k5, (E,), 0, N, dtype=jnp.int64)
        return {'inputs': inputs, 'Wh': Wh, 'weight': weight, 'src': src, 'dst': dst}
    _L1_gnn_all = _L1_gnn_setup()
    _L1_gnn_in = {k: v for k, v in _L1_gnn_all.items() if k in ('Wh', 'weight')}
    del _L1_gnn_all

    def _L2_gnn_setup():
        import jax, jax.numpy as jnp
        import numpy as np
        N, E = (10000, 10000)
        D, S, HE = (64, 9, 64)
        H, DQK, DV = (8, 16, 16)
        OK, OV = (H * DQK, H * DV)
        EPS_BN = 1e-05

        def tensor_product(x_e, sh, w, C):
            acc = sh[:, 0:1] * (x_e @ C[:, 0, :])
            for s in range(1, S):
                acc = acc + sh[:, s:s + 1] * (x_e @ C[:, s, :])
            return acc * w

        def mlp2(x, w1, b1, w2, b2):
            return jax.nn.relu(x @ w1 + b1) @ w2 + b2
        key = jax.random.key(seed)
        ks = jax.random.split(key, 20)
        g = lambda k, shape, fan: jax.random.normal(k, shape, jnp.float32) / np.float32(np.sqrt(fan))
        return {'tfn_features': jax.random.normal(ks[0], (N, D), jnp.float32), 'edge_features': jax.random.normal(ks[1], (E, HE), jnp.float32), 'edge_sh': jax.random.normal(ks[2], (E, S), jnp.float32), 'Wq': g(ks[3], (D, OK), D), 'Cqk': g(ks[4], (D, S, OK), D * S), 'Cv': g(ks[5], (D, S, OV), D * S), 'k_w1': g(ks[6], (HE, HE), HE), 'k_b1': jnp.zeros((HE,), jnp.float32), 'k_w2': g(ks[7], (HE, OK), HE), 'k_b2': jnp.zeros((OK,), jnp.float32), 'v_w1': g(ks[8], (HE, HE), HE), 'v_b1': jnp.zeros((HE,), jnp.float32), 'v_w2': g(ks[9], (HE, OV), HE), 'v_b2': jnp.zeros((OV,), jnp.float32), 'W_out': g(ks[10], (OV, D), OV), 'W_self': g(ks[11], (D, D), D), 'gamma': jnp.ones((D,), jnp.float32), 'beta': jnp.zeros((D,), jnp.float32), 'edge_index': jax.random.randint(ks[12], (2, E), 0, N, dtype=jnp.int32)}
    _L2_gnn_all = _L2_gnn_setup()
    _L2_gnn_in = {k: v for k, v in _L2_gnn_all.items() if k in ('Wq', 'Cqk', 'Cv', 'k_w1', 'k_b1', 'k_w2', 'k_b2', 'v_w1', 'v_b1', 'v_w2', 'v_b2', 'W_out', 'W_self', 'gamma', 'beta')}
    del _L2_gnn_all

    def _L3_gnn_setup():
        import jax, jax.numpy as jnp
        import numpy as np
        N_NODES = 50000
        N_EDGES = 25000
        D_IN = 64
        D_OUT = 64
        key = jax.random.key(seed)
        k1, k2, k3, k4 = jax.random.split(key, 4)
        x = jax.random.normal(k1, (N_NODES, D_IN), dtype=jnp.float32)
        edge_index = jax.random.randint(k2, (2, N_EDGES), 0, N_NODES, dtype=jnp.int64)
        lim = 1.0 / np.sqrt(D_IN)
        W = jax.random.uniform(k3, (D_OUT, D_IN), dtype=jnp.float32, minval=-lim, maxval=lim)
        b = jax.random.uniform(k4, (D_OUT,), dtype=jnp.float32, minval=-lim, maxval=lim)
        return {'x': x, 'edge_index': edge_index, 'W': W, 'b': b}
    _L3_gnn_all = _L3_gnn_setup()
    _L3_gnn_in = {k: v for k, v in _L3_gnn_all.items() if k in ('W', 'b')}
    del _L3_gnn_all
    return {'x': x, 'src': src, 'dst': dst, 'edge_attr_64': edge_attr_64, 'edge_attr_9': edge_attr_9, 'edge_type_8': edge_type_8, 'edge_weight': edge_weight, 'L0_gnn_W': _L0_gnn_in['W'], 'L1_gnn_Wh': _L1_gnn_in['Wh'], 'L1_gnn_weight': _L1_gnn_in['weight'], 'L2_gnn_Wq': _L2_gnn_in['Wq'], 'L2_gnn_Cqk': _L2_gnn_in['Cqk'], 'L2_gnn_Cv': _L2_gnn_in['Cv'], 'L2_gnn_k_w1': _L2_gnn_in['k_w1'], 'L2_gnn_k_b1': _L2_gnn_in['k_b1'], 'L2_gnn_k_w2': _L2_gnn_in['k_w2'], 'L2_gnn_k_b2': _L2_gnn_in['k_b2'], 'L2_gnn_v_w1': _L2_gnn_in['v_w1'], 'L2_gnn_v_b1': _L2_gnn_in['v_b1'], 'L2_gnn_v_w2': _L2_gnn_in['v_w2'], 'L2_gnn_v_b2': _L2_gnn_in['v_b2'], 'L2_gnn_W_out': _L2_gnn_in['W_out'], 'L2_gnn_W_self': _L2_gnn_in['W_self'], 'L2_gnn_gamma': _L2_gnn_in['gamma'], 'L2_gnn_beta': _L2_gnn_in['beta'], 'L3_gnn_W': _L3_gnn_in['W'], 'L3_gnn_b': _L3_gnn_in['b']}

def reference(x, src, dst, edge_attr_64, edge_attr_9, edge_type_8, edge_weight, L0_gnn_W, L1_gnn_Wh, L1_gnn_weight, L2_gnn_Wq, L2_gnn_Cqk, L2_gnn_Cv, L2_gnn_k_w1, L2_gnn_k_b1, L2_gnn_k_w2, L2_gnn_k_b2, L2_gnn_v_w1, L2_gnn_v_b1, L2_gnn_v_w2, L2_gnn_v_b2, L2_gnn_W_out, L2_gnn_W_self, L2_gnn_gamma, L2_gnn_beta, L3_gnn_W, L3_gnn_b):
    import jax
    import jax.numpy as jnp

    def _L0_gnn_ref(X, W, A, src, dst, etype):
        import jax, jax.numpy as jnp
        import numpy as np
        N_NODES = 3125
        N_EDGES = 100000
        N_RELS = 8
        F_IN = 64
        F_OUT = 64
        XW = jnp.einsum('nf,rfo->rno', X, W)
        msg = XW[etype, src] * A[:, None]
        Y = jax.ops.segment_sum(msg, dst, num_segments=X.shape[0])
        return Y

    def _L1_gnn_ref(inputs, Wh, weight, src, dst):
        import jax, jax.numpy as jnp
        import numpy as np
        N, D, H, E = (50000, 64, 4, 25000)
        n, d = inputs.shape
        h = inputs
        a = jnp.einsum('nd,hde->nhe', h, Wh)
        scores = jnp.sum(a * h[:, None, :], axis=-1) / jnp.sqrt(jnp.asarray(d, h.dtype))
        attn = jax.nn.softmax(scores, axis=0)
        msg = h[src][:, None, :] * attn[src][:, :, None]
        neigh = jax.ops.segment_sum(msg, dst, num_segments=n)
        out = neigh.reshape(n, -1) @ weight
        return jax.nn.elu(out)

    def _L2_gnn_ref(tfn_features, edge_features, edge_sh, Wq, Cqk, Cv, k_w1, k_b1, k_w2, k_b2, v_w1, v_b1, v_w2, v_b2, W_out, W_self, gamma, beta, edge_index):
        import jax, jax.numpy as jnp
        import numpy as np
        N, E = (10000, 10000)
        D, S, HE = (64, 9, 64)
        H, DQK, DV = (8, 16, 16)
        OK, OV = (H * DQK, H * DV)
        EPS_BN = 1e-05

        def tensor_product(x_e, sh, w, C):
            acc = sh[:, 0:1] * (x_e @ C[:, 0, :])
            for s in range(1, S):
                acc = acc + sh[:, s:s + 1] * (x_e @ C[:, s, :])
            return acc * w

        def mlp2(x, w1, b1, w2, b2):
            return jax.nn.relu(x @ w1 + b1) @ w2 + b2
        edge_dst, edge_src = (edge_index[0], edge_index[1])
        n = tfn_features.shape[0]
        q = (tfn_features @ Wq).reshape(n, H, DQK)
        x_dst = tfn_features[edge_dst]
        wk = mlp2(edge_features, k_w1, k_b1, k_w2, k_b2)
        wv = mlp2(edge_features, v_w1, v_b1, v_w2, v_b2)
        k = tensor_product(x_dst, edge_sh, wk, Cqk).reshape(-1, H, DQK)
        v = tensor_product(x_dst, edge_sh, wv, Cv).reshape(-1, H, DV)
        attn = jnp.einsum('ehd,ehd->eh', q[edge_src], k)
        amax = jax.ops.segment_max(attn, edge_src, num_segments=n)
        ex = jnp.exp(attn - amax[edge_src])
        denom = jax.ops.segment_sum(ex, edge_src, num_segments=n)
        alpha = ex / (denom[edge_src] + 1e-16)
        upd = jax.ops.segment_sum(v * alpha[..., None], edge_src, num_segments=n)
        upd = upd.reshape(n, OV) @ W_out
        out = tfn_features @ W_self + upd
        mu = out.mean(axis=0)
        var = out.var(axis=0)
        return (out - mu) * jax.lax.rsqrt(var + EPS_BN) * gamma + beta

    def _L3_gnn_ref(x, edge_index, W, b):
        import jax, jax.numpy as jnp
        import numpy as np
        N_NODES = 50000
        N_EDGES = 25000
        D_IN = 64
        D_OUT = 64
        N = x.shape[0]
        loops = jnp.arange(N, dtype=edge_index.dtype)
        ei = jnp.concatenate([edge_index, jnp.stack([loops, loops], axis=0)], axis=1)
        row, col = (ei[0], ei[1])
        h = x @ W.T + b
        deg = jax.ops.segment_sum(jnp.ones(row.shape, dtype=h.dtype), row, num_segments=N)
        dinv = deg ** (-0.5)
        norm = dinv[row] * dinv[col]
        msg = norm[:, None] * h[col]
        return jax.ops.segment_sum(msg, row, num_segments=N)
    edge_index = jnp.stack([src, dst])
    x = _layernorm(x + _L0_gnn_ref(x, L0_gnn_W, edge_weight, src, dst, edge_type_8), axis=-1)
    x = _layernorm(x + _L1_gnn_ref(x, L1_gnn_Wh, L1_gnn_weight, src, dst), axis=-1)
    x = _layernorm(x + _L2_gnn_ref(x, edge_attr_64, edge_attr_9, L2_gnn_Wq, L2_gnn_Cqk, L2_gnn_Cv, L2_gnn_k_w1, L2_gnn_k_b1, L2_gnn_k_w2, L2_gnn_k_b2, L2_gnn_v_w1, L2_gnn_v_b1, L2_gnn_v_w2, L2_gnn_v_b2, L2_gnn_W_out, L2_gnn_W_self, L2_gnn_gamma, L2_gnn_beta, edge_index), axis=-1)
    x = _layernorm(x + _L3_gnn_ref(x, edge_index, L3_gnn_W, L3_gnn_b), axis=-1)
    return x

_drawn_inputs = setup_inputs


def setup_inputs(seed=0):
    import zlib

    import numpy as np

    out = dict(_drawn_inputs(seed))
    spreads = {'L2_gnn_k_b1': (0.0, 0.1),
     'L2_gnn_k_b2': (0.0, 0.1),
     'L2_gnn_v_b1': (0.0, 0.1),
     'L2_gnn_v_b2': (0.0, 0.1),
     'L2_gnn_gamma': (1.0, 0.2),
     'L2_gnn_beta': (0.0, 0.1)}
    factors = {'L1_gnn_Wh': 7.042, 'L1_gnn_weight': 6.06}
    for name, (base, spread) in spreads.items():
        noise = np.random.default_rng([zlib.crc32(name.encode()), seed]).standard_normal(out[name].shape)
        drawn = base * np.exp(spread * noise) if base else spread * noise
        out[name] = jnp.asarray(drawn.astype(out[name].dtype))
    for name, factor in factors.items():
        out[name] = (out[name] * factor).astype(out[name].dtype)
    return out
```

```python
from contextlib import ExitStack

import numpy as np

import concourse.bass as bass
from concourse import mybir

RMAX = bass.bass_isa.ReduceOp.max
RADD = bass.bass_isa.ReduceOp.add
P = 128
N = 3125
E = 100000
D = 64
R = 8
H1 = 4
S9 = 9
OK = 128
H2 = 8
NW = -(-N // P)
NP = NW * P
LAST = N - (NW - 1) * P
NT = 784
U = 4
REAL_TILES = -(-E // P)
NB = (REAL_TILES + NW - 1 + NW * (U - 1)) // U
NS = NB * U
NBLK = -(-NS // P)
NSP = NBLK * P
CENTRE = 1562
BIG = 1.0e38
SCP = NB // 2
SCL = NS // SCP * P
VW = OK + H2
XC = 5


def build(nc, A, out_dram, dump=None):
    f32, i32, bf16, f16 = mybir.dt.float32, mybir.dt.int32, mybir.dt.bfloat16, mybir.dt.float16
    ALU = mybir.AluOpType
    ACT = mybir.ActivationFunctionType
    AX = mybir.AxisListType
    ds = bass.ds
    ctx = ExitStack()
    with ctx:
        def sb(name, shape, dt=f32):
            return ctx.enter_context(nc.sbuf_tensor(name, shape, dt))

        def sem(name):
            return ctx.enter_context(nc.semaphore(name))

        def dram(name, shape, dt=f32):
            return nc.dram_tensor(name, shape, dt, kind="Internal").ap()

        d_rel = dram("d_valid_dst", (NSP, P))
        d_tile = dram("d_slot_tile", (NSP,), i32)
        d_xw = dram("d_xw", (NP * R, D))
        d_adj = dram("d_adj", (NW, P, N))
        d_x = dram("d_x", (NP, D))
        d_q = dram("d_q", (NP, OK))
        d_v = dram("d_v", (NS, P, OK))
        d_lg = dram("d_logits", (NS, H2, P))
        d_ex = dram("d_exps", (NS, H2, P))

        ident = sb("ident", [P, P])
        ones = sb("ones", [P, P])
        iota128 = sb("iota128", [P, P])
        pcol = sb("pcol", [P, 1])
        realrow = sb("realrow", [P, 1])
        rel_t = sb("rel_t", [P, NSP])
        srcc_t = sb("srcc_t", [P, NSP])
        w_t = sb("w_t", [P, NSP])
        src_t = sb("src_t", [P, NSP], i32)
        xwi_t = sb("xwi_t", [P, NSP], i32)
        dst_t = sb("dst_t", [P, NSP], i32)
        blk_i = sb("blk_i", [P, NW + 1], i32)
        tile_row = sb("tile_row", [1, NSP], i32)
        x = sb("x", [P, NW, D])
        agg = sb("agg", [P, NW, D])
        t1 = sb("t1", [P, NW, D])
        t2 = sb("t2", [P, NW, D])
        st = sb("st", [P, 8, NW])
        xT = sb("xT", [D, NP])
        dinv = sb("dinv", [P, NW])
        deg = sb("deg", [P, NW])
        small = sb("small", [P, 64])

        w0 = sb("w0", [D, R, D])
        w1 = sb("w1", [D, 2, H1, D])
        w2n = sb("w2n", [D, OK + D])
        wout = sb("wout", [P, D])
        w3 = sb("w3", [D, D])
        w3T = sb("w3T", [D, D])
        gam = sb("gam", [P, 3, D])

        ps = ctx.enter_context(nc.psum_tensor("ps", [P, 8, 512], f32))
        psf = ps[:, :, :].rearrange("p b c -> p (b c)")

        phase = sem("phase")
        lk = {e: sem(f"chain_{e}") for e in ("dve", "act", "pool")}
        lkn = {"dve": 0, "act": 0, "pool": 0}

        def link(eng, name, ins):
            lkn[name] += 1
            ins.then_inc(lk[name], 1)
            eng.wait_ge(lk[name], lkn[name])

        def barrier(eng, n):
            eng.drain().then_inc(phase, 1)
            eng.wait_ge(phase, 5 * n)

        sems = {}

        def S(name):
            if name not in sems:
                sems[name] = sem(name)
            return sems[name]

        tick = sem("tick")

        agg_f = agg[:, :, :].rearrange("p w d -> p (w d)")

        def hold(eng):
            eng.sem_inc(tick, 1)

        AREA = 24576
        area = sb("area", [P, AREA])

        class Cut:
            def __init__(self):
                self.at = 0

            def take(self, cols, rows=P, dt=f32):
                words = cols if dt in (f32, i32) else -(-cols // 2)
                v = area[0:rows, self.at:self.at + words]
                self.at += -(-words // 8) * 8
                assert self.at <= AREA, self.at
                return v if dt == f32 else v.bitcast(dt)[:, 0:cols]

        c = Cut()
        p1_dst_i = c.take(NT, dt=i32)
        p1_dst = c.take(NT)
        p1_lt = c.take(NT)
        p1_cnt = c.take(32)
        p1_bi = c.take(32, dt=i32)
        p1_te = c.take(32)
        p1_ts = c.take(32)
        p1_nb = c.take(32)
        p1_nbi = c.take(32, dt=i32)
        p1_cum = c.take(32)
        p1_sb = c.take(32)
        p1_off = c.take(32)
        p1_doff = c.take(32)
        p1_i = c.take(NBLK)
        p1_mask = c.take(NBLK * 24)
        p1_mo = c.take(NBLK * 24)
        p1_w = c.take(NBLK)
        p1_o = c.take(NBLK)
        p1_t = c.take(NBLK)
        p1_ti = c.take(NBLK, dt=i32)
        p1_g = {n: c.take(NSP, dt=(f32 if n == "wgt" else i32)) for n in ("dst", "src", "typ", "wgt")}
        p1_f = c.take(NSP)
        p1_a = c.take(NSP)
        p1_b = c.take(NSP)
        p1_rel = c.take(NSP)
        p1_dv = c.take(NSP)
        p1_q = c.take(NSP)
        p1_s = c.take(NSP)
        p1_x = c.take(NSP)

        c = Cut()
        c.at = 20000
        p2_o = [c.take(R * D) for _ in range(2)]

        c = Cut()
        p3_idx = [c.take(U, dt=i32) for _ in range(2)]
        p3_msg = [c.take(D) for _ in range(U)]
        p3_iota = c.take(N, dt=f16)
        p3_ohs = [c.take(N, dt=bf16) for _ in range(U)]
        p3_ohd = [c.take(P, dt=bf16) for _ in range(U)]
        p3_ohw = [c.take(P) for _ in range(U)]
        p3_z = c.take(512, dt=bf16)
        p3_ev = c.take(N)

        c = Cut()
        p5_hw = c.take(NW * H1 * D)
        p5_pr = [c.take(H1 * D) for _ in range(2)]
        p5_s = c.take(NW * H1)
        p5_e = c.take(NW * H1)
        p5_m = c.take(H1)
        p5_mm = c.take(H1)
        p5_z = c.take(H1)
        p5_zz = c.take(H1)
        p5_ri = c.take(H1)
        p5_zt = c.take(NW * D)
        p5_adj = [c.take(NP) for _ in range(2)]
        p5_at = c.take(NP)

        c = Cut()
        p8_qo = [c.take(OK + D) for _ in range(2)]
        self_o = t2
        cc = c.at
        p8_c = c.take(XC * 2 * OK)
        p8_w1 = c.take(P, rows=D)
        p8_b1 = c.take(1)
        p8_w2 = c.take(2 * OK)
        p8_b2 = c.take(2 * OK)
        p8_idx = [c.take(2 * U, dt=i32) for _ in range(2)]
        p8_at = [c.take(D) for _ in range(U)]
        p8_sh = [c.take(S9) for _ in range(U)]
        p8_xg = [c.take(D) for _ in range(U)]
        p8_qg = [c.take(OK) for _ in range(U)]
        p8_xs = [c.take(XC * P) for _ in range(2)]
        p8_xt = [c.take(XC * P) for _ in range(2)]
        p8_att = c.take(U * P, rows=D)
        p8_hid = c.take(U * P)
        p8_wk = [c.take(2 * OK) for _ in range(2)]
        p8_kv = [c.take(2 * OK) for _ in range(U)]
        p8_pr = [c.take(OK) for _ in range(2)]
        lg = c.take(NS * H2)
        c = Cut()
        c.at = AREA - (-(-(NS * H2) // 8) * 8)
        assert c.take(NS * H2).offset == lg.offset or True
        NG = NS * H2 // P
        pA_row = [sb(f"scan_row{i}", [P, 512]) for i in range(2)]
        c = Cut()
        pS_a = c.take(H2 * SCL)
        pS_f = c.take(H2 * SCL)
        pS_dv = c.take(SCL)
        pS_val = c.take(SCL)
        pS_pm = c.take(SCL)
        pS_new = c.take(SCL)
        pS_v1 = c.take(SCL)
        pS_l = c.take(64)
        pS_tr = c.take(8 * P, rows=8)

        c = Cut()
        pB_ex = c.take(NS * H2)
        pB_v = [c.take(OK) for _ in range(U)]
        pB_vx = [c.take(VW) for _ in range(U)]
        pB_oh = [c.take(P) for _ in range(U)]
        pB_z = c.take(P)
        pB_acc = c.take(NW * VW)
        pB_r = c.take(NW * H2)
        pB_uT = [c.take(P) for _ in range(2)]
        pB_n = c.take(D * 4)

        c = Cut()
        pD_adj = [c.take(N) for _ in range(2)]
        pD_oT = c.take(NP, rows=D)

        block = ctx.enter_context(nc.Block())

        @block.sync
        def _(sp):
            sp.dma_start(p1_dst_i, A["dst"].rearrange("a e -> (a e)").rearrange("(p c) -> p c", p=P)).then_inc(S("ld_dst"), 16)
            sp.wait_ge(S("x_zero"), 1)
            sp.dma_start(x[:, 0:NW - 1, :], A["x"][0:(NW - 1) * P, :].rearrange("(w p) d -> p w d", p=P)
                         ).then_inc(S("ld_x"), 16)
            sp.dma_start(x[0:LAST, NW - 1, :], A["x"][(NW - 1) * P:N, :]).then_inc(S("ld_x"), 16)
            sp.dma_start(w0[:, :, :], A["L0_gnn_W"].rearrange("r f o -> f r o")).then_inc(S("ld_w"), 16)
            sp.dma_start(w1[:, 0, :, :], A["L1_gnn_Wh"].rearrange("h d e -> d h e")).then_inc(S("ld_w"), 16)
            sp.dma_start(w1[:, 1, :, :], A["L1_gnn_weight"].rearrange("(h d) e -> d h e", h=H1)
                         ).then_inc(S("ld_w"), 16)
            sp.dma_start(w2n[:, 0:OK], A["L2_gnn_Wq"]).then_inc(S("ld_w"), 16)
            sp.dma_start(w2n[:, OK:OK + D], A["L2_gnn_W_self"]).then_inc(S("ld_w"), 16)
            sp.dma_start(wout[:, :], A["L2_gnn_W_out"]).then_inc(S("ld_w"), 16)
            sp.dma_start(w3[:, :], A["L3_gnn_W"]).then_inc(S("ld_w"), 16)
            for j, n in enumerate(("L2_gnn_gamma", "L2_gnn_beta", "L3_gnn_b")):
                sp.dma_start(gam[:, j, :], A[n].partition_broadcast(P)).then_inc(S("ld_w"), 16)
            sp.wait_ge(S("tiles_known"), 1)
            sp.dma_start(d_tile.rearrange("(b p) -> p b", p=P), p1_ti, allow_slow_non_contiguous=True).then_inc(S("st_tile"), 16)
            sp.wait_ge(S("st_tile"), 16)
            sp.dma_start(tile_row[0:1, :], d_tile.rearrange("(o n) -> o n", o=1)).then_inc(S("st_tile"), 16)
            sp.wait_ge(S("rel_known"), 1)
            sp.dma_start(d_rel.rearrange("(b p) e -> p b e", p=P), p1_dv.rearrange("p (b e) -> p b e", e=P)
                         ).then_inc(S("st_rel"), 16)
            sp.wait_ge(S("st_tile"), 32)
            sp.wait_ge(S("st_rel"), 16)
            sp.wait_ge(S("ld_w"), 160)
            barrier(sp, 1)
            xw_v = d_xw.rearrange("(w p r) o -> w p (r o)", p=P, r=R)
            for w in range(NW):
                sp.wait_ge(S("xw_out"), w + 1)
                sp.dma_start(xw_v[w], p2_o[w % 2]).then_inc(S(f"st_xw{w % 2}"), 16)
            sp.wait_ge(S("st_xw0"), 16 * 13)
            sp.wait_ge(S("st_xw1"), 16 * 12)
            barrier(sp, 2)
            with sp.Fori(0, NW) as w:
                sp.wait_ge(S("adj_out"), w + 1)
                sp.dma_start(d_adj[ds(w, 1), :, :].rearrange("o p c -> (o p) c"), p3_ev).then_inc(S("st_adj"), 16)
            sp.wait_ge(S("st_adj"), 16 * NW)
            barrier(sp, 3)
            barrier(sp, 4)
            sp.wait_ge(S("adj_zero"), 1)
            for w in range(NW):
                if w >= 2:
                    sp.wait_ge(S("at_tr"), 7 * (w - 1))
                sp.dma_start(p5_adj[w % 2][:, 0:N], d_adj[w]).then_inc(S(f"ld_adj{w % 2}"), 16)
            barrier(sp, 5)
            sp.dma_start(d_x.rearrange("(w p) d -> p w d", p=P), x[:, :, :]).then_inc(S("st_x"), 16)
            q_v = d_q.rearrange("(w p) o -> w p o", p=P)
            for w in range(NW):
                sp.wait_ge(S("q_out"), w + 1)
                sp.dma_start(q_v[w], p8_qo[w % 2][:, 0:OK]).then_inc(S(f"st_q{w % 2}"), 16)
            sp.wait_ge(S("st_x"), 16)
            sp.wait_ge(S("st_q0"), 16 * 13)
            sp.wait_ge(S("st_q1"), 16 * 12)
            for j, n in enumerate(("L2_gnn_Cqk", "L2_gnn_Cv")):
                for s in range(S9):
                    half = 64 * (s % 2)
                    at = (s // 2) * 2 * OK + j * OK
                    sp.dma_start(p8_c[half:half + D, at:at + OK], A[n][:, s, :]).then_inc(S("ld_c"), 16)
            sp.wait_ge(S("w2_zero"), 1)
            for j, n in enumerate(("k", "v")):
                sp.dma_start(p8_w1[:, j * D:(j + 1) * D], A[f"L2_gnn_{n}_w1"]).then_inc(S("ld_c"), 16)
                sp.dma_start(p8_b1[j * D:(j + 1) * D, :], A[f"L2_gnn_{n}_b1"].rearrange("(d o) -> d o", o=1)
                             ).then_inc(S("ld_c"), 16)
                sp.dma_start(p8_w2[j * D:(j + 1) * D, j * OK:(j + 1) * OK], A[f"L2_gnn_{n}_w2"]
                             ).then_inc(S("ld_c"), 16)
                sp.dma_start(p8_b2[:, j * OK:(j + 1) * OK], A[f"L2_gnn_{n}_b2"].partition_broadcast(P)
                             ).then_inc(S("ld_c"), 16)
            sp.wait_ge(S("ld_c"), 16 * (2 * S9 + 8))
            barrier(sp, 6)
            with sp.Fori(0, NB) as b:
                for k in range(U):
                    t = sp.value_load(tile_row[0:1, ds(b * U + k, 1)], min_val=0, max_val=NT - 1)
                    sp.wait_ge(S("at_free"), b * U + k + 1)
                    sp.dma_start(p8_at[k], A["edge_attr_64"][ds(t * P, P), :]).then_inc(S(f"ld_at{k}"), 16)
                    sp.wait_ge(S("xs_made"), b * U + k + 1)
                    sp.dma_start(p8_sh[k], A["edge_attr_9"][ds(t * P, P), :]).then_inc(S(f"ld_sh{k}"), 16)
            barrier(sp, 7)
            lg_v = d_lg.rearrange("s h e -> (s h) e")
            ex_v = d_ex.rearrange("s h e -> (s h) e")
            rows_g = [min(4, NG - 4 * g) for g in range(-(-NG // 4))]
            for g, n in enumerate(rows_g):
                sp.wait_ge(S("lg_row"), g + 1)
                sp.dma_start(lg_v[g * 4 * P:(g * 4 + n) * P, :].rearrange("(n p) e -> p n e", p=P),
                             pA_row[g % 2][:, 0:n * P].rearrange("p (n e) -> p n e", e=P)
                             ).then_inc(S(f"st_lg{g % 2}"), 16)
            for j in range(2):
                sp.wait_ge(S(f"st_lg{j}"), 16 * len(rows_g[j::2]))
            sp.wait_ge(S("lg_gone"), 1)
            sl = NS // SCP
            lgs = d_lg.rearrange("(p s) h e -> p h s e", p=SCP)
            for h in range(H2):
                sp.dma_start(pS_a[0:SCP, h * SCL:(h + 1) * SCL].rearrange("p (s e) -> p s e", e=P), lgs[:, h, :, :]
                             ).then_inc(S("ld_scan"), 16)
            sp.dma_start(pS_dv[0:SCP, :], d_rel[0:NS, :].rearrange("(p s) e -> p (s e)", p=SCP)
                         ).then_inc(S("ld_scan"), 16)
            exs = d_ex.rearrange("(p s) h e -> p h s e", p=SCP)
            sp.wait_ge(S("ex_done"), 1)
            for h in range(H2):
                sp.dma_start(exs[:, h, :, :], pS_a[0:SCP, h * SCL:(h + 1) * SCL].rearrange("p (s e) -> p s e", e=P)
                             ).then_inc(S("st_ex"), 16)
            sp.wait_ge(S("st_ex"), 16 * H2)
            for g, n in enumerate(rows_g):
                if g >= 2:
                    sp.wait_ge(S("ex_tr"), g - 1)
                sp.dma_start(pA_row[g % 2][:, 0:n * P].rearrange("p (n e) -> p n e", e=P),
                             ex_v[g * 4 * P:(g * 4 + n) * P, :].rearrange("(n p) e -> p n e", p=P)
                             ).then_inc(S(f"ld_ex{g % 2}"), 16)
            barrier(sp, 8)
            with sp.Fori(0, NB) as b:
                for k in range(U):
                    sp.wait_ge(S("v_used"), b * U + k + 1)
                    sp.dma_start(pB_v[k], d_v[ds(b * U + k, 1), :, :].rearrange("o p c -> (o p) c")
                                 ).then_inc(S(f"ld_v{k}"), 16)
            barrier(sp, 9)
            barrier(sp, 10)
            for w in range(NW):
                if w >= 2:
                    sp.wait_ge(S("out_mm"), w - 1)
                sp.dma_start(pD_adj[w % 2], d_adj[w]).then_inc(S(f"ld_adjb{w % 2}"), 16)
            sp.wait_ge(S("final"), 1)
            sp.dma_start(out_dram[0:(NW - 1) * P, :].rearrange("(w p) d -> p w d", p=P), x[:, 0:NW - 1, :]
                         ).then_inc(S("st_out"), 16)
            sp.dma_start(out_dram[(NW - 1) * P:N, :], x[0:LAST, NW - 1, :]).then_inc(S("st_out"), 16)
            sp.wait_ge(S("st_out"), 32)

        @block.gpsimd
        def _(pool):
            nc.gpsimd.memset(x[:, :, :], 0.0).then_inc(S("x_zero"), 1)
            nc.gpsimd.iota(iota128[:, :], [[1, P]], base=0, channel_multiplier=0,
                           allow_small_or_imprecise_dtypes=True)
            nc.gpsimd.iota(p1_i, [[P, NBLK]], base=0, channel_multiplier=1, allow_small_or_imprecise_dtypes=True)
            nc.gpsimd.iota(pcol[:, :], [[0, 1]], base=0, channel_multiplier=1, allow_small_or_imprecise_dtypes=True)
            nc.gpsimd.memset(ones[:, :], 1.0)
            link(pool, "pool", nc.gpsimd.memset(ident[:, :], 0.0))
            nc.gpsimd.affine_select(out=ident[:, :], in_=ident[:, :], compare_op=ALU.not_equal, fill=1.0, base=0,
                                    pattern=[[-1, P]], channel_multiplier=1).then_inc(S("consts"), 1)
            pool.wait_ge(S("tiles_known"), 1)
            for name, arr in (("dst", "dst"), ("src", "src"), ("typ", "edge_type_8"), ("wgt", "edge_weight")):
                for j in range(NBLK):
                    pool.indirect_dma_start(out=p1_g[name][:, j * P:(j + 1) * P], out_offset=None, in_=A[arr],
                                            in_offset=bass.IndirectOffsetOnAxis(ap=p1_ti[:, j:j + 1], axis=0)
                                            ).then_inc(S(f"g_{name}"), 16)
            pool.wait_ge(S("g_wgt"), 16 * NBLK)
            barrier(pool, 1)
            nc.gpsimd.iota(p3_iota, [[1, N]], base=-CENTRE, channel_multiplier=0,
                           allow_small_or_imprecise_dtypes=True)
            barrier(pool, 2)
            with pool.Fori(0, NB // 2) as b2:
                for j in range(2):
                    nc.gpsimd.tensor_copy(p3_idx[j], xwi_t[:, ds(b2 * (2 * U) + j * U, U)]).then_inc(S("idx3"), 1)
                    pool.wait_ge(S("idx3"), b2 * 2 + j + 1)
                    hold(pool)
                    for k in range(U):
                        pool.wait_ge(S("slot3_free"), b2 * (2 * U) + (j * U + k + 1))
                        hold(pool)
                        pool.indirect_dma_start(out=p3_msg[k], out_offset=None, in_=d_xw,
                                                in_offset=bass.IndirectOffsetOnAxis(ap=p3_idx[j][:, k:k + 1], axis=0)
                                                ).then_inc(S(f"g_msg{k}"), 16)
            barrier(pool, 3)
            pool.wait_ge(S("sc_max"), 1)
            nc.gpsimd.partition_all_reduce(p5_mm, p5_m, P, RMAX).then_inc(S("sc_gmax"), 1)
            pool.wait_ge(S("sc_sum"), 1)
            nc.gpsimd.partition_all_reduce(p5_zz, p5_z, P, RADD).then_inc(S("sc_gsum"), 1)
            barrier(pool, 4)
            barrier(pool, 5)
            barrier(pool, 6)
            with pool.Fori(0, NB // 2) as b2:
                for j in range(2):
                    nc.gpsimd.tensor_copy(p8_idx[j][:, 0:U], src_t[:, ds(b2 * (2 * U) + j * U, U)])
                    nc.gpsimd.tensor_copy(p8_idx[j][:, U:2 * U], dst_t[:, ds(b2 * (2 * U) + j * U, U)]
                                          ).then_inc(S("idx8"), 1)
                    pool.wait_ge(S("idx8"), b2 * 2 + j + 1)
                    hold(pool)
                    for k in range(U):
                        pool.wait_ge(S("xs_made"), b2 * (2 * U) + (j * U + k + 1))
                        hold(pool)
                        pool.indirect_dma_start(out=p8_xg[k], out_offset=None, in_=d_x,
                                                in_offset=bass.IndirectOffsetOnAxis(ap=p8_idx[j][:, k:k + 1], axis=0)
                                                ).then_inc(S(f"g_x{k}"), 16)
                        pool.wait_ge(S("q_used"), b2 * (2 * U) + (j * U + k + 1))
                        hold(pool)
                        pool.indirect_dma_start(out=p8_qg[k], out_offset=None, in_=d_q,
                                                in_offset=bass.IndirectOffsetOnAxis(
                                                    ap=p8_idx[j][:, U + k:U + k + 1], axis=0)
                                                ).then_inc(S(f"g_q{k}"), 16)
            for n in range(7, 11):
                barrier(pool, n)

        @block.scalar
        def _(act):
            barrier(act, 1)
            for w in range(NW):
                act.wait_ge(S("xw_mm"), w + 1)
                if w >= 2:
                    act.wait_ge(S(f"st_xw{w % 2}"), 16 * (w // 2))
                nc.scalar.activation(p2_o[w % 2], ps[:, 4 + w % 2, :], ACT.Copy).then_inc(S("xw_out"), 1)
            barrier(act, 2)
            with act.Fori(0, NW) as w:
                act.wait_ge(S("win3"), w + 1)
                hold(act)
                nc.scalar.activation(agg_f[:, ds(w * D, D)], ps[:, 7, 0:D], ACT.Copy)
                act.wait_ge(S("st_adj"), w * 16)
                hold(act)
                nc.scalar.activation(p3_ev, psf[:, 0:N], ACT.Copy).then_inc(S("adj_out"), 1)
            barrier(act, 3)
            act.wait_ge(S("ln_var"), 1)
            nc.scalar.activation(st[:, 4, :], st[:, 3, :], ACT.Sqrt).then_inc(S("ln_sd"), 1)
            for w in range(NW):
                act.wait_ge(S("sc_mm"), w + 1)
                nc.scalar.activation(p5_hw[:, w * 256:(w + 1) * 256], ps[:, 6 + w % 2, 0:256], ACT.Copy
                                     ).then_inc(S("hw_out"), 1)
            act.wait_ge(S("sc_sub"), 1)
            nc.scalar.activation(p5_e, p5_e, ACT.Exp).then_inc(S("sc_exp"), 1)
            barrier(act, 4)
            for w in range(NW):
                for g in range(7):
                    cols = min(512, NP - g * 512)
                    act.wait_ge(S("at_tr"), 7 * w + g + 1)
                    if w >= 1:
                        act.wait_ge(S("z_mm"), 7 * (w - 1) + g + 1)
                        act.wait_ge(S("deg_red"), 7 * (w - 1) + g + 1)
                    nc.scalar.activation(p5_at[:, g * 512:g * 512 + cols], ps[:, (7 * w + g) % 4, 0:cols], ACT.Copy
                                         ).then_inc(S("at_out"), 1)
            act.wait_ge(S("elu_min"), 1)
            nc.scalar.activation(t1[:, :, :], t1[:, :, :], ACT.Exp).then_inc(S("elu_exp"), 1)
            act.wait_ge(S("ln_var"), 2)
            nc.scalar.activation(st[:, 4, :], st[:, 3, :], ACT.Sqrt).then_inc(S("ln_sd"), 1)
            barrier(act, 5)
            for w in range(NW):
                act.wait_ge(S("q_mm"), w + 1)
                if w >= 2:
                    act.wait_ge(S(f"st_q{w % 2}"), 16 * (w // 2))
                nc.scalar.activation(p8_qo[w % 2][:, 0:OK], ps[:, 4 + w % 2, 0:OK], ACT.Copy).then_inc(S("q_out"), 1)
                nc.scalar.activation(self_o[:, w, :], ps[:, 4 + w % 2, OK:OK + D], ACT.Copy
                                     ).then_inc(S("self_out"), 1)
            barrier(act, 6)
            act.sem_inc(S("xt_out"), 2)
            with act.Fori(0, NB) as b:
                def xs_out(k):
                    act.wait_ge(S("xs_tr"), b * U + (k + 3))
                    act.wait_ge(S("tp_mm"), b * U + k + 1)
                    nc.scalar.activation(p8_xt[k % 2], psf[:, (k % 2) * 1024:(k % 2) * 1024 + XC * P], ACT.Copy
                                         ).then_inc(S("xt_out"), 1)

                def v_store(k):
                    act.wait_ge(S("kv_made"), b * U + (k + 3))
                    act.dma_start(d_v[ds(b * U + k, 1), :, :].rearrange("o p c -> (o p) c"), p8_kv[k][:, OK:2 * OK]
                                  ).then_inc(S(f"st_v{k}"), 16)

                xs_out(0)
                act.wait_ge(S("at_free"), b * U + 2 * U)
                act.wait_ge(S("hid_mm"), b)
                nc.scalar.activation(p8_att, ps[0:D, 4, :], ACT.Copy).then_inc(S("att_out"), 1)
                xs_out(1)
                act.wait_ge(S("hid_mm"), b + 1)
                act.wait_ge(S("w_mm"), b * U)
                nc.scalar.activation(p8_hid, ps[:, 5, :], ACT.Relu, bias=p8_b1).then_inc(S("hid_out"), 1)
                xs_out(2)
                v_store(0)
                xs_out(3)
                for k in range(1, U):
                    v_store(k)
            for k in range(U):
                act.wait_ge(S(f"st_v{k}"), 16 * NB)
            barrier(act, 7)
            act.wait_ge(S("ex_sub"), 1)
            nc.scalar.activation(pS_a[0:SCP, :], pS_a[0:SCP, :], ACT.Exp).then_inc(S("ex_done"), 1)
            barrier(act, 8)
            with act.Fori(0, NW) as w:
                act.wait_ge(S("winB"), w + 1)
                hold(act)
                nc.scalar.activation(pB_acc[:, ds(w * VW, VW)], ps[:, 0, 0:VW], ACT.Copy).then_inc(S("accB"), 1)
            barrier(act, 9)
            act.wait_ge(S("bn_var"), 1)
            nc.scalar.activation(pB_n[:, 0:D], pB_n[:, 0:D], ACT.Sqrt).then_inc(S("bn_sd"), 1)
            act.wait_ge(S("ln_var"), 3)
            nc.scalar.activation(st[:, 4, :], st[:, 3, :], ACT.Sqrt).then_inc(S("ln_sd"), 1)
            nc.scalar.activation(dinv[:, :], deg[:, :], ACT.Sqrt).then_inc(S("deg_sd"), 1)
            barrier(act, 10)
            act.wait_ge(S("out_mm"), NW)
            nc.scalar.activation(pD_oT[:, 0:N], psf[0:D, 0:N], ACT.Copy).then_inc(S("oT"), 1)
            act.wait_ge(S("ln_var"), 4)
            nc.scalar.activation(st[:, 4, :], st[:, 3, :], ACT.Sqrt).then_inc(S("ln_sd"), 1)

        @block.vector
        def _(dve):
            V = nc.vector

            def L(ins):
                link(dve, "dve", ins)

            def bw(a, n=D):
                return a.unsqueeze(2).to_broadcast([P, NW, n])

            def layer_norm(j):
                L(V.tensor_reduce(out=st[:, 0, :], in_=t1[:, :, :], axis=AX.X, op=ALU.add))
                L(V.tensor_scalar(st[:, 1, :], st[:, 0, :], 1.0 / D, None, ALU.mult))
                L(V.tensor_tensor(t1[:, :, :], t1[:, :, :], bw(st[:, 1, :]), ALU.subtract))
                L(V.tensor_tensor(agg[:, :, :], t1[:, :, :], t1[:, :, :], ALU.mult))
                L(V.tensor_reduce(out=st[:, 2, :], in_=agg[:, :, :], axis=AX.X, op=ALU.add))
                V.tensor_scalar(st[:, 3, :], st[:, 2, :], 1.0 / D, 1e-5, ALU.mult, ALU.add).then_inc(S("ln_var"), 1)
                dve.wait_ge(S("ln_sd"), j + 1)
                L(V.reciprocal(st[:, 5, :], st[:, 4, :]))
                L(V.tensor_tensor(x[:, :, :], t1[:, :, :], bw(st[:, 5, :]), ALU.mult))

            def x_transposes(tag):
                for w in range(NW):
                    dve.wait_ge(S("xT_tr"), tag * NW + w + 1)
                    V.tensor_copy(xT[:, w * P:(w + 1) * P], ps[0:D, w % 4, 0:P]).then_inc(S("xT_out"), 1)

            dve.wait_ge(S("ld_dst"), 16)
            L(V.memset(p1_cnt, 0.0))
            L(V.tensor_copy(p1_dst, p1_dst_i))
            for w in range(1, NW):
                L(V.tensor_scalar(p1_lt, p1_dst, float(P * w), None, ALU.is_lt))
                L(V.tensor_reduce(out=p1_cnt[:, w - 1:w], in_=p1_lt, axis=AX.X, op=ALU.add))
            V.memset(p1_ts, 0.0).then_inc(S("cnt"), 1)
            V.memset(p1_sb, 0.0)
            L(V.memset(p1_off, 0.0))
            dve.wait_ge(S("cnt_mm"), 1)
            L(V.tensor_copy(p1_bi, ps[:, 0, 0:32]))
            L(V.tensor_scalar(p1_bi, p1_bi, 7, None, ALU.arith_shift_right))
            L(V.tensor_copy(p1_te, p1_bi))
            L(V.memset(p1_te[:, NW - 1:NW], float(REAL_TILES - 1)))
            L(V.tensor_copy(p1_ts[:, 1:NW], p1_te[:, 0:NW - 1]))
            L(V.tensor_tensor(p1_nb[:, 0:NW], p1_te[:, 0:NW], p1_ts[:, 0:NW], ALU.subtract))
            L(V.tensor_scalar(p1_nb[:, 0:NW], p1_nb[:, 0:NW], float(U), None, ALU.add))
            L(V.tensor_copy(p1_nbi[:, 0:NW], p1_nb[:, 0:NW]))
            L(V.tensor_scalar(p1_nbi[:, 0:NW], p1_nbi[:, 0:NW], 2, None, ALU.arith_shift_right))
            L(V.tensor_copy(p1_nb[:, 0:NW], p1_nbi[:, 0:NW]))
            L(V.tensor_tensor_scan(p1_cum[:, 0:NW], ones[:, 0:NW], p1_nb[:, 0:NW], 0.0, ALU.mult, ALU.add))
            L(V.tensor_copy(p1_sb[:, 1:NW], p1_cum[:, 0:NW - 1]))
            L(V.memset(p1_sb[:, NW:NW + 1], float(NB)))
            L(V.tensor_copy(blk_i[:, :], p1_sb[:, 0:NW + 1]))
            L(V.tensor_scalar(p1_cum[:, 0:NW], p1_sb[:, 0:NW], float(U), None, ALU.mult))
            L(V.tensor_tensor(p1_off[:, 0:NW], p1_ts[:, 0:NW], p1_cum[:, 0:NW], ALU.subtract))
            L(V.tensor_tensor(p1_doff[:, 0:NW - 1], p1_off[:, 1:NW], p1_off[:, 0:NW - 1], ALU.subtract))
            m3 = p1_mask.rearrange("p (b w) -> p b w", w=24)
            o3 = p1_mo.rearrange("p (b w) -> p b w", w=24)
            dve.wait_ge(S("consts"), 1)
            L(V.tensor_tensor(m3, p1_cum[:, 1:NW].unsqueeze(1).to_broadcast([P, NBLK, 24]),
                              p1_i.unsqueeze(2).to_broadcast([P, NBLK, 24]), ALU.is_le))
            L(V.tensor_tensor(o3, m3, p1_doff[:, 0:NW - 1].unsqueeze(1).to_broadcast([P, NBLK, 24]), ALU.mult))
            L(V.tensor_reduce(out=p1_w, in_=m3, axis=AX.X, op=ALU.add))
            L(V.tensor_reduce(out=p1_o, in_=o3, axis=AX.X, op=ALU.add))
            L(V.tensor_tensor(p1_t, p1_i, p1_o, ALU.add))
            L(V.tensor_scalar(p1_t, p1_t, float(NT - 1), None, ALU.min))
            V.tensor_copy(p1_ti, p1_t).then_inc(S("tiles_known"), 1)
            L(V.tensor_scalar(p1_w, p1_w, float(P), None, ALU.mult))
            V.tensor_scalar(realrow[:, :], pcol[:, :], float(LAST), None, ALU.is_lt)
            g3 = {n: p1_g[n].rearrange("p (b e) -> p b e", e=P) for n in p1_g}
            dve.wait_ge(S("g_dst"), 16 * NBLK)
            L(V.tensor_copy(p1_f, p1_g["dst"]))
            L(V.tensor_tensor(p1_rel.rearrange("p (b e) -> p b e", e=P), p1_f.rearrange("p (b e) -> p b e", e=P),
                              p1_w.unsqueeze(2).to_broadcast([P, NBLK, P]), ALU.subtract))
            L(V.tensor_scalar(p1_a, p1_rel, 0.0, None, ALU.is_ge))
            L(V.tensor_scalar(p1_b, p1_rel, float(P), None, ALU.is_lt))
            L(V.tensor_tensor(p1_a, p1_a, p1_b, ALU.mult))
            L(V.tensor_scalar(p1_rel, p1_rel, 1.0, None, ALU.add))
            L(V.tensor_tensor(p1_rel, p1_rel, p1_a, ALU.mult))
            L(V.tensor_scalar(p1_rel, p1_rel, -1.0, None, ALU.add))
            L(V.tensor_scalar(p1_dv, p1_f, 1.0, None, ALU.add))
            L(V.tensor_tensor(p1_dv, p1_dv, p1_a, ALU.mult))
            L(V.tensor_scalar(p1_dv, p1_dv, -1.0, None, ALU.add))
            V.tensor_scalar(p1_q, p1_f, float(NP - 1), None, ALU.min).then_inc(S("rel_known"), 1)
            dve.wait_ge(S("g_src"), 16 * NBLK)
            dve.wait_ge(S("g_typ"), 16 * NBLK)
            V.tensor_copy(p1_s, p1_g["src"])
            L(V.tensor_copy(p1_b, p1_g["typ"]))
            dve.wait_ge(S("g_wgt"), 16 * NBLK)
            V.scalar_tensor_tensor(out=p1_x, in0=p1_s, scalar=float(R), in1=p1_b, op0=ALU.mult, op1=ALU.add
                                   ).then_inc(S("tab_in"), 1)
            dve.wait_ge(S("tab_tr"), 1)
            for r, (dst_ap, srcps) in enumerate(((rel_t[:, :], 0), (src_t[:, :], 2), (xwi_t[:, :], 4), (w_t[:, :], 6))):
                V.tensor_copy(dst_ap, psf[:, srcps * 512:srcps * 512 + NSP])
            V.tensor_scalar(srcc_t[:, :], psf[:, 1024:1024 + NSP], float(-CENTRE), None, ALU.add
                            ).then_inc(S("tab_out"), 1)
            dve.wait_ge(S("tab_tr"), 2)
            L(V.tensor_copy(dst_t[:, :], psf[:, 0:NSP]))
            barrier(dve, 1)
            x_transposes(0)
            V.memset(p3_z, 0.0)
            barrier(dve, 2)
            with dve.Fori(0, NB) as b:
                for k in range(U):
                    i = b * U + k
                    dve.wait_ge(S("slot3_free"), b * U + (k + 1))
                    V.tensor_scalar(p3_ohs[k], p3_iota, srcc_t[:, ds(i, 1)], None, ALU.is_equal)
                    V.tensor_scalar(p3_ohd[k], iota128[:, :], rel_t[:, ds(i, 1)], None, ALU.is_equal)
                    V.tensor_scalar(p3_ohw[k], iota128[:, :], rel_t[:, ds(i, 1)], w_t[:, ds(i, 1)],
                                    ALU.is_equal, ALU.mult).then_inc(S("oh3"), 1)
            barrier(dve, 3)
            L(V.tensor_tensor(t1[:, :, :], x[:, :, :], agg[:, :, :], ALU.add))
            layer_norm(0)
            V.memset(p5_adj[0][:, N:NP], 0.0).then_inc(S("x_ready"), 1)
            V.memset(p5_adj[1][:, N:NP], 0.0).then_inc(S("adj_zero"), 1)
            x_transposes(1)
            s3 = p5_s.rearrange("p (w h) -> p w h", h=H1)
            e3 = p5_e.rearrange("p (w h) -> p w h", h=H1)
            for w in range(NW):
                dve.wait_ge(S("sc_mm"), w + 1)
                pr = p5_pr[w % 2].rearrange("p (h e) -> p h e", h=H1)
                L(V.tensor_tensor(pr, ps[:, 4 + w % 2, 0:256].rearrange("p (h e) -> p h e", h=H1),
                                  x[:, w, :].unsqueeze(1).to_broadcast([P, H1, D]), ALU.mult))
                V.tensor_reduce(out=s3[:, w, :], in_=pr, axis=AX.X, op=ALU.add).then_inc(S("sc_used"), 1)
            dve.wait_ge(S("sc_used"), NW)
            L(V.tensor_scalar(p5_s, p5_s, D ** -0.5, None, ALU.mult))
            L(V.tensor_scalar(small[:, 0:1], realrow[:, :], BIG, -BIG, ALU.mult, ALU.add))
            L(V.tensor_tensor(s3[:, NW - 1, :], s3[:, NW - 1, :], small[:, 0:1].to_broadcast([P, H1]), ALU.add))
            V.tensor_reduce(out=p5_m, in_=p5_s.rearrange("p (w h) -> p h w", h=H1), axis=AX.X, op=ALU.max
                            ).then_inc(S("sc_max"), 1)
            dve.wait_ge(S("sc_gmax"), 1)
            V.tensor_tensor(e3, s3, p5_mm.unsqueeze(1).to_broadcast([P, NW, H1]), ALU.subtract
                            ).then_inc(S("sc_sub"), 1)
            dve.wait_ge(S("sc_exp"), 1)
            V.tensor_reduce(out=p5_z, in_=p5_e.rearrange("p (w h) -> p h w", h=H1), axis=AX.X, op=ALU.add
                            ).then_inc(S("sc_sum"), 1)
            dve.wait_ge(S("sc_gsum"), 1)
            L(V.reciprocal(p5_ri, p5_zz))
            L(V.tensor_tensor(e3, e3, p5_ri.unsqueeze(1).to_broadcast([P, NW, H1]), ALU.mult))
            dve.wait_ge(S("hw_out"), NW)
            hw4 = p5_hw.rearrange("p (g e) -> p g e", e=D)
            L(V.tensor_tensor(hw4, hw4, p5_e.unsqueeze(2).to_broadcast([P, NW * H1, D]), ALU.mult))
            L(V.tensor_reduce(out=p5_zt.rearrange("p (w e) -> p w e", e=D),
                              in_=p5_hw.rearrange("p (w h e) -> p w e h", h=H1, e=D), axis=AX.X, op=ALU.add))
            V.memset(deg[:, :], 1.0)
            barrier(dve, 4)
            for w in range(NW):
                for g in range(7):
                    cols = min(512, NP - g * 512)
                    dve.wait_ge(S("at_out"), 7 * w + g + 1)
                    V.tensor_reduce(out=t1[:, w % 2, g * 4:g * 4 + cols // P],
                                    in_=p5_at[:, g * 512:g * 512 + cols].rearrange("p (c e) -> p c e", e=P), axis=AX.X, op=ALU.add
                                    ).then_inc(S("deg_red"), 1)
                dve.wait_ge(S("deg_red"), 7 * w + 7)
                L(V.tensor_tensor(deg[:, :], deg[:, :], t1[:, w % 2, 0:NW], ALU.add))
                dve.wait_ge(S("z_mm"), 7 * w + 7)
                V.tensor_copy(agg[:, w, :], ps[:, 4 + w % 2, 0:D]).then_inc(S("z_out"), 1)
            dve.wait_ge(S("z_out"), NW)
            V.tensor_scalar(t1[:, :, :], agg[:, :, :], 0.0, None, ALU.min).then_inc(S("elu_min"), 1)
            L(V.tensor_scalar(agg[:, :, :], agg[:, :, :], 0.0, -1.0, ALU.max, ALU.add))
            dve.wait_ge(S("elu_exp"), 1)
            L(V.tensor_tensor(agg[:, :, :], agg[:, :, :], t1[:, :, :], ALU.add))
            L(V.tensor_tensor(t1[:, :, :], x[:, :, :], agg[:, :, :], ALU.add))
            layer_norm(1)
            barrier(dve, 5)
            x_transposes(2)
            V.memset(p8_w2, 0.0)
            V.memset(p8_xs[0][:, S9 * D:XC * P], 0.0)
            V.memset(p8_xs[1][:, S9 * D:XC * P], 0.0)
            V.memset(p8_c[D:P, 4 * 2 * OK:XC * 2 * OK], 0.0).then_inc(S("w2_zero"), 1)
            barrier(dve, 6)
            dve.sem_inc(S("xs_made"), U)
            dve.sem_inc(S("q_used"), U)
            dve.sem_inc(S("kv_made"), 2)
            with dve.Fori(0, NB) as b:
                def outer(k):
                    dve.wait_ge(S(f"g_x{k}"), b * 16 + 16)
                    dve.wait_ge(S(f"ld_sh{k}"), b * 16 + 16)
                    dve.wait_ge(S("xs_tr"), b * U + (k + 1))
                    V.tensor_tensor(p8_xs[k % 2][:, 0:S9 * D].rearrange("p (s d) -> p s d", d=D),
                                    p8_xg[k].unsqueeze(1).to_broadcast([P, S9, D]),
                                    p8_sh[k].unsqueeze(2).to_broadcast([P, S9, D]), ALU.mult
                                    ).then_inc(S("xs_made"), 1)

                def products(k):
                    dve.wait_ge(S("w_mm"), b * U + (k + 1))
                    V.tensor_tensor(p8_wk[k % 2], ps[:, 6 + k % 2, 256:512], p8_b2, ALU.add).then_inc(S("wk_made"), 1)
                    dve.wait_ge(S(f"st_v{k}"), b * 16)
                    dve.wait_ge(S("wk_made"), b * U + (k + 1))
                    V.tensor_tensor(p8_kv[k], ps[:, 6 + k % 2, 0:256], p8_wk[k % 2], ALU.mult
                                    ).then_inc(S("kv_made"), 1)
                    dve.wait_ge(S(f"g_q{k}"), b * 16 + 16)
                    dve.wait_ge(S("kv_made"), b * U + (k + 3))
                    V.tensor_tensor(p8_pr[k % 2], p8_kv[k][:, 0:OK], p8_qg[k], ALU.mult).then_inc(S("q_used"), 1)
                    dve.wait_ge(S("q_used"), b * U + (U + k + 1))
                    hold(dve)
                    V.tensor_reduce(out=lg[:, ds((b * U + k) * H2, H2)],
                                    in_=p8_pr[k % 2].rearrange("p (h c) -> p h c", h=H2), axis=AX.X, op=ALU.add
                                    ).then_inc(S("lg_made"), 1)

                outer(0)
                outer(1)
                products(0)
                outer(2)
                products(1)
                outer(3)
                products(2)
                products(3)
            dve.wait_ge(S("lg_made"), NS)
            barrier(dve, 7)
            rows_g = [min(4, NG - 4 * g) for g in range(-(-NG // 4))]
            for g, n in enumerate(rows_g):
                dve.wait_ge(S("lg_tr"), g + 1)
                if g >= 2:
                    dve.wait_ge(S(f"st_lg{g % 2}"), 16 * (g // 2))
                V.tensor_copy(pA_row[g % 2][:, 0:n * P], ps[:, g % 2, 0:n * P]).then_inc(S("lg_row"), 1)
            q = slice(0, SCP)
            dve.wait_ge(S("lg_row"), len(rows_g))
            V.memset(pS_l, 0.0).then_inc(S("lg_gone"), 1)
            dve.wait_ge(S("ld_scan"), 16 * (H2 + 1))
            a3 = pS_a[q, :].rearrange("p (h j) -> p h j", h=H2)
            L(V.tensor_scalar(pS_val[q, :], pS_dv[q, :], 0.0, None, ALU.is_ge))
            L(V.tensor_scalar(pS_v1[q, :], pS_val[q, :], BIG, -BIG, ALU.mult, ALU.add))
            L(V.tensor_tensor(a3, a3, pS_val[q, :].unsqueeze(1).to_broadcast([SCP, H2, SCL]), ALU.mult))
            L(V.tensor_tensor(a3, a3, pS_v1[q, :].unsqueeze(1).to_broadcast([SCP, H2, SCL]), ALU.add))
            L(V.memset(pS_v1[q, :], 0.0))
            L(V.tensor_tensor_scan(pS_pm[q, :], pS_v1[q, :], pS_dv[q, :], -1.0, ALU.add, ALU.max))
            L(V.tensor_copy(pS_l[q, 0:8], pS_pm[q, SCL - 1:SCL].to_broadcast([SCP, 8])))
            V.tensor_copy(pS_l[q, 8:9], pS_l[q, 0:1]).then_inc(S("sc_in"), 1)
            T = [pS_tr[:, i * P:(i + 1) * P] for i in range(8)]
            dve.wait_ge(S("sc_tr"), 1)
            L(V.memset(pS_tr, 0.0))
            L(V.tensor_copy(T[0][:, 0:SCP], ps[0:8, 2, 0:SCP]))
            L(V.memset(T[2][:, 0:1], -1.0))
            L(V.tensor_tensor_scan(T[2][:, 1:SCP], T[1][:, 0:SCP - 1], T[0][:, 0:SCP - 1], -1.0, ALU.add, ALU.max))
            V.memset(T[3][:, 0:1], 0.0).then_inc(S("sc_back"), 1)
            dve.wait_ge(S("sc_bk"), 1)
            L(V.tensor_copy(pS_l[q, 16:24], ps[0:SCP, 3, 0:8]))
            L(V.tensor_scalar(pS_pm[q, :], pS_pm[q, :], pS_l[q, 16:17], None, ALU.max))
            L(V.tensor_tensor(pS_new[q, 1:SCL], pS_dv[q, 1:SCL], pS_pm[q, 0:SCL - 1], ALU.is_gt))
            L(V.tensor_tensor(pS_new[q, 0:1], pS_dv[q, 0:1], pS_l[q, 16:17], ALU.is_gt))
            L(V.tensor_scalar(pS_new[q, :], pS_new[q, :], -BIG, None, ALU.mult))
            L(V.tensor_reduce(out=pS_l[q, 24:25], in_=pS_new[q, :], axis=AX.X, op=ALU.min))
            L(V.tensor_reduce(out=pS_l[q, 25:26], in_=pS_new[q, 1:SCL], axis=AX.X, op=ALU.min))
            for h in range(H2):
                L(V.tensor_tensor_scan(pS_f[q, h * SCL:(h + 1) * SCL], pS_new[q, :], pS_a[q, h * SCL:(h + 1) * SCL],
                                       -BIG, ALU.add, ALU.max))
            f3 = pS_f[q, :].rearrange("p (h j) -> p h j", h=H2)
            L(V.tensor_copy(pS_l[q, 32:40], f3[:, :, SCL - 1]))
            V.tensor_copy(pS_l[q, 40:48], pS_l[q, 24:25].to_broadcast([SCP, 8])).then_inc(S("sc_in"), 1)
            dve.wait_ge(S("sc_tr"), 2)
            V.tensor_copy(T[0][:, 0:SCP], ps[0:8, 2, 0:SCP])
            L(V.tensor_copy(T[1][:, 0:SCP], ps[0:8, 2, P:P + SCP]))
            L(V.memset(T[2][:, 0:1], -BIG))
            L(V.tensor_tensor_scan(T[2][:, 1:SCP], T[1][:, 0:SCP - 1], T[0][:, 0:SCP - 1], -BIG, ALU.add, ALU.max))
            V.memset(T[3][:, 0:1], 0.0).then_inc(S("sc_back"), 1)
            dve.wait_ge(S("sc_bk"), 2)
            L(V.tensor_copy(pS_l[q, 48:56], ps[0:SCP, 3, 0:8]))
            for h in range(H2):
                L(V.tensor_tensor_scan(pS_f[q, h * SCL:(h + 1) * SCL], pS_new[q, :], pS_a[q, h * SCL:(h + 1) * SCL],
                                       pS_l[q, 48 + h:49 + h], ALU.add, ALU.max))
            L(V.memset(pS_v1[q, SCL - 1:SCL], 0.0))
            L(V.tensor_copy(pS_v1[q, 0:SCL - 1], pS_new[q, 1:SCL]))
            bwd = pS_pm
            for h in range(H2):
                L(V.tensor_tensor_scan(bwd[q, ::-1], pS_v1[q, ::-1], pS_f[q, h * SCL:(h + 1) * SCL][:, ::-1],
                                       -BIG, ALU.add, ALU.max))
                L(V.tensor_copy(pS_l[q, 32 + h:33 + h], bwd[q, 0:1]))
            V.tensor_copy(pS_l[q, 40:48], pS_l[q, 25:26].to_broadcast([SCP, 8]))
            L(V.tensor_copy(pS_l[q, 56:64], pS_new[q, 0:1].to_broadcast([SCP, 8])))
            V.memset(T[3][:, 0:1], 0.0).then_inc(S("sc_in"), 1)
            dve.wait_ge(S("sc_tr"), 3)
            V.tensor_copy(T[0][:, 0:SCP], ps[0:8, 2, 0:SCP])
            V.tensor_copy(T[1][:, 0:SCP], ps[0:8, 2, P:P + SCP])
            L(V.tensor_copy(T[4][:, 0:SCP], ps[0:8, 2, 2 * P:2 * P + SCP]))
            L(V.memset(T[5][:, 0:P], -BIG))
            L(V.tensor_copy(T[6][:, 0:SCP], T[1][:, 0:SCP]))
            L(V.tensor_tensor(T[6][:, 0:SCP - 1], T[1][:, 0:SCP - 1], T[4][:, 1:SCP], ALU.add))
            L(V.tensor_tensor_scan(T[5][:, 0:SCP][:, ::-1], T[6][:, 0:SCP][:, ::-1], T[0][:, 0:SCP][:, ::-1],
                                   -BIG, ALU.add, ALU.max))
            L(V.memset(T[2][:, 0:P], -BIG))
            L(V.tensor_tensor(T[2][:, 0:SCP - 1], T[5][:, 1:SCP], T[4][:, 1:SCP], ALU.add))
            V.memset(T[3][:, 0:1], 0.0).then_inc(S("sc_back"), 1)
            dve.wait_ge(S("sc_bk"), 3)
            L(V.tensor_copy(pS_l[q, 48:56], ps[0:SCP, 3, 0:8]))
            for h in range(H2):
                L(V.tensor_tensor_scan(bwd[q, ::-1], pS_v1[q, ::-1], pS_f[q, h * SCL:(h + 1) * SCL][:, ::-1],
                                       pS_l[q, 48 + h:49 + h], ALU.add, ALU.max))
                L(V.tensor_tensor(pS_a[q, h * SCL:(h + 1) * SCL], pS_a[q, h * SCL:(h + 1) * SCL], bwd[q, :],
                                  ALU.subtract))
            V.tensor_scalar(pS_a[q, :], pS_a[q, :], 0.0, None, ALU.min).then_inc(S("ex_sub"), 1)
            dve.wait_ge(S("st_ex"), 16 * H2)
            for g, n in enumerate(rows_g):
                dve.wait_ge(S("ex_tr"), g + 1)
                V.tensor_copy(pB_ex[:, g * 512:g * 512 + n * P], ps[:, g % 2, 0:n * P]).then_inc(S("ex_col"), 1)
            V.memset(pB_z, 0.0)
            barrier(dve, 8)
            dve.sem_inc(S("v_used"), U)
            with dve.Fori(0, NB) as b:
                for k in range(U):
                    i = b * U + k
                    dve.wait_ge(S("slotB_free"), b * U + (k + 1))
                    V.tensor_scalar(pB_oh[k], iota128[:, :], rel_t[:, ds(i, 1)], None, ALU.is_equal)
                    V.tensor_copy(pB_vx[k][:, OK:VW], pB_ex[:, ds(i * H2, H2)])
                    dve.wait_ge(S(f"ld_v{k}"), b * 16 + 16)
                    V.tensor_tensor(pB_vx[k][:, 0:OK].rearrange("p (h c) -> p h c", h=H2),
                                    pB_v[k].rearrange("p (h c) -> p h c", h=H2),
                                    pB_ex[:, ds(i * H2, H2)].unsqueeze(2).to_broadcast([P, H2, OK // H2]), ALU.mult
                                    ).then_inc(S("v_used"), 1)
            barrier(dve, 9)
            dve.wait_ge(S("accB"), NW)
            ac3 = pB_acc.rearrange("p (w c) -> p w c", c=VW)
            r3 = pB_r.rearrange("p (w h) -> p w h", h=H2)
            L(V.tensor_scalar(r3, ac3[:, :, OK:VW], 1e-16, None, ALU.add))
            L(V.reciprocal(r3, r3))
            for w in range(NW):
                u3 = ac3[:, w, 0:OK].rearrange("p (h c) -> p h c", h=H2)
                V.tensor_tensor(u3, u3, r3[:, w, :].unsqueeze(2).to_broadcast([P, H2, OK // H2]), ALU.mult
                                ).then_inc(S("upd"), 1)
            for w in range(NW):
                dve.wait_ge(S("u_tr"), w + 1)
                if w >= 2:
                    dve.wait_ge(S("u_mm"), w - 1)
                V.tensor_copy(pB_uT[w % 2], ps[:, w % 2, 0:P]).then_inc(S("u_out"), 1)
                dve.wait_ge(S("u_mm"), w + 1)
                V.tensor_tensor(t1[:, w, :], self_o[:, w, :], ps[:, 2 + w % 2, 0:D], ALU.add).then_inc(S("u_add"), 1)
            dve.wait_ge(S("u_add"), NW)
            V.tensor_reduce(out=pB_n[:, 0:D], in_=t1[:, :, :].rearrange("p w d -> p d w"), axis=AX.X, op=ALU.add
                            ).then_inc(S("bn_in"), 1)
            dve.wait_ge(S("bn_mm"), 1)
            L(V.tensor_scalar(pB_n[:, D:2 * D], ps[:, 4, 0:D], 1.0 / N, None, ALU.mult))
            L(V.tensor_tensor(t1[:, :, :], t1[:, :, :], pB_n[:, D:2 * D].unsqueeze(1).to_broadcast([P, NW, D]),
                              ALU.subtract))
            L(V.tensor_scalar(t1[:, NW - 1, :], t1[:, NW - 1, :], realrow[:, :], None, ALU.mult))
            L(V.tensor_tensor(agg[:, :, :], t1[:, :, :], t1[:, :, :], ALU.mult))
            V.tensor_reduce(out=pB_n[:, 0:D], in_=agg[:, :, :].rearrange("p w d -> p d w"), axis=AX.X, op=ALU.add
                            ).then_inc(S("bn_in"), 1)
            dve.wait_ge(S("bn_mm"), 2)
            V.tensor_scalar(pB_n[:, 0:D], ps[:, 4, 0:D], 1.0 / N, 1e-5, ALU.mult, ALU.add).then_inc(S("bn_var"), 1)
            dve.wait_ge(S("bn_sd"), 1)
            L(V.reciprocal(pB_n[:, 2 * D:3 * D], pB_n[:, 0:D]))
            L(V.tensor_tensor(pB_n[:, 2 * D:3 * D], pB_n[:, 2 * D:3 * D], gam[:, 0, :], ALU.mult))
            L(V.tensor_tensor(t1[:, :, :], t1[:, :, :], pB_n[:, 2 * D:3 * D].unsqueeze(1).to_broadcast([P, NW, D]),
                              ALU.mult))
            L(V.tensor_tensor(t1[:, :, :], t1[:, :, :], gam[:, 1, :].unsqueeze(1).to_broadcast([P, NW, D]), ALU.add))
            L(V.tensor_tensor(t1[:, :, :], t1[:, :, :], x[:, :, :], ALU.add))
            layer_norm(2)
            dve.wait_ge(S("deg_sd"), 1)
            L(V.reciprocal(dinv[:, :], dinv[:, :]))
            barrier(dve, 10)
            dve.wait_ge(S("w3_tr"), 1)
            V.tensor_copy(w3T[:, :], ps[0:D, 6, 0:D]).then_inc(S("w3_out"), 1)
            x_transposes(3)
            for w in range(NW):
                dve.wait_ge(S("h_mm"), w + 1)
                V.tensor_tensor(t1[:, w, :], ps[:, 4 + w % 2, 0:D], gam[:, 2, :], ALU.add).then_inc(S("h_add"), 1)
            dve.wait_ge(S("h_add"), NW)
            V.tensor_tensor(t1[:, :, :], t1[:, :, :], bw(dinv[:, :]), ALU.mult).then_inc(S("g_ready"), 1)
            V.memset(pD_oT[:, N:NP], 0.0).then_inc(S("oT_zero"), 1)
            for w in range(NW):
                dve.wait_ge(S("o_tr"), w + 1)
                V.tensor_copy(agg[:, w, :], ps[:, w % 4, 0:D]).then_inc(S("o_out"), 1)
            dve.wait_ge(S("o_out"), NW)
            L(V.tensor_tensor(t1[:, :, :], t1[:, :, :], agg[:, :, :], ALU.add))
            L(V.tensor_tensor(t1[:, :, :], t1[:, :, :], bw(dinv[:, :]), ALU.mult))
            L(V.tensor_tensor(t1[:, :, :], t1[:, :, :], x[:, :, :], ALU.add))
            layer_norm(3)
            V.memset(small[:, 2:3], 0.0).then_inc(S("final"), 1)

        @block.tensor
        def _(pe):
            def mm(out, lhsT, rhs, start=True, stop=True, **kw):
                return nc.tensor.matmul(out, lhsT, rhs, start=start, stop=stop, **kw)

            def tr(out, in_):
                k = in_.shape[0]
                return nc.tensor.transpose(out, in_, ident[0:k, 0:k])

            def x_transposes(tag):
                for w in range(NW):
                    if w >= 4:
                        pe.wait_ge(S("xT_out"), tag * NW + w - 3)
                    tr(ps[0:D, w % 4, 0:P], x[:, w, :]).then_inc(S("xT_tr"), 1)
                pe.wait_ge(S("xT_out"), tag * NW + NW)

            pe.wait_ge(S("cnt"), 1)
            pe.wait_ge(S("consts"), 1)
            mm(ps[:, 0, 0:32], ones[:, :], p1_cnt).then_inc(S("cnt_mm"), 1)
            pe.wait_ge(S("tab_in"), 1)
            for j, t in enumerate((p1_rel, p1_s, p1_x, p1_g["wgt"])):
                for c_ in range(NBLK):
                    last = tr(psf[:, j * 1024 + c_ * P:j * 1024 + (c_ + 1) * P], t[:, c_ * P:(c_ + 1) * P])
            last.then_inc(S("tab_tr"), 1)
            pe.wait_ge(S("tab_out"), 1)
            for c_ in range(NBLK):
                last = tr(psf[:, c_ * P:(c_ + 1) * P], p1_q[:, c_ * P:(c_ + 1) * P])
            last.then_inc(S("tab_tr"), 1)
            pe.wait_ge(S("ld_x"), 32)
            barrier(pe, 1)
            x_transposes(0)
            for w in range(NW):
                if w >= 2:
                    pe.wait_ge(S("xw_out"), w - 1)
                mm(ps[:, 4 + w % 2, :], xT[:, w * P:(w + 1) * P], w0[:, :, :].rearrange("f r o -> f (r o)")
                   ).then_inc(S("xw_mm"), 1)
            barrier(pe, 2)
            pe.sem_inc(S("slot3_free"), U)
            with pe.Fori(0, NW) as w:
                pe.wait_ge(S("adj_out"), w)
                for g in range(8):
                    mm(ps[:, g, :], p3_z[:, 0:P], p3_z, start=True, stop=False, skip_group_check=True)
                b0 = pe.value_load(blk_i[0:1, ds(w, 1)], min_val=0, max_val=NB)
                b1 = pe.value_load(blk_i[0:1, ds(w + 1, 1)], min_val=1, max_val=NB)
                with pe.Fori(b0, b1) as b:
                    for k in range(U):
                        pe.wait_ge(S("oh3"), b * U + (k + 1))
                        for g in range(7):
                            cols = min(512, N - g * 512)
                            mm(ps[:, g, 0:cols], p3_ohd[k], p3_ohs[k][:, g * 512:g * 512 + cols],
                               start=False, stop=False, skip_group_check=True)
                        pe.wait_ge(S(f"g_msg{k}"), b * 16 + 16)
                        mm(ps[:, 7, 0:D], p3_ohw[k], p3_msg[k], start=False, stop=False, skip_group_check=True
                           ).then_inc(S("slot3_free"), 1)
                mm(ps[:, 7, 0:2], p3_z[:, 0:P], p3_z[:, 0:2], start=False, stop=True, skip_group_check=True
                   ).then_inc(S("win3"), 1)
            barrier(pe, 3)
            pe.wait_ge(S("x_ready"), 1)
            x_transposes(1)
            for w in range(NW):
                if w >= 2:
                    pe.wait_ge(S("sc_used"), w - 1)
                    pe.wait_ge(S("hw_out"), w - 1)
                for a in range(2):
                    last = mm(ps[:, 4 + 2 * a + w % 2, 0:H1 * D], xT[:, w * P:(w + 1) * P],
                              w1[:, a, :, :].rearrange("f h o -> f (h o)"))
                last.then_inc(S("sc_mm"), 1)
            barrier(pe, 4)
            for w in range(NW):
                pe.wait_ge(S(f"ld_adj{w % 2}"), 16 * (w // 2 + 1))
                for g in range(9):
                    if g < 7:
                        n = 7 * w + g
                        if n >= 4:
                            pe.wait_ge(S("at_out"), n - 3)
                        for c_ in range(g * 4, min(g * 4 + 4, NW)):
                            last = tr(ps[:, n % 4, (c_ % 4) * P:(c_ % 4 + 1) * P],
                                      p5_adj[w % 2][:, c_ * P:(c_ + 1) * P])
                        last.then_inc(S("at_tr"), 1)
                    if g >= 2:
                        gg = g - 2
                        pe.wait_ge(S("at_out"), 7 * w + gg + 1)
                        if gg == 0 and w >= 2:
                            pe.wait_ge(S("z_out"), w - 1)
                        for c_ in range(gg * 4, min(gg * 4 + 4, NW)):
                            last = mm(ps[:, 4 + w % 2, 0:D], p5_at[:, c_ * P:(c_ + 1) * P],
                                      p5_zt[:, c_ * D:(c_ + 1) * D], start=(c_ == 0), stop=(c_ == NW - 1))
                        last.then_inc(S("z_mm"), 1)
            barrier(pe, 5)
            x_transposes(2)
            for w in range(NW):
                if w >= 2:
                    pe.wait_ge(S("self_out"), w - 1)
                mm(ps[:, 4 + w % 2, 0:OK + D], xT[:, w * P:(w + 1) * P], w2n[:, :]).then_inc(S("q_mm"), 1)
            barrier(pe, 6)
            pe.sem_inc(S("at_free"), U)
            pe.sem_inc(S("xs_tr"), 2)
            pe.sem_inc(S("tp_mm"), 2)
            with pe.Fori(0, NB) as b:
                def xs_transpose(k):
                    pe.wait_ge(S("xs_made"), b * U + (U + k + 1))
                    pe.wait_ge(S("xt_out"), b * U + k + 1)
                    o = (k % 2) * 1024
                    for c_ in range(XC):
                        last = tr(psf[:, o + c_ * P:o + (c_ + 1) * P], p8_xs[k % 2][:, c_ * P:(c_ + 1) * P])
                    last.then_inc(S("xs_tr"), 1)

                def tensor_product(k):
                    pe.wait_ge(S("xt_out"), b * U + (2 + k + 1))
                    pe.wait_ge(S("kv_made"), b * U + (k + 1))
                    for c_ in range(XC):
                        last = mm(ps[:, 6 + k % 2, 0:2 * OK], p8_xt[k % 2][:, c_ * P:(c_ + 1) * P],
                                  p8_c[:, c_ * 2 * OK:(c_ + 1) * 2 * OK], start=(c_ == 0), stop=(c_ == XC - 1))
                    last.then_inc(S("tp_mm"), 1)
                    mm(ps[:, 6 + k % 2, 2 * OK:4 * OK], p8_hid[:, k * P:(k + 1) * P], p8_w2).then_inc(S("w_mm"), 1)

                xs_transpose(0)
                pe.wait_ge(S("att_out"), b)
                for k in range(U):
                    pe.wait_ge(S(f"ld_at{k}"), b * 16 + 16)
                    hold(pe)
                    tr(ps[0:D, 4, k * P:(k + 1) * P], p8_at[k]).then_inc(S("at_free"), 1)
                xs_transpose(1)
                pe.wait_ge(S("att_out"), b + 1)
                pe.wait_ge(S("hid_out"), b)
                mm(ps[:, 5, :], p8_w1, p8_att).then_inc(S("hid_mm"), 1)
                pe.wait_ge(S("hid_out"), b + 1)
                tensor_product(0)
                xs_transpose(2)
                tensor_product(1)
                xs_transpose(3)
                tensor_product(2)
                tensor_product(3)
            barrier(pe, 7)
            rows_g = [min(4, NG - 4 * g) for g in range(-(-NG // 4))]
            for g, n in enumerate(rows_g):
                if g >= 2:
                    pe.wait_ge(S("lg_row"), g - 1)
                for c_ in range(n):
                    last = tr(ps[:, g % 2, c_ * P:(c_ + 1) * P], lg[:, (g * 4 + c_) * P:(g * 4 + c_ + 1) * P])
                last.then_inc(S("lg_tr"), 1)
            T = [pS_tr[:, i * P:(i + 1) * P] for i in range(8)]
            for r, cols in enumerate(((0,), (32, 40), (32, 40, 56))):
                pe.wait_ge(S("sc_in"), r + 1)
                for j, c_ in enumerate(cols):
                    last = tr(ps[0:8, 2, j * P:j * P + SCP], pS_l[0:SCP, c_:c_ + 8])
                last.then_inc(S("sc_tr"), 1)
                pe.wait_ge(S("sc_back"), r + 1)
                tr(ps[0:SCP, 3, 0:8], T[2][:, 0:SCP]).then_inc(S("sc_bk"), 1)
            for g, n in enumerate(rows_g):
                pe.wait_ge(S(f"ld_ex{g % 2}"), 16 * (g // 2 + 1))
                if g >= 2:
                    pe.wait_ge(S("ex_col"), g - 1)
                for c_ in range(n):
                    last = tr(ps[:, g % 2, c_ * P:(c_ + 1) * P], pA_row[g % 2][:, c_ * P:(c_ + 1) * P])
                last.then_inc(S("ex_tr"), 1)
            barrier(pe, 8)
            pe.sem_inc(S("slotB_free"), U)
            with pe.Fori(0, NW) as w:
                pe.wait_ge(S("accB"), w)
                mm(ps[:, 0, 0:P], pB_z, pB_z, start=True, stop=False, skip_group_check=True)
                mm(ps[:, 0, P:VW], pB_z, pB_z[:, 0:H2], start=False, stop=False, skip_group_check=True)
                b0 = pe.value_load(blk_i[0:1, ds(w, 1)], min_val=0, max_val=NB)
                b1 = pe.value_load(blk_i[0:1, ds(w + 1, 1)], min_val=1, max_val=NB)
                with pe.Fori(b0, b1) as b:
                    for k in range(U):
                        pe.wait_ge(S("v_used"), b * U + (U + k + 1))
                        mm(ps[:, 0, 0:VW], pB_oh[k], pB_vx[k], start=False, stop=False, skip_group_check=True
                           ).then_inc(S("slotB_free"), 1)
                mm(ps[:, 0, 0:2], pB_z, pB_z[:, 0:2], start=False, stop=True, skip_group_check=True
                   ).then_inc(S("winB"), 1)
            barrier(pe, 9)
            for w in range(NW):
                pe.wait_ge(S("upd"), w + 1)
                if w >= 2:
                    pe.wait_ge(S("u_out"), w - 1)
                tr(ps[:, w % 2, 0:P], pB_acc[:, w * VW:w * VW + OK]).then_inc(S("u_tr"), 1)
                pe.wait_ge(S("u_out"), w + 1)
                if w >= 2:
                    pe.wait_ge(S("u_add"), w - 1)
                mm(ps[:, 2 + w % 2, 0:D], pB_uT[w % 2], wout[:, :]).then_inc(S("u_mm"), 1)
            for r in range(2):
                pe.wait_ge(S("bn_in"), r + 1)
                mm(ps[:, 4, 0:D], ones[:, :], pB_n[:, 0:D]).then_inc(S("bn_mm"), 1)
            barrier(pe, 10)
            tr(ps[0:D, 6, 0:D], w3[:, :]).then_inc(S("w3_tr"), 1)
            x_transposes(3)
            pe.wait_ge(S("w3_out"), 1)
            for w in range(NW):
                if w >= 2:
                    pe.wait_ge(S("h_add"), w - 1)
                mm(ps[:, 4 + w % 2, 0:D], xT[:, w * P:(w + 1) * P], w3T[:, :]).then_inc(S("h_mm"), 1)
            pe.wait_ge(S("g_ready"), 1)
            for w in range(NW):
                pe.wait_ge(S(f"ld_adjb{w % 2}"), 16 * (w // 2 + 1))
                for g in range(7):
                    cols = min(512, N - g * 512)
                    last = mm(ps[0:D, g, 0:cols], t1[:, w, :], pD_adj[w % 2][:, g * 512:g * 512 + cols],
                              start=(w == 0), stop=(w == NW - 1))
                last.then_inc(S("out_mm"), 1)
            pe.wait_ge(S("oT"), 1)
            pe.wait_ge(S("oT_zero"), 1)
            for w in range(NW):
                if w >= 4:
                    pe.wait_ge(S("o_out"), w - 3)
                tr(ps[:, w % 4, 0:D], pD_oT[:, w * P:(w + 1) * P]).then_inc(S("o_tr"), 1)


_ROWS = ("dst", "src", "edge_type_8", "edge_weight")


def kernel(**inputs):
    import concourse.bacc as _bacc
    from concourse.bass_utils import run_bass_kernel_spmd as _run

    nc = _bacc.Bacc("TRN2", target_bir_lowering=False, num_devices=1)
    arrays, args = {}, {}
    for name, a in inputs.items():
        a = np.ascontiguousarray(a)
        if name in _ROWS:
            fill = NP if name == "dst" else 0
            a = np.concatenate([a, np.full((NT * P - E,), fill, a.dtype)]).reshape(NT, P)
        elif name.startswith("edge_attr"):
            a = np.concatenate([a, np.zeros((NT * P - E, a.shape[1]), a.dtype)])
        arrays["in_" + name] = a
        args[name] = nc.dram_tensor("in_" + name, a.shape, mybir.dt.from_np(a.dtype), kind="ExternalInput").ap()
    out = nc.dram_tensor("out", (N, D), mybir.dt.float32, kind="ExternalOutput").ap()
    build(nc, args, out)
    return _run(nc, [arrays], core_ids=[0]).results[0]["out"]
```

```python
from contextlib import ExitStack

import numpy as np

import concourse.bass as bass
from concourse import mybir

RMAX = bass.bass_isa.ReduceOp.max
RADD = bass.bass_isa.ReduceOp.add
P = 128
N = 3125
E = 100000
D = 64
R = 8
H1 = 4
S9 = 9
OK = 128
H2 = 8
NW = -(-N // P)
NP = NW * P
LAST = N - (NW - 1) * P
NT = 784
NTR = NT + 4
U = 4
REAL_TILES = -(-E // P)
NB = (REAL_TILES + NW - 1 + NW * (U - 1)) // U
NS = NB * U
NBLK = -(-NS // P)
NSP = NBLK * P
CENTRE = 1562
BIG = 1.0e38
G = 8
NIT = NT // G
SCP = NT // 7
SCL = NT // SCP * P
VW = OK + H2
XC = 5


def build(nc, A, out_dram, dump=None):
    f32, i32, bf16, f16 = mybir.dt.float32, mybir.dt.int32, mybir.dt.bfloat16, mybir.dt.float16
    ALU = mybir.AluOpType
    ACT = mybir.ActivationFunctionType
    AX = mybir.AxisListType
    ds = bass.ds
    ctx = ExitStack()
    with ctx:
        def sb(name, shape, dt=f32):
            return ctx.enter_context(nc.sbuf_tensor(name, shape, dt))

        def sem(name):
            return ctx.enter_context(nc.semaphore(name))

        def dram(name, shape, dt=f32):
            return nc.dram_tensor(name, shape, dt, kind="Internal").ap()

        d_tile = dram("d_slot_tile", (NSP,), i32)
        d_xw = dram("d_xw", (NP * R, D))
        d_adj = dram("d_adj", (NW, P, N))
        d_x = dram("d_x", (NP, D))
        d_q = dram("d_q", (NP, OK))
        d_v = dram("d_v", (P, NTR, OK))
        d_lg = dram("d_logits", (NT, H2, P))
        d_ex = dram("d_exps", (NT, H2, P))

        ident = sb("ident", [P, P])
        ones = sb("ones", [P, P])
        iota128 = sb("iota128", [P, P])
        pcol = sb("pcol", [P, 1])
        realrow = sb("realrow", [P, 1])
        rel_t = sb("rel_t", [P, NSP])
        srcc_t = sb("srcc_t", [P, NSP])
        w_t = sb("w_t", [P, NSP])
        src_t = sb("src_t", [P, NT], i32)
        xwi_t = sb("xwi_t", [P, NSP], i32)
        dst_t = sb("dst_t", [P, NT], i32)
        blk_i = sb("blk_i", [P, NW + 1], i32)
        tile_row = sb("tile_row", [1, NSP], i32)
        x = sb("x", [P, NW, D])
        agg = sb("agg", [P, NW, D])
        t1 = sb("t1", [P, NW, D])
        t2 = sb("t2", [P, NW, D])
        st = sb("st", [P, 8, NW])
        xT = sb("xT", [D, NP])
        dinv = sb("dinv", [P, NW])
        deg = sb("deg", [P, NW])
        small = sb("small", [P, 64])

        w0 = sb("w0", [D, R, D])
        w1 = sb("w1", [D, 2, H1, D])
        w2n = sb("w2n", [D, OK + D])
        wout = sb("wout", [P, D])
        w3 = sb("w3", [D, D])
        w3T = sb("w3T", [D, D])
        gam = sb("gam", [P, 3, D])

        ps = ctx.enter_context(nc.psum_tensor("ps", [P, 8, 512], f32))
        psf = ps[:, :, :].rearrange("p b c -> p (b c)")

        phase = sem("phase")
        lk = {e: sem(f"chain_{e}") for e in ("dve", "act", "pool")}
        lkn = {"dve": 0, "act": 0, "pool": 0}

        def link(eng, name, ins):
            lkn[name] += 1
            ins.then_inc(lk[name], 1)
            eng.wait_ge(lk[name], lkn[name])

        def barrier(eng, n):
            eng.drain().then_inc(phase, 1)
            eng.wait_ge(phase, 5 * n)

        sems = {}

        def S(name):
            if name not in sems:
                sems[name] = sem(name)
            return sems[name]

        tick = sem("tick")

        agg_f = agg[:, :, :].rearrange("p w d -> p (w d)")

        def hold(eng):
            eng.sem_inc(tick, 1)

        AREA = 28000
        area = sb("area", [P, AREA])

        class Cut:
            def __init__(self):
                self.at = 0

            def take(self, cols, rows=P, dt=f32):
                words = cols if dt in (f32, i32) else -(-cols // 2)
                v = area[0:rows, self.at:self.at + words]
                self.at += -(-words // 8) * 8
                assert self.at <= AREA, self.at
                return v if dt == f32 else v.bitcast(dt)[:, 0:cols]

        c = Cut()
        p1_dst_i = c.take(NT, dt=i32)
        p1_k = c.take(NBLK)
        p1_ki = c.take(NBLK, dt=i32)
        p1_dst = c.take(NT)
        p1_lt = c.take(NT)
        p1_cnt = c.take(32)
        p1_bi = c.take(32, dt=i32)
        p1_te = c.take(32)
        p1_ts = c.take(32)
        p1_nb = c.take(32)
        p1_nbi = c.take(32, dt=i32)
        p1_cum = c.take(32)
        p1_sb = c.take(32)
        p1_off = c.take(32)
        p1_doff = c.take(32)
        p1_i = c.take(NBLK)
        p1_mask = c.take(NBLK * 24)
        p1_mo = c.take(NBLK * 24)
        p1_w = c.take(NBLK)
        p1_o = c.take(NBLK)
        p1_t = c.take(NBLK)
        p1_ti = c.take(NBLK, dt=i32)
        p1_g = {n: c.take(NSP, dt=(f32 if n == "wgt" else i32)) for n in ("dst", "src", "typ", "wgt")}
        p1_f = c.take(NSP)
        p1_a = c.take(NSP)
        p1_b = c.take(NSP)
        p1_rel = c.take(NSP)
        p1_s = c.take(NSP)
        p1_x = c.take(NSP)

        c = Cut()
        c.at = 20000
        p2_o = [c.take(R * D) for _ in range(2)]

        c = Cut()
        p3_idx = [c.take(U, dt=i32) for _ in range(2)]
        p3_msg = [c.take(D) for _ in range(U)]
        p3_iota = c.take(N, dt=f16)
        p3_ohs = [c.take(N, dt=bf16) for _ in range(U)]
        p3_ohd = [c.take(P, dt=bf16) for _ in range(U)]
        p3_ohw = [c.take(P) for _ in range(U)]
        p3_z = c.take(512, dt=bf16)
        p3_ev = c.take(N)

        c = Cut()
        p5_hw = c.take(NW * H1 * D)
        p5_pr = [c.take(H1 * D) for _ in range(2)]
        p5_s = c.take(NW * H1)
        p5_e = c.take(NW * H1)
        p5_m = c.take(H1)
        p5_mm = c.take(H1)
        p5_z = c.take(H1)
        p5_zz = c.take(H1)
        p5_ri = c.take(H1)
        p5_zt = c.take(NW * D)
        p5_adj = [c.take(NP) for _ in range(2)]
        p5_at = c.take(NP)

        c = Cut()
        p8_qo = [c.take(OK + D) for _ in range(2)]
        self_o = t2
        cc = c.at
        p8_c = c.take(XC * 2 * OK)
        p8_w1 = c.take(P, rows=D)
        p8_b1 = c.take(1)
        p8_w2 = c.take(2 * OK)
        p8_b2 = c.take(2 * OK)
        p8_idx = [c.take(G, dt=i32) for _ in range(2)]
        p8_att = [c.take(U * P, rows=D) for _ in range(2)]
        p8_sh = c.take(NT * S9)
        p8_xg = [c.take(D) for _ in range(G)]
        p8_qg = [c.take(OK) for _ in range(G)]
        p8_xs = [c.take(XC * P) for _ in range(4)]
        p8_xt = [c.take(XC * P) for _ in range(2)]
        p8_hid = [c.take(U * P) for _ in range(2)]
        p8_wk = [c.take(2 * OK) for _ in range(2)]
        p8_kv = c.take(G * 2 * OK)
        p8_pr = [c.take(OK) for _ in range(2)]
        lg = c.take(NT * H2)
        NG = NT * H2 // P
        pA_row = [sb(f"scan_row{i}", [P, 512]) for i in range(2)]
        c = Cut()
        pS_a = c.take(H2 * SCL)
        pS_f = c.take(H2 * SCL)
        pS_dv = c.take(SCL)
        pS_di = c.take(SCL, dt=i32)
        pS_pm = c.take(SCL)
        pS_new = c.take(SCL)
        pS_v1 = c.take(SCL)
        pS_l = c.take(64)
        pS_tr = c.take(8 * P, rows=8)

        c = Cut()
        pB_ex = c.take(NTR * H2)
        pB_v = [c.take(U * OK) for _ in range(2)]
        pB_vx = [c.take(VW) for _ in range(U)]
        pB_oh = [c.take(P) for _ in range(U)]
        pB_z = c.take(P)
        pB_acc = c.take(NW * VW)
        pB_r = c.take(NW * H2)
        pB_uT = [c.take(P) for _ in range(2)]
        pB_n = c.take(D * 4)

        c = Cut()
        pD_adj = [c.take(N) for _ in range(2)]
        pD_oT = c.take(NP, rows=D)

        block = ctx.enter_context(nc.Block())

        @block.sync
        def _(sp):
            sp.dma_start(p1_dst_i, A["dst_cols"]).then_inc(S("ld_dst"), 16)
            sp.dma_start(src_t[:, :], A["src_cols"]).then_inc(S("ld_w"), 16)
            sp.wait_ge(S("x_zero"), 1)
            sp.dma_start(x[:, 0:NW - 1, :], A["x"][0:(NW - 1) * P, :].rearrange("(w p) d -> p w d", p=P)
                         ).then_inc(S("ld_x"), 16)
            sp.dma_start(x[0:LAST, NW - 1, :], A["x"][(NW - 1) * P:N, :]).then_inc(S("ld_x"), 16)
            sp.dma_start(w0[:, :, :], A["L0_gnn_W"].rearrange("r f o -> f r o")).then_inc(S("ld_w"), 16)
            sp.dma_start(w1[:, 0, :, :], A["L1_gnn_Wh"].rearrange("h d e -> d h e")).then_inc(S("ld_w"), 16)
            sp.dma_start(w1[:, 1, :, :], A["L1_gnn_weight"].rearrange("(h d) e -> d h e", h=H1)
                         ).then_inc(S("ld_w"), 16)
            sp.dma_start(w2n[:, 0:OK], A["L2_gnn_Wq"]).then_inc(S("ld_w"), 16)
            sp.dma_start(w2n[:, OK:OK + D], A["L2_gnn_W_self"]).then_inc(S("ld_w"), 16)
            sp.dma_start(wout[:, :], A["L2_gnn_W_out"]).then_inc(S("ld_w"), 16)
            sp.dma_start(w3[:, :], A["L3_gnn_W"]).then_inc(S("ld_w"), 16)
            for j, n in enumerate(("L2_gnn_gamma", "L2_gnn_beta", "L3_gnn_b")):
                sp.dma_start(gam[:, j, :], A[n].partition_broadcast(P)).then_inc(S("ld_w"), 16)
            sp.wait_ge(S("tiles_known"), 1)
            sp.dma_start(d_tile.rearrange("(b p) -> p b", p=P), p1_ti, allow_slow_non_contiguous=True).then_inc(S("st_tile"), 16)
            sp.wait_ge(S("st_tile"), 16)
            sp.dma_start(tile_row[0:1, :], d_tile.rearrange("(o n) -> o n", o=1)).then_inc(S("st_tile"), 16)
            sp.wait_ge(S("st_tile"), 32)
            sp.wait_ge(S("ld_w"), 176)
            barrier(sp, 1)
            xw_v = d_xw.rearrange("(w p r) o -> w p (r o)", p=P, r=R)
            for w in range(NW):
                sp.wait_ge(S("xw_out"), w + 1)
                sp.dma_start(xw_v[w], p2_o[w % 2]).then_inc(S(f"st_xw{w % 2}"), 16)
            sp.wait_ge(S("st_xw0"), 16 * 13)
            sp.wait_ge(S("st_xw1"), 16 * 12)
            barrier(sp, 2)
            with sp.Fori(0, NW) as w:
                sp.wait_ge(S("adj_out"), w + 1)
                sp.dma_start(d_adj[ds(w, 1), :, :].rearrange("o p c -> (o p) c"), p3_ev).then_inc(S("st_adj"), 16)
            sp.wait_ge(S("st_adj"), 16 * NW)
            barrier(sp, 3)
            barrier(sp, 4)
            sp.wait_ge(S("adj_zero"), 1)
            for w in range(NW):
                if w >= 2:
                    sp.wait_ge(S("at_tr"), 7 * (w - 1))
                sp.dma_start(p5_adj[w % 2][:, 0:N], d_adj[w]).then_inc(S(f"ld_adj{w % 2}"), 16)
            barrier(sp, 5)
            sp.dma_start(d_x.rearrange("(w p) d -> p w d", p=P), x[:, :, :]).then_inc(S("st_x"), 16)
            q_v = d_q.rearrange("(w p) o -> w p o", p=P)
            for w in range(NW):
                sp.wait_ge(S("q_out"), w + 1)
                sp.dma_start(q_v[w], p8_qo[w % 2][:, 0:OK]).then_inc(S(f"st_q{w % 2}"), 16)
            sp.wait_ge(S("st_x"), 16)
            sp.wait_ge(S("st_q0"), 16 * 13)
            sp.wait_ge(S("st_q1"), 16 * 12)
            for j, n in enumerate(("L2_gnn_Cqk", "L2_gnn_Cv")):
                for s in range(S9):
                    half = 64 * (s % 2)
                    at = (s // 2) * 2 * OK + j * OK
                    sp.dma_start(p8_c[half:half + D, at:at + OK], A[n][:, s, :]).then_inc(S("ld_c"), 16)
            sp.wait_ge(S("w2_zero"), 1)
            for j, n in enumerate(("k", "v")):
                sp.dma_start(p8_w1[:, j * D:(j + 1) * D], A[f"L2_gnn_{n}_w1"]).then_inc(S("ld_c"), 16)
                sp.dma_start(p8_b1[j * D:(j + 1) * D, :], A[f"L2_gnn_{n}_b1"].rearrange("(d o) -> d o", o=1)
                             ).then_inc(S("ld_c"), 16)
                sp.dma_start(p8_w2[j * D:(j + 1) * D, j * OK:(j + 1) * OK], A[f"L2_gnn_{n}_w2"]
                             ).then_inc(S("ld_c"), 16)
                sp.dma_start(p8_b2[:, j * OK:(j + 1) * OK], A[f"L2_gnn_{n}_b2"].partition_broadcast(P)
                             ).then_inc(S("ld_c"), 16)
            sp.dma_start(p8_sh, A["edge_attr_9"].rearrange("p t s -> p (t s)")).then_inc(S("ld_c"), 16)
            sp.wait_ge(S("ld_c"), 16 * (2 * S9 + 9))
            barrier(sp, 6)
            def att_load(n, turn):
                sp.dma_start(p8_att[n % 2], A["edge_attr_64"][turn]).then_inc(S(f"ld_at{n % 2}"), 16)

            def v_store(h, t, kvs):
                sp.wait_ge(S("kv_made"), kvs)
                sp.dma_start(d_v[:, t, :],
                             p8_kv3[:, h * U:(h + 1) * U, OK:2 * OK]).then_inc(S(f"st_v{h}"), 16)

            p8_kv3 = p8_kv.rearrange("p (j c) -> p j c", c=2 * OK)
            att_load(0, 0)
            att_load(1, 1)
            with sp.Fori(1, NIT) as it:
                for h in range(2):
                    sp.wait_ge(S("hid_mm"), it * 2 + h - 1)
                    sp.dma_start(p8_att[h], A["edge_attr_64"][ds(it * 2 + h, 1), :, :].rearrange("o d e -> (o d) e")
                                 ).then_inc(S(f"ld_at{h}"), 16)
                    v_store(h, ds(it * G + (h * U - G), U), it * G + (h * U - G + U + 2))
            for h in range(2):
                v_store(h, slice(NT - G + h * U, NT - G + (h + 1) * U), NT - G + (h + 1) * U + 2)
            for h in range(2):
                sp.wait_ge(S(f"st_v{h}"), 16 * NIT)
            barrier(sp, 7)
            lg_v = d_lg.rearrange("s h e -> (s h) e")
            ex_v = d_ex.rearrange("s h e -> (s h) e")
            rows_g = [min(4, NG - 4 * g) for g in range(-(-NG // 4))]
            for g, n in enumerate(rows_g):
                sp.wait_ge(S("lg_row"), g + 1)
                sp.dma_start(lg_v[g * 4 * P:(g * 4 + n) * P, :].rearrange("(n p) e -> p n e", p=P),
                             pA_row[g % 2][:, 0:n * P].rearrange("p (n e) -> p n e", e=P)
                             ).then_inc(S(f"st_lg{g % 2}"), 16)
            for j in range(2):
                sp.wait_ge(S(f"st_lg{j}"), 16 * len(rows_g[j::2]))
            sp.wait_ge(S("lg_gone"), 1)
            lgs = d_lg.rearrange("(p s) h e -> p h s e", p=SCP)
            for h in range(H2):
                sp.dma_start(pS_a[0:SCP, h * SCL:(h + 1) * SCL].rearrange("p (s e) -> p s e", e=P), lgs[:, h, :, :]
                             ).then_inc(S("ld_scan"), 16)
            sp.dma_start(pS_di[0:SCP, :], A["dst"][0:NT, :].rearrange("(p s) e -> p (s e)", p=SCP)
                         ).then_inc(S("ld_scan"), 16)
            exs = d_ex.rearrange("(p s) h e -> p h s e", p=SCP)
            sp.wait_ge(S("ex_done"), 1)
            for h in range(H2):
                sp.dma_start(exs[:, h, :, :], pS_a[0:SCP, h * SCL:(h + 1) * SCL].rearrange("p (s e) -> p s e", e=P)
                             ).then_inc(S("st_ex"), 16)
            sp.wait_ge(S("st_ex"), 16 * H2)
            for g, n in enumerate(rows_g):
                if g >= 2:
                    sp.wait_ge(S("ex_tr"), g - 1)
                sp.dma_start(pA_row[g % 2][:, 0:n * P].rearrange("p (n e) -> p n e", e=P),
                             ex_v[g * 4 * P:(g * 4 + n) * P, :].rearrange("(n p) e -> p n e", p=P)
                             ).then_inc(S(f"ld_ex{g % 2}"), 16)
            sp.wait_ge(S("v_zero"), 1)
            sp.dma_start(d_v[:, NT:NTR, :], pB_v[0].rearrange("p (t c) -> p t c", c=OK)).then_inc(S("st_v0"), 16)
            sp.wait_ge(S("st_v0"), 16 * (NIT + 1))
            barrier(sp, 8)
            with sp.Fori(0, NB // 2) as b2:
                for j in range(2):
                    t = sp.value_load(tile_row[0:1, ds(b2 * (2 * U) + j * U, 1)], min_val=0, max_val=NT)
                    sp.wait_ge(S("v_used"), b2 * (2 * U) + (j * U + U))
                    sp.dma_start(pB_v[j], d_v[:, ds(t, U), :].rearrange("p t c -> p (t c)")).then_inc(S(f"ld_v{j}"), 16)
            barrier(sp, 9)
            barrier(sp, 10)
            for w in range(NW):
                if w >= 2:
                    sp.wait_ge(S("out_mm"), w - 1)
                sp.dma_start(pD_adj[w % 2], d_adj[w]).then_inc(S(f"ld_adjb{w % 2}"), 16)
            sp.wait_ge(S("final"), 1)
            sp.dma_start(out_dram[0:(NW - 1) * P, :].rearrange("(w p) d -> p w d", p=P), x[:, 0:NW - 1, :]
                         ).then_inc(S("st_out"), 16)
            sp.dma_start(out_dram[(NW - 1) * P:N, :], x[0:LAST, NW - 1, :]).then_inc(S("st_out"), 16)
            sp.wait_ge(S("st_out"), 32)

        @block.gpsimd
        def _(pool):
            nc.gpsimd.memset(x[:, :, :], 0.0).then_inc(S("x_zero"), 1)
            nc.gpsimd.iota(iota128[:, :], [[1, P]], base=0, channel_multiplier=0,
                           allow_small_or_imprecise_dtypes=True)
            nc.gpsimd.iota(p1_i, [[P, NBLK]], base=0, channel_multiplier=1, allow_small_or_imprecise_dtypes=True)
            nc.gpsimd.iota(p1_k, [[0, NBLK]], base=0, channel_multiplier=1, allow_small_or_imprecise_dtypes=True)
            nc.gpsimd.iota(pcol[:, :], [[0, 1]], base=0, channel_multiplier=1, allow_small_or_imprecise_dtypes=True)
            nc.gpsimd.memset(ones[:, :], 1.0)
            link(pool, "pool", nc.gpsimd.memset(ident[:, :], 0.0))
            nc.gpsimd.affine_select(out=ident[:, :], in_=ident[:, :], compare_op=ALU.not_equal, fill=1.0, base=0,
                                    pattern=[[-1, P]], channel_multiplier=1).then_inc(S("consts"), 1)
            pool.wait_ge(S("tiles_known"), 1)
            for name, arr in (("dst", "dst"), ("src", "src"), ("typ", "edge_type_8"), ("wgt", "edge_weight")):
                for j in range(NBLK):
                    pool.indirect_dma_start(out=p1_g[name][:, j * P:(j + 1) * P], out_offset=None, in_=A[arr],
                                            in_offset=bass.IndirectOffsetOnAxis(ap=p1_ti[:, j:j + 1], axis=0)
                                            ).then_inc(S(f"g_{name}"), 16)
            pool.wait_ge(S("g_wgt"), 16 * NBLK)
            barrier(pool, 1)
            nc.gpsimd.iota(p3_iota, [[1, N]], base=-CENTRE, channel_multiplier=0,
                           allow_small_or_imprecise_dtypes=True)
            barrier(pool, 2)
            with pool.Fori(0, NB // 2) as b2:
                for j in range(2):
                    nc.gpsimd.tensor_copy(p3_idx[j], xwi_t[:, ds(b2 * (2 * U) + j * U, U)]).then_inc(S("idx3"), 1)
                    pool.wait_ge(S("idx3"), b2 * 2 + j + 1)
                    hold(pool)
                    for k in range(U):
                        pool.wait_ge(S("slot3_free"), b2 * (2 * U) + (j * U + k + 1))
                        hold(pool)
                        pool.indirect_dma_start(out=p3_msg[k], out_offset=None, in_=d_xw,
                                                in_offset=bass.IndirectOffsetOnAxis(ap=p3_idx[j][:, k:k + 1], axis=0)
                                                ).then_inc(S(f"g_msg{k}"), 16)
            barrier(pool, 3)
            pool.wait_ge(S("sc_max"), 1)
            nc.gpsimd.partition_all_reduce(p5_mm, p5_m, P, RMAX).then_inc(S("sc_gmax"), 1)
            pool.wait_ge(S("sc_sum"), 1)
            nc.gpsimd.partition_all_reduce(p5_zz, p5_z, P, RADD).then_inc(S("sc_gsum"), 1)
            barrier(pool, 4)
            barrier(pool, 5)
            barrier(pool, 6)
            with pool.Fori(0, NIT) as it:
                for h in range(2):
                    pool.wait_ge(S("xs_made"), it * G + (h + 1) * U)
                    pool.wait_ge(S("q_used"), it * G + (h + 1) * U)
                    hold(pool)
                    nc.gpsimd.tensor_copy(p8_idx[h][:, 0:U], src_t[:, ds(it * G + h * U, U)])
                    nc.gpsimd.tensor_copy(p8_idx[h][:, U:G], dst_t[:, ds(it * G + h * U, U)]
                                          ).then_inc(S("idx8"), 1)
                    pool.wait_ge(S("idx8"), it * 2 + (h + 1))
                    hold(pool)
                    for k in range(U):
                        j = h * U + k
                        pool.wait_ge(S("xs_made"), it * G + (j + 1))
                        hold(pool)
                        pool.indirect_dma_start(out=p8_xg[j], out_offset=None, in_=d_x,
                                                in_offset=bass.IndirectOffsetOnAxis(ap=p8_idx[h][:, k:k + 1], axis=0)
                                                ).then_inc(S(f"g_x{j}"), 16)
                        pool.wait_ge(S("q_used"), it * G + (j + 1))
                        hold(pool)
                        pool.indirect_dma_start(out=p8_qg[j], out_offset=None, in_=d_q,
                                                in_offset=bass.IndirectOffsetOnAxis(
                                                    ap=p8_idx[h][:, U + k:U + k + 1], axis=0)
                                                ).then_inc(S(f"g_q{j}"), 16)
            for n in range(7, 11):
                barrier(pool, n)

        @block.scalar
        def _(act):
            barrier(act, 1)
            for w in range(NW):
                act.wait_ge(S("xw_mm"), w + 1)
                if w >= 2:
                    act.wait_ge(S(f"st_xw{w % 2}"), 16 * (w // 2))
                nc.scalar.activation(p2_o[w % 2], ps[:, 4 + w % 2, :], ACT.Copy).then_inc(S("xw_out"), 1)
            barrier(act, 2)
            with act.Fori(0, NW) as w:
                act.wait_ge(S("win3"), w + 1)
                hold(act)
                nc.scalar.activation(agg_f[:, ds(w * D, D)], ps[:, 7, 0:D], ACT.Copy)
                act.wait_ge(S("st_adj"), w * 16)
                hold(act)
                nc.scalar.activation(p3_ev, psf[:, 0:N], ACT.Copy).then_inc(S("adj_out"), 1)
            barrier(act, 3)
            act.wait_ge(S("ln_var"), 1)
            nc.scalar.activation(st[:, 4, :], st[:, 3, :], ACT.Sqrt).then_inc(S("ln_sd"), 1)
            for w in range(NW):
                act.wait_ge(S("sc_mm"), w + 1)
                nc.scalar.activation(p5_hw[:, w * 256:(w + 1) * 256], ps[:, 6 + w % 2, 0:256], ACT.Copy
                                     ).then_inc(S("hw_out"), 1)
            act.wait_ge(S("sc_sub"), 1)
            nc.scalar.activation(p5_e, p5_e, ACT.Exp).then_inc(S("sc_exp"), 1)
            barrier(act, 4)
            for w in range(NW):
                for g in range(7):
                    cols = min(512, NP - g * 512)
                    act.wait_ge(S("at_tr"), 7 * w + g + 1)
                    if w >= 1:
                        act.wait_ge(S("z_mm"), 7 * (w - 1) + g + 1)
                        act.wait_ge(S("deg_red"), 7 * (w - 1) + g + 1)
                    nc.scalar.activation(p5_at[:, g * 512:g * 512 + cols], ps[:, (7 * w + g) % 4, 0:cols], ACT.Copy
                                         ).then_inc(S("at_out"), 1)
            act.wait_ge(S("elu_min"), 1)
            nc.scalar.activation(t1[:, :, :], t1[:, :, :], ACT.Exp).then_inc(S("elu_exp"), 1)
            act.wait_ge(S("ln_var"), 2)
            nc.scalar.activation(st[:, 4, :], st[:, 3, :], ACT.Sqrt).then_inc(S("ln_sd"), 1)
            barrier(act, 5)
            for w in range(NW):
                act.wait_ge(S("q_mm"), w + 1)
                if w >= 2:
                    act.wait_ge(S(f"st_q{w % 2}"), 16 * (w // 2))
                nc.scalar.activation(p8_qo[w % 2][:, 0:OK], ps[:, 4 + w % 2, 0:OK], ACT.Copy).then_inc(S("q_out"), 1)
                nc.scalar.activation(self_o[:, w, :], ps[:, 4 + w % 2, OK:OK + D], ACT.Copy
                                     ).then_inc(S("self_out"), 1)
            barrier(act, 6)
            act.sem_inc(S("xt_out"), 2)

            def xs_out(j, i):
                act.wait_ge(S("xs_tr"), i + 5)
                act.wait_ge(S("tp_mm"), i + 1)
                nc.scalar.activation(p8_xt[j % 2], psf[:, (j % 2) * 1024:(j % 2) * 1024 + XC * P], ACT.Copy
                                     ).then_inc(S("xt_out"), 1)

            def hid_out(h, n):
                act.wait_ge(S("hid_mm"), n + 1)
                nc.scalar.activation(p8_hid[h], ps[:, 5, :], ACT.Relu, bias=p8_b1).then_inc(S("hid_out"), 1)

            def act_tiles(it, last):
                for j in range(G):
                    if not (last and j == G - 1):
                        xs_out(j + 1, it * G + (j + 1))
                    if j == 2:
                        act.wait_ge(S("w_mm"), it * G)
                        hid_out(1, it * 2 + 1)
                    if j == 6 and not last:
                        act.wait_ge(S("w_mm"), it * G + U)
                        hid_out(0, it * 2 + 2)

            xs_out(0, 0)
            hid_out(0, 0)
            with act.Fori(0, NIT - 1) as it:
                act_tiles(it, False)
            act_tiles(NIT - 1, True)
            barrier(act, 7)
            act.wait_ge(S("ex_sub"), 1)
            nc.scalar.activation(pS_a[0:SCP, :], pS_a[0:SCP, :], ACT.Exp).then_inc(S("ex_done"), 1)
            barrier(act, 8)
            with act.Fori(0, NW) as w:
                act.wait_ge(S("winB"), w + 1)
                hold(act)
                nc.scalar.activation(pB_acc[:, ds(w * VW, VW)], ps[:, 0, 0:VW], ACT.Copy).then_inc(S("accB"), 1)
            barrier(act, 9)
            act.wait_ge(S("bn_var"), 1)
            nc.scalar.activation(pB_n[:, 0:D], pB_n[:, 0:D], ACT.Sqrt).then_inc(S("bn_sd"), 1)
            act.wait_ge(S("ln_var"), 3)
            nc.scalar.activation(st[:, 4, :], st[:, 3, :], ACT.Sqrt).then_inc(S("ln_sd"), 1)
            nc.scalar.activation(dinv[:, :], deg[:, :], ACT.Sqrt).then_inc(S("deg_sd"), 1)
            barrier(act, 10)
            act.wait_ge(S("out_mm"), NW)
            nc.scalar.activation(pD_oT[:, 0:N], psf[0:D, 0:N], ACT.Copy).then_inc(S("oT"), 1)
            act.wait_ge(S("ln_var"), 4)
            nc.scalar.activation(st[:, 4, :], st[:, 3, :], ACT.Sqrt).then_inc(S("ln_sd"), 1)

        @block.vector
        def _(dve):
            V = nc.vector

            def L(ins):
                link(dve, "dve", ins)

            def bw(a, n=D):
                return a.unsqueeze(2).to_broadcast([P, NW, n])

            def layer_norm(j):
                L(V.tensor_reduce(out=st[:, 0, :], in_=t1[:, :, :], axis=AX.X, op=ALU.add))
                L(V.tensor_scalar(st[:, 1, :], st[:, 0, :], 1.0 / D, None, ALU.mult))
                L(V.tensor_tensor(t1[:, :, :], t1[:, :, :], bw(st[:, 1, :]), ALU.subtract))
                L(V.tensor_tensor(agg[:, :, :], t1[:, :, :], t1[:, :, :], ALU.mult))
                L(V.tensor_reduce(out=st[:, 2, :], in_=agg[:, :, :], axis=AX.X, op=ALU.add))
                V.tensor_scalar(st[:, 3, :], st[:, 2, :], 1.0 / D, 1e-5, ALU.mult, ALU.add).then_inc(S("ln_var"), 1)
                dve.wait_ge(S("ln_sd"), j + 1)
                L(V.reciprocal(st[:, 5, :], st[:, 4, :]))
                L(V.tensor_tensor(x[:, :, :], t1[:, :, :], bw(st[:, 5, :]), ALU.mult))

            def x_transposes(tag):
                for w in range(NW):
                    dve.wait_ge(S("xT_tr"), tag * NW + w + 1)
                    V.tensor_copy(xT[:, w * P:(w + 1) * P], ps[0:D, w % 4, 0:P]).then_inc(S("xT_out"), 1)

            dve.wait_ge(S("ld_dst"), 16)
            L(V.memset(p1_cnt, 0.0))
            L(V.tensor_copy(p1_dst, p1_dst_i))
            L(V.tensor_scalar(p1_lt, p1_dst, float(NP - 1), None, ALU.min))
            L(V.tensor_copy(dst_t[:, :], p1_lt))
            for w in range(1, NW):
                L(V.tensor_scalar(p1_lt, p1_dst, float(P * w), None, ALU.is_lt))
                L(V.tensor_reduce(out=p1_cnt[:, w - 1:w], in_=p1_lt, axis=AX.X, op=ALU.add))
            V.memset(p1_ts, 0.0).then_inc(S("cnt"), 1)
            V.memset(p1_sb, 0.0)
            L(V.memset(p1_off, 0.0))
            dve.wait_ge(S("cnt_mm"), 1)
            L(V.tensor_copy(p1_bi, ps[:, 0, 0:32]))
            L(V.tensor_scalar(p1_bi, p1_bi, 7, None, ALU.arith_shift_right))
            L(V.tensor_copy(p1_te, p1_bi))
            L(V.memset(p1_te[:, NW - 1:NW], float(REAL_TILES - 1)))
            L(V.tensor_copy(p1_ts[:, 1:NW], p1_te[:, 0:NW - 1]))
            L(V.tensor_tensor(p1_nb[:, 0:NW], p1_te[:, 0:NW], p1_ts[:, 0:NW], ALU.subtract))
            L(V.tensor_scalar(p1_nb[:, 0:NW], p1_nb[:, 0:NW], float(U), None, ALU.add))
            L(V.tensor_copy(p1_nbi[:, 0:NW], p1_nb[:, 0:NW]))
            L(V.tensor_scalar(p1_nbi[:, 0:NW], p1_nbi[:, 0:NW], 2, None, ALU.arith_shift_right))
            L(V.tensor_copy(p1_nb[:, 0:NW], p1_nbi[:, 0:NW]))
            L(V.tensor_tensor_scan(p1_cum[:, 0:NW], ones[:, 0:NW], p1_nb[:, 0:NW], 0.0, ALU.mult, ALU.add))
            L(V.tensor_copy(p1_sb[:, 1:NW], p1_cum[:, 0:NW - 1]))
            L(V.memset(p1_sb[:, NW:NW + 1], float(NB)))
            L(V.tensor_copy(blk_i[:, :], p1_sb[:, 0:NW + 1]))
            L(V.tensor_scalar(p1_cum[:, 0:NW], p1_sb[:, 0:NW], float(U), None, ALU.mult))
            L(V.tensor_tensor(p1_off[:, 0:NW], p1_ts[:, 0:NW], p1_cum[:, 0:NW], ALU.subtract))
            L(V.tensor_tensor(p1_doff[:, 0:NW - 1], p1_off[:, 1:NW], p1_off[:, 0:NW - 1], ALU.subtract))
            m3 = p1_mask.rearrange("p (b w) -> p b w", w=24)
            o3 = p1_mo.rearrange("p (b w) -> p b w", w=24)
            dve.wait_ge(S("consts"), 1)
            L(V.tensor_tensor(m3, p1_cum[:, 1:NW].unsqueeze(1).to_broadcast([P, NBLK, 24]),
                              p1_i.unsqueeze(2).to_broadcast([P, NBLK, 24]), ALU.is_le))
            L(V.tensor_tensor(o3, m3, p1_doff[:, 0:NW - 1].unsqueeze(1).to_broadcast([P, NBLK, 24]), ALU.mult))
            L(V.tensor_reduce(out=p1_w, in_=m3, axis=AX.X, op=ALU.add))
            L(V.tensor_reduce(out=p1_o, in_=o3, axis=AX.X, op=ALU.add))
            L(V.tensor_copy(p1_ki, p1_k))
            L(V.tensor_scalar(p1_ki, p1_ki, U - 1, None, ALU.bitwise_and))
            L(V.tensor_copy(p1_k, p1_ki))
            L(V.tensor_tensor(p1_t, p1_i, p1_o, ALU.add))
            L(V.tensor_tensor(p1_t, p1_t, p1_k, ALU.subtract))
            L(V.tensor_scalar(p1_t, p1_t, float(NT), None, ALU.min))
            L(V.tensor_tensor(p1_t, p1_t, p1_k, ALU.add))
            V.tensor_copy(p1_ti, p1_t).then_inc(S("tiles_known"), 1)
            L(V.tensor_scalar(p1_w, p1_w, float(P), None, ALU.mult))
            V.tensor_scalar(realrow[:, :], pcol[:, :], float(LAST), None, ALU.is_lt)
            g3 = {n: p1_g[n].rearrange("p (b e) -> p b e", e=P) for n in p1_g}
            dve.wait_ge(S("g_dst"), 16 * NBLK)
            L(V.tensor_copy(p1_f, p1_g["dst"]))
            L(V.tensor_tensor(p1_rel.rearrange("p (b e) -> p b e", e=P), p1_f.rearrange("p (b e) -> p b e", e=P),
                              p1_w.unsqueeze(2).to_broadcast([P, NBLK, P]), ALU.subtract))
            L(V.tensor_scalar(p1_a, p1_rel, 0.0, None, ALU.is_ge))
            L(V.tensor_scalar(p1_b, p1_rel, float(P), None, ALU.is_lt))
            L(V.tensor_tensor(p1_a, p1_a, p1_b, ALU.mult))
            L(V.tensor_scalar(p1_rel, p1_rel, 1.0, None, ALU.add))
            L(V.tensor_tensor(p1_rel, p1_rel, p1_a, ALU.mult))
            L(V.tensor_scalar(p1_rel, p1_rel, -1.0, None, ALU.add))
            dve.wait_ge(S("g_src"), 16 * NBLK)
            dve.wait_ge(S("g_typ"), 16 * NBLK)
            V.tensor_copy(p1_s, p1_g["src"])
            L(V.tensor_copy(p1_b, p1_g["typ"]))
            dve.wait_ge(S("g_wgt"), 16 * NBLK)
            V.scalar_tensor_tensor(out=p1_x, in0=p1_s, scalar=float(R), in1=p1_b, op0=ALU.mult, op1=ALU.add
                                   ).then_inc(S("tab_in"), 1)
            dve.wait_ge(S("tab_tr"), 1)
            for r, (dst_ap, srcps) in enumerate(((rel_t[:, :], 0), (xwi_t[:, :], 4), (w_t[:, :], 6))):
                V.tensor_copy(dst_ap, psf[:, srcps * 512:srcps * 512 + NSP])
            V.tensor_scalar(srcc_t[:, :], psf[:, 1024:1024 + NSP], float(-CENTRE), None, ALU.add
                            ).then_inc(S("tab_out"), 1)
            barrier(dve, 1)
            x_transposes(0)
            V.memset(p3_z, 0.0)
            barrier(dve, 2)
            with dve.Fori(0, NB) as b:
                for k in range(U):
                    i = b * U + k
                    dve.wait_ge(S("slot3_free"), b * U + (k + 1))
                    V.tensor_scalar(p3_ohs[k], p3_iota, srcc_t[:, ds(i, 1)], None, ALU.is_equal)
                    V.tensor_scalar(p3_ohd[k], iota128[:, :], rel_t[:, ds(i, 1)], None, ALU.is_equal)
                    V.tensor_scalar(p3_ohw[k], iota128[:, :], rel_t[:, ds(i, 1)], w_t[:, ds(i, 1)],
                                    ALU.is_equal, ALU.mult).then_inc(S("oh3"), 1)
            barrier(dve, 3)
            L(V.tensor_tensor(t1[:, :, :], x[:, :, :], agg[:, :, :], ALU.add))
            layer_norm(0)
            V.memset(p5_adj[0][:, N:NP], 0.0).then_inc(S("x_ready"), 1)
            V.memset(p5_adj[1][:, N:NP], 0.0).then_inc(S("adj_zero"), 1)
            x_transposes(1)
            s3 = p5_s.rearrange("p (w h) -> p w h", h=H1)
            e3 = p5_e.rearrange("p (w h) -> p w h", h=H1)
            for w in range(NW):
                dve.wait_ge(S("sc_mm"), w + 1)
                pr = p5_pr[w % 2].rearrange("p (h e) -> p h e", h=H1)
                L(V.tensor_tensor(pr, ps[:, 4 + w % 2, 0:256].rearrange("p (h e) -> p h e", h=H1),
                                  x[:, w, :].unsqueeze(1).to_broadcast([P, H1, D]), ALU.mult))
                V.tensor_reduce(out=s3[:, w, :], in_=pr, axis=AX.X, op=ALU.add).then_inc(S("sc_used"), 1)
            dve.wait_ge(S("sc_used"), NW)
            L(V.tensor_scalar(p5_s, p5_s, D ** -0.5, None, ALU.mult))
            L(V.tensor_scalar(small[:, 0:1], realrow[:, :], BIG, -BIG, ALU.mult, ALU.add))
            L(V.tensor_tensor(s3[:, NW - 1, :], s3[:, NW - 1, :], small[:, 0:1].to_broadcast([P, H1]), ALU.add))
            V.tensor_reduce(out=p5_m, in_=p5_s.rearrange("p (w h) -> p h w", h=H1), axis=AX.X, op=ALU.max
                            ).then_inc(S("sc_max"), 1)
            dve.wait_ge(S("sc_gmax"), 1)
            V.tensor_tensor(e3, s3, p5_mm.unsqueeze(1).to_broadcast([P, NW, H1]), ALU.subtract
                            ).then_inc(S("sc_sub"), 1)
            dve.wait_ge(S("sc_exp"), 1)
            V.tensor_reduce(out=p5_z, in_=p5_e.rearrange("p (w h) -> p h w", h=H1), axis=AX.X, op=ALU.add
                            ).then_inc(S("sc_sum"), 1)
            dve.wait_ge(S("sc_gsum"), 1)
            L(V.reciprocal(p5_ri, p5_zz))
            L(V.tensor_tensor(e3, e3, p5_ri.unsqueeze(1).to_broadcast([P, NW, H1]), ALU.mult))
            dve.wait_ge(S("hw_out"), NW)
            hw4 = p5_hw.rearrange("p (g e) -> p g e", e=D)
            L(V.tensor_tensor(hw4, hw4, p5_e.unsqueeze(2).to_broadcast([P, NW * H1, D]), ALU.mult))
            L(V.tensor_reduce(out=p5_zt.rearrange("p (w e) -> p w e", e=D),
                              in_=p5_hw.rearrange("p (w h e) -> p w e h", h=H1, e=D), axis=AX.X, op=ALU.add))
            V.memset(deg[:, :], 1.0)
            barrier(dve, 4)
            for w in range(NW):
                for g in range(7):
                    cols = min(512, NP - g * 512)
                    dve.wait_ge(S("at_out"), 7 * w + g + 1)
                    V.tensor_reduce(out=t1[:, w % 2, g * 4:g * 4 + cols // P],
                                    in_=p5_at[:, g * 512:g * 512 + cols].rearrange("p (c e) -> p c e", e=P), axis=AX.X, op=ALU.add
                                    ).then_inc(S("deg_red"), 1)
                dve.wait_ge(S("deg_red"), 7 * w + 7)
                L(V.tensor_tensor(deg[:, :], deg[:, :], t1[:, w % 2, 0:NW], ALU.add))
                dve.wait_ge(S("z_mm"), 7 * w + 7)
                V.tensor_copy(agg[:, w, :], ps[:, 4 + w % 2, 0:D]).then_inc(S("z_out"), 1)
            dve.wait_ge(S("z_out"), NW)
            V.tensor_scalar(t1[:, :, :], agg[:, :, :], 0.0, None, ALU.min).then_inc(S("elu_min"), 1)
            L(V.tensor_scalar(agg[:, :, :], agg[:, :, :], 0.0, -1.0, ALU.max, ALU.add))
            dve.wait_ge(S("elu_exp"), 1)
            L(V.tensor_tensor(agg[:, :, :], agg[:, :, :], t1[:, :, :], ALU.add))
            L(V.tensor_tensor(t1[:, :, :], x[:, :, :], agg[:, :, :], ALU.add))
            layer_norm(1)
            barrier(dve, 5)
            x_transposes(2)
            V.memset(p8_w2, 0.0)
            for xs in p8_xs:
                V.memset(xs[:, S9 * D:XC * P], 0.0)
            V.memset(p8_c[D:P, 4 * 2 * OK:XC * 2 * OK], 0.0).then_inc(S("w2_zero"), 1)
            barrier(dve, 6)
            dve.sem_inc(S("xs_made"), G)
            dve.sem_inc(S("q_used"), G)
            dve.sem_inc(S("kv_made"), 2)

            def outer(j, i, it):
                dve.wait_ge(S(f"g_x{j}"), it * 16 + 16)
                dve.wait_ge(S("xs_tr"), i + 1)
                V.tensor_tensor(p8_xs[j % 4][:, 0:S9 * D].rearrange("p (s d) -> p s d", d=D),
                                p8_xg[j].unsqueeze(1).to_broadcast([P, S9, D]),
                                p8_sh[:, ds(i * S9, S9)].unsqueeze(2).to_broadcast([P, S9, D]), ALU.mult
                                ).then_inc(S("xs_made"), 1)

            def products(j, i, it):
                kv = p8_kv[:, j * 2 * OK:(j + 1) * 2 * OK]
                dve.wait_ge(S("w_mm"), i + 1)
                V.tensor_tensor(p8_wk[j % 2], ps[:, 6 + j % 2, 256:512], p8_b2, ALU.add).then_inc(S("wk_made"), 1)
                dve.wait_ge(S(f"st_v{j // U}"), it * 16)
                dve.wait_ge(S("wk_made"), i + 1)
                V.tensor_tensor(kv, ps[:, 6 + j % 2, 0:256], p8_wk[j % 2], ALU.mult).then_inc(S("kv_made"), 1)
                dve.wait_ge(S(f"g_q{j}"), it * 16 + 16)
                dve.wait_ge(S("kv_made"), i + 3)
                V.tensor_tensor(p8_pr[j % 2], kv[:, 0:OK], p8_qg[j], ALU.mult).then_inc(S("q_used"), 1)
                dve.wait_ge(S("q_used"), i + (G + 1))
                hold(dve)
                V.tensor_reduce(out=lg[:, ds(i * H2, H2)], in_=p8_pr[j % 2].rearrange("p (h c) -> p h c", h=H2),
                                axis=AX.X, op=ALU.add).then_inc(S("lg_made"), 1)

            def dve_tiles(it, last):
                for j in range(G):
                    if j < G - 2:
                        outer(j + 2, it * G + (j + 2), it)
                    elif not last:
                        outer(j + 2 - G, it * G + (j + 2), it + 1)
                    products(j, it * G + j, it)

            outer(0, 0, 0)
            outer(1, 1, 0)
            with dve.Fori(0, NIT - 1) as it:
                dve_tiles(it, False)
            dve_tiles(NIT - 1, True)
            dve.wait_ge(S("lg_made"), NT)
            barrier(dve, 7)
            rows_g = [min(4, NG - 4 * g) for g in range(-(-NG // 4))]
            for g, n in enumerate(rows_g):
                dve.wait_ge(S("lg_tr"), g + 1)
                if g >= 2:
                    dve.wait_ge(S(f"st_lg{g % 2}"), 16 * (g // 2))
                V.tensor_copy(pA_row[g % 2][:, 0:n * P], ps[:, g % 2, 0:n * P]).then_inc(S("lg_row"), 1)
            q = slice(0, SCP)
            dve.wait_ge(S("lg_row"), len(rows_g))
            V.memset(pS_l, 0.0).then_inc(S("lg_gone"), 1)
            dve.wait_ge(S("ld_scan"), 16 * (H2 + 1))
            a3 = pS_a[q, :].rearrange("p (h j) -> p h j", h=H2)
            L(V.tensor_copy(pS_dv[q, :], pS_di[q, :]))
            L(V.memset(pS_v1[q, :], 0.0))
            L(V.tensor_tensor_scan(pS_pm[q, :], pS_v1[q, :], pS_dv[q, :], -1.0, ALU.add, ALU.max))
            L(V.tensor_copy(pS_l[q, 0:8], pS_pm[q, SCL - 1:SCL].to_broadcast([SCP, 8])))
            V.tensor_copy(pS_l[q, 8:9], pS_l[q, 0:1]).then_inc(S("sc_in"), 1)
            T = [pS_tr[:, i * P:(i + 1) * P] for i in range(8)]
            dve.wait_ge(S("sc_tr"), 1)
            L(V.memset(pS_tr, 0.0))
            L(V.tensor_copy(T[0][:, 0:SCP], ps[0:8, 2, 0:SCP]))
            L(V.memset(T[2][:, 0:1], -1.0))
            L(V.tensor_tensor_scan(T[2][:, 1:SCP], T[1][:, 0:SCP - 1], T[0][:, 0:SCP - 1], -1.0, ALU.add, ALU.max))
            V.memset(T[3][:, 0:1], 0.0).then_inc(S("sc_back"), 1)
            dve.wait_ge(S("sc_bk"), 1)
            L(V.tensor_copy(pS_l[q, 16:24], ps[0:SCP, 3, 0:8]))
            L(V.tensor_scalar(pS_pm[q, :], pS_pm[q, :], pS_l[q, 16:17], None, ALU.max))
            L(V.tensor_tensor(pS_new[q, 1:SCL], pS_dv[q, 1:SCL], pS_pm[q, 0:SCL - 1], ALU.is_gt))
            L(V.tensor_tensor(pS_new[q, 0:1], pS_dv[q, 0:1], pS_l[q, 16:17], ALU.is_gt))
            L(V.tensor_scalar(pS_new[q, :], pS_new[q, :], -BIG, None, ALU.mult))
            L(V.tensor_reduce(out=pS_l[q, 24:25], in_=pS_new[q, :], axis=AX.X, op=ALU.min))
            L(V.tensor_reduce(out=pS_l[q, 25:26], in_=pS_new[q, 1:SCL], axis=AX.X, op=ALU.min))
            for h in range(H2):
                L(V.tensor_tensor_scan(pS_f[q, h * SCL:(h + 1) * SCL], pS_new[q, :], pS_a[q, h * SCL:(h + 1) * SCL],
                                       -BIG, ALU.add, ALU.max))
            f3 = pS_f[q, :].rearrange("p (h j) -> p h j", h=H2)
            L(V.tensor_copy(pS_l[q, 32:40], f3[:, :, SCL - 1]))
            V.tensor_copy(pS_l[q, 40:48], pS_l[q, 24:25].to_broadcast([SCP, 8])).then_inc(S("sc_in"), 1)
            dve.wait_ge(S("sc_tr"), 2)
            V.tensor_copy(T[0][:, 0:SCP], ps[0:8, 2, 0:SCP])
            L(V.tensor_copy(T[1][:, 0:SCP], ps[0:8, 2, P:P + SCP]))
            L(V.memset(T[2][:, 0:1], -BIG))
            L(V.tensor_tensor_scan(T[2][:, 1:SCP], T[1][:, 0:SCP - 1], T[0][:, 0:SCP - 1], -BIG, ALU.add, ALU.max))
            V.memset(T[3][:, 0:1], 0.0).then_inc(S("sc_back"), 1)
            dve.wait_ge(S("sc_bk"), 2)
            L(V.tensor_copy(pS_l[q, 48:56], ps[0:SCP, 3, 0:8]))
            for h in range(H2):
                L(V.tensor_tensor_scan(pS_f[q, h * SCL:(h + 1) * SCL], pS_new[q, :], pS_a[q, h * SCL:(h + 1) * SCL],
                                       pS_l[q, 48 + h:49 + h], ALU.add, ALU.max))
            L(V.memset(pS_v1[q, SCL - 1:SCL], 0.0))
            L(V.tensor_copy(pS_v1[q, 0:SCL - 1], pS_new[q, 1:SCL]))
            bwd = pS_pm
            for h in range(H2):
                L(V.tensor_tensor_scan(bwd[q, ::-1], pS_v1[q, ::-1], pS_f[q, h * SCL:(h + 1) * SCL][:, ::-1],
                                       -BIG, ALU.add, ALU.max))
                L(V.tensor_copy(pS_l[q, 32 + h:33 + h], bwd[q, 0:1]))
            V.tensor_copy(pS_l[q, 40:48], pS_l[q, 25:26].to_broadcast([SCP, 8]))
            L(V.tensor_copy(pS_l[q, 56:64], pS_new[q, 0:1].to_broadcast([SCP, 8])))
            V.memset(T[3][:, 0:1], 0.0).then_inc(S("sc_in"), 1)
            dve.wait_ge(S("sc_tr"), 3)
            V.tensor_copy(T[0][:, 0:SCP], ps[0:8, 2, 0:SCP])
            V.tensor_copy(T[1][:, 0:SCP], ps[0:8, 2, P:P + SCP])
            L(V.tensor_copy(T[4][:, 0:SCP], ps[0:8, 2, 2 * P:2 * P + SCP]))
            L(V.memset(T[5][:, 0:P], -BIG))
            L(V.tensor_copy(T[6][:, 0:SCP], T[1][:, 0:SCP]))
            L(V.tensor_tensor(T[6][:, 0:SCP - 1], T[1][:, 0:SCP - 1], T[4][:, 1:SCP], ALU.add))
            L(V.tensor_tensor_scan(T[5][:, 0:SCP][:, ::-1], T[6][:, 0:SCP][:, ::-1], T[0][:, 0:SCP][:, ::-1],
                                   -BIG, ALU.add, ALU.max))
            L(V.memset(T[2][:, 0:P], -BIG))
            L(V.tensor_tensor(T[2][:, 0:SCP - 1], T[5][:, 1:SCP], T[4][:, 1:SCP], ALU.add))
            V.memset(T[3][:, 0:1], 0.0).then_inc(S("sc_back"), 1)
            dve.wait_ge(S("sc_bk"), 3)
            L(V.tensor_copy(pS_l[q, 48:56], ps[0:SCP, 3, 0:8]))
            for h in range(H2):
                L(V.tensor_tensor_scan(bwd[q, ::-1], pS_v1[q, ::-1], pS_f[q, h * SCL:(h + 1) * SCL][:, ::-1],
                                       pS_l[q, 48 + h:49 + h], ALU.add, ALU.max))
                L(V.tensor_tensor(pS_a[q, h * SCL:(h + 1) * SCL], pS_a[q, h * SCL:(h + 1) * SCL], bwd[q, :],
                                  ALU.subtract))
            V.tensor_scalar(pS_a[q, :], pS_a[q, :], 0.0, None, ALU.min).then_inc(S("ex_sub"), 1)
            dve.wait_ge(S("st_ex"), 16 * H2)
            for g, n in enumerate(rows_g):
                dve.wait_ge(S("ex_tr"), g + 1)
                V.tensor_copy(pB_ex[:, g * 512:g * 512 + n * P], ps[:, g % 2, 0:n * P]).then_inc(S("ex_col"), 1)
            V.memset(pB_ex[:, NT * H2:NTR * H2], 0.0)
            V.memset(pB_z, 0.0)
            L(V.memset(pB_v[0], 0.0))
            V.memset(pB_r, 0.0).then_inc(S("v_zero"), 1)
            barrier(dve, 8)
            dve.sem_inc(S("v_used"), 2 * U)
            with dve.Fori(0, NB // 2) as b2:
                for j in range(2):
                    t = dve.value_load(tile_row[0:1, ds(b2 * (2 * U) + j * U, 1)], min_val=0, max_val=NT)
                    for k in range(U):
                        i = b2 * (2 * U) + (j * U + k)
                        dve.wait_ge(S("slotB_free"), i + 1)
                        V.tensor_scalar(pB_oh[k], iota128[:, :], rel_t[:, ds(i, 1)], None, ALU.is_equal)
                        V.tensor_copy(pB_vx[k][:, OK:VW], pB_ex[:, ds(t * H2 + k * H2, H2)])
                        if k == 0:
                            dve.wait_ge(S(f"ld_v{j}"), b2 * 16 + 16)
                        V.tensor_tensor(pB_vx[k][:, 0:OK].rearrange("p (h c) -> p h c", h=H2),
                                        pB_v[j][:, k * OK:(k + 1) * OK].rearrange("p (h c) -> p h c", h=H2),
                                        pB_ex[:, ds(t * H2 + k * H2, H2)].unsqueeze(2).to_broadcast([P, H2, OK // H2]),
                                        ALU.mult).then_inc(S("v_used"), 1)
            barrier(dve, 9)
            dve.wait_ge(S("accB"), NW)
            ac3 = pB_acc.rearrange("p (w c) -> p w c", c=VW)
            r3 = pB_r.rearrange("p (w h) -> p w h", h=H2)
            L(V.tensor_scalar(r3, ac3[:, :, OK:VW], 1e-16, None, ALU.add))
            L(V.reciprocal(r3, r3))
            for w in range(NW):
                u3 = ac3[:, w, 0:OK].rearrange("p (h c) -> p h c", h=H2)
                V.tensor_tensor(u3, u3, r3[:, w, :].unsqueeze(2).to_broadcast([P, H2, OK // H2]), ALU.mult
                                ).then_inc(S("upd"), 1)
            for w in range(NW):
                dve.wait_ge(S("u_tr"), w + 1)
                if w >= 2:
                    dve.wait_ge(S("u_mm"), w - 1)
                V.tensor_copy(pB_uT[w % 2], ps[:, w % 2, 0:P]).then_inc(S("u_out"), 1)
                dve.wait_ge(S("u_mm"), w + 1)
                V.tensor_tensor(t1[:, w, :], self_o[:, w, :], ps[:, 2 + w % 2, 0:D], ALU.add).then_inc(S("u_add"), 1)
            dve.wait_ge(S("u_add"), NW)
            V.tensor_reduce(out=pB_n[:, 0:D], in_=t1[:, :, :].rearrange("p w d -> p d w"), axis=AX.X, op=ALU.add
                            ).then_inc(S("bn_in"), 1)
            dve.wait_ge(S("bn_mm"), 1)
            L(V.tensor_scalar(pB_n[:, D:2 * D], ps[:, 4, 0:D], 1.0 / N, None, ALU.mult))
            L(V.tensor_tensor(t1[:, :, :], t1[:, :, :], pB_n[:, D:2 * D].unsqueeze(1).to_broadcast([P, NW, D]),
                              ALU.subtract))
            L(V.tensor_scalar(t1[:, NW - 1, :], t1[:, NW - 1, :], realrow[:, :], None, ALU.mult))
            L(V.tensor_tensor(agg[:, :, :], t1[:, :, :], t1[:, :, :], ALU.mult))
            V.tensor_reduce(out=pB_n[:, 0:D], in_=agg[:, :, :].rearrange("p w d -> p d w"), axis=AX.X, op=ALU.add
                            ).then_inc(S("bn_in"), 1)
            dve.wait_ge(S("bn_mm"), 2)
            V.tensor_scalar(pB_n[:, 0:D], ps[:, 4, 0:D], 1.0 / N, 1e-5, ALU.mult, ALU.add).then_inc(S("bn_var"), 1)
            dve.wait_ge(S("bn_sd"), 1)
            L(V.reciprocal(pB_n[:, 2 * D:3 * D], pB_n[:, 0:D]))
            L(V.tensor_tensor(pB_n[:, 2 * D:3 * D], pB_n[:, 2 * D:3 * D], gam[:, 0, :], ALU.mult))
            L(V.tensor_tensor(t1[:, :, :], t1[:, :, :], pB_n[:, 2 * D:3 * D].unsqueeze(1).to_broadcast([P, NW, D]),
                              ALU.mult))
            L(V.tensor_tensor(t1[:, :, :], t1[:, :, :], gam[:, 1, :].unsqueeze(1).to_broadcast([P, NW, D]), ALU.add))
            L(V.tensor_tensor(t1[:, :, :], t1[:, :, :], x[:, :, :], ALU.add))
            layer_norm(2)
            dve.wait_ge(S("deg_sd"), 1)
            L(V.reciprocal(dinv[:, :], dinv[:, :]))
            barrier(dve, 10)
            dve.wait_ge(S("w3_tr"), 1)
            V.tensor_copy(w3T[:, :], ps[0:D, 6, 0:D]).then_inc(S("w3_out"), 1)
            x_transposes(3)
            for w in range(NW):
                dve.wait_ge(S("h_mm"), w + 1)
                V.tensor_tensor(t1[:, w, :], ps[:, 4 + w % 2, 0:D], gam[:, 2, :], ALU.add).then_inc(S("h_add"), 1)
            dve.wait_ge(S("h_add"), NW)
            V.tensor_tensor(t1[:, :, :], t1[:, :, :], bw(dinv[:, :]), ALU.mult).then_inc(S("g_ready"), 1)
            V.memset(pD_oT[:, N:NP], 0.0).then_inc(S("oT_zero"), 1)
            for w in range(NW):
                dve.wait_ge(S("o_tr"), w + 1)
                V.tensor_copy(agg[:, w, :], ps[:, w % 4, 0:D]).then_inc(S("o_out"), 1)
            dve.wait_ge(S("o_out"), NW)
            L(V.tensor_tensor(t1[:, :, :], t1[:, :, :], agg[:, :, :], ALU.add))
            L(V.tensor_tensor(t1[:, :, :], t1[:, :, :], bw(dinv[:, :]), ALU.mult))
            L(V.tensor_tensor(t1[:, :, :], t1[:, :, :], x[:, :, :], ALU.add))
            layer_norm(3)
            V.memset(small[:, 2:3], 0.0).then_inc(S("final"), 1)

        @block.tensor
        def _(pe):
            def mm(out, lhsT, rhs, start=True, stop=True, **kw):
                return nc.tensor.matmul(out, lhsT, rhs, start=start, stop=stop, **kw)

            def tr(out, in_):
                k = in_.shape[0]
                return nc.tensor.transpose(out, in_, ident[0:k, 0:k])

            def x_transposes(tag):
                for w in range(NW):
                    if w >= 4:
                        pe.wait_ge(S("xT_out"), tag * NW + w - 3)
                    tr(ps[0:D, w % 4, 0:P], x[:, w, :]).then_inc(S("xT_tr"), 1)
                pe.wait_ge(S("xT_out"), tag * NW + NW)

            pe.wait_ge(S("cnt"), 1)
            pe.wait_ge(S("consts"), 1)
            mm(ps[:, 0, 0:32], ones[:, :], p1_cnt).then_inc(S("cnt_mm"), 1)
            pe.wait_ge(S("tab_in"), 1)
            for j, t in enumerate((p1_rel, p1_s, p1_x, p1_g["wgt"])):
                for c_ in range(NBLK):
                    last = tr(psf[:, j * 1024 + c_ * P:j * 1024 + (c_ + 1) * P], t[:, c_ * P:(c_ + 1) * P])
            last.then_inc(S("tab_tr"), 1)
            pe.wait_ge(S("ld_x"), 32)
            barrier(pe, 1)
            x_transposes(0)
            for w in range(NW):
                if w >= 2:
                    pe.wait_ge(S("xw_out"), w - 1)
                mm(ps[:, 4 + w % 2, :], xT[:, w * P:(w + 1) * P], w0[:, :, :].rearrange("f r o -> f (r o)")
                   ).then_inc(S("xw_mm"), 1)
            barrier(pe, 2)
            pe.sem_inc(S("slot3_free"), U)
            with pe.Fori(0, NW) as w:
                pe.wait_ge(S("adj_out"), w)
                for g in range(8):
                    mm(ps[:, g, :], p3_z[:, 0:P], p3_z, start=True, stop=False, skip_group_check=True)
                b0 = pe.value_load(blk_i[0:1, ds(w, 1)], min_val=0, max_val=NB)
                b1 = pe.value_load(blk_i[0:1, ds(w + 1, 1)], min_val=1, max_val=NB)
                with pe.Fori(b0, b1) as b:
                    for k in range(U):
                        pe.wait_ge(S("oh3"), b * U + (k + 1))
                        for g in range(7):
                            cols = min(512, N - g * 512)
                            mm(ps[:, g, 0:cols], p3_ohd[k], p3_ohs[k][:, g * 512:g * 512 + cols],
                               start=False, stop=False, skip_group_check=True)
                        pe.wait_ge(S(f"g_msg{k}"), b * 16 + 16)
                        mm(ps[:, 7, 0:D], p3_ohw[k], p3_msg[k], start=False, stop=False, skip_group_check=True
                           ).then_inc(S("slot3_free"), 1)
                mm(ps[:, 7, 0:2], p3_z[:, 0:P], p3_z[:, 0:2], start=False, stop=True, skip_group_check=True
                   ).then_inc(S("win3"), 1)
            barrier(pe, 3)
            pe.wait_ge(S("x_ready"), 1)
            x_transposes(1)
            for w in range(NW):
                if w >= 2:
                    pe.wait_ge(S("sc_used"), w - 1)
                    pe.wait_ge(S("hw_out"), w - 1)
                for a in range(2):
                    last = mm(ps[:, 4 + 2 * a + w % 2, 0:H1 * D], xT[:, w * P:(w + 1) * P],
                              w1[:, a, :, :].rearrange("f h o -> f (h o)"))
                last.then_inc(S("sc_mm"), 1)
            barrier(pe, 4)
            for w in range(NW):
                pe.wait_ge(S(f"ld_adj{w % 2}"), 16 * (w // 2 + 1))
                for g in range(9):
                    if g < 7:
                        n = 7 * w + g
                        if n >= 4:
                            pe.wait_ge(S("at_out"), n - 3)
                        for c_ in range(g * 4, min(g * 4 + 4, NW)):
                            last = tr(ps[:, n % 4, (c_ % 4) * P:(c_ % 4 + 1) * P],
                                      p5_adj[w % 2][:, c_ * P:(c_ + 1) * P])
                        last.then_inc(S("at_tr"), 1)
                    if g >= 2:
                        gg = g - 2
                        pe.wait_ge(S("at_out"), 7 * w + gg + 1)
                        if gg == 0 and w >= 2:
                            pe.wait_ge(S("z_out"), w - 1)
                        for c_ in range(gg * 4, min(gg * 4 + 4, NW)):
                            last = mm(ps[:, 4 + w % 2, 0:D], p5_at[:, c_ * P:(c_ + 1) * P],
                                      p5_zt[:, c_ * D:(c_ + 1) * D], start=(c_ == 0), stop=(c_ == NW - 1))
                        last.then_inc(S("z_mm"), 1)
            barrier(pe, 5)
            x_transposes(2)
            for w in range(NW):
                if w >= 2:
                    pe.wait_ge(S("self_out"), w - 1)
                mm(ps[:, 4 + w % 2, 0:OK + D], xT[:, w * P:(w + 1) * P], w2n[:, :]).then_inc(S("q_mm"), 1)
            barrier(pe, 6)
            pe.sem_inc(S("xs_tr"), 4)
            pe.sem_inc(S("tp_mm"), 2)

            def xs_transpose(j, i):
                pe.wait_ge(S("xs_made"), i + (G + 1))
                pe.wait_ge(S("xt_out"), i + 1)
                o = (j % 2) * 1024
                for c_ in range(XC):
                    last = tr(psf[:, o + c_ * P:o + (c_ + 1) * P], p8_xs[j % 4][:, c_ * P:(c_ + 1) * P])
                last.then_inc(S("xs_tr"), 1)

            def hidden(h, n, turn):
                pe.wait_ge(S(f"ld_at{h}"), turn * 16 + 16)
                pe.wait_ge(S("hid_out"), n)
                mm(ps[:, 5, :], p8_w1, p8_att[h]).then_inc(S("hid_mm"), 1)

            def tensor_product(j, i):
                pe.wait_ge(S("xt_out"), i + 3)
                pe.wait_ge(S("kv_made"), i + 1)
                for c_ in range(XC):
                    last = mm(ps[:, 6 + j % 2, 0:2 * OK], p8_xt[j % 2][:, c_ * P:(c_ + 1) * P],
                              p8_c[:, c_ * 2 * OK:(c_ + 1) * 2 * OK], start=(c_ == 0), stop=(c_ == XC - 1))
                last.then_inc(S("tp_mm"), 1)

            def pe_tiles(it, last_turn):
                for j in range(G):
                    if not (last_turn and j == G - 1):
                        xs_transpose(j + 1, it * G + (j + 1))
                    if j == 2:
                        hidden(1, it * 2 + 1, it)
                    if j == 6 and not last_turn:
                        hidden(0, it * 2 + 2, it + 1)
                    tensor_product(j, it * G + j)
                    if j % U == 0:
                        pe.wait_ge(S("hid_out"), it * 2 + (j // U + 1))
                    mm(ps[:, 6 + j % 2, 2 * OK:4 * OK], p8_hid[j // U][:, (j % U) * P:(j % U + 1) * P], p8_w2
                       ).then_inc(S("w_mm"), 1)

            xs_transpose(0, 0)
            hidden(0, 0, 0)
            with pe.Fori(0, NIT - 1) as it:
                pe_tiles(it, False)
            pe_tiles(NIT - 1, True)
            barrier(pe, 7)
            rows_g = [min(4, NG - 4 * g) for g in range(-(-NG // 4))]
            for g, n in enumerate(rows_g):
                if g >= 2:
                    pe.wait_ge(S("lg_row"), g - 1)
                for c_ in range(n):
                    last = tr(ps[:, g % 2, c_ * P:(c_ + 1) * P], lg[:, (g * 4 + c_) * P:(g * 4 + c_ + 1) * P])
                last.then_inc(S("lg_tr"), 1)
            T = [pS_tr[:, i * P:(i + 1) * P] for i in range(8)]
            for r, cols in enumerate(((0,), (32, 40), (32, 40, 56))):
                pe.wait_ge(S("sc_in"), r + 1)
                for j, c_ in enumerate(cols):
                    last = tr(ps[0:8, 2, j * P:j * P + SCP], pS_l[0:SCP, c_:c_ + 8])
                last.then_inc(S("sc_tr"), 1)
                pe.wait_ge(S("sc_back"), r + 1)
                tr(ps[0:SCP, 3, 0:8], T[2][:, 0:SCP]).then_inc(S("sc_bk"), 1)
            for g, n in enumerate(rows_g):
                pe.wait_ge(S(f"ld_ex{g % 2}"), 16 * (g // 2 + 1))
                if g >= 2:
                    pe.wait_ge(S("ex_col"), g - 1)
                for c_ in range(n):
                    last = tr(ps[:, g % 2, c_ * P:(c_ + 1) * P], pA_row[g % 2][:, c_ * P:(c_ + 1) * P])
                last.then_inc(S("ex_tr"), 1)
            barrier(pe, 8)
            pe.sem_inc(S("slotB_free"), U)
            with pe.Fori(0, NW) as w:
                pe.wait_ge(S("accB"), w)
                mm(ps[:, 0, 0:P], pB_z, pB_z, start=True, stop=False, skip_group_check=True)
                mm(ps[:, 0, P:VW], pB_z, pB_z[:, 0:H2], start=False, stop=False, skip_group_check=True)
                b0 = pe.value_load(blk_i[0:1, ds(w, 1)], min_val=0, max_val=NB)
                b1 = pe.value_load(blk_i[0:1, ds(w + 1, 1)], min_val=1, max_val=NB)
                with pe.Fori(b0, b1) as b:
                    for k in range(U):
                        pe.wait_ge(S("v_used"), b * U + (2 * U + k + 1))
                        mm(ps[:, 0, 0:VW], pB_oh[k], pB_vx[k], start=False, stop=False, skip_group_check=True
                           ).then_inc(S("slotB_free"), 1)
                mm(ps[:, 0, 0:2], pB_z, pB_z[:, 0:2], start=False, stop=True, skip_group_check=True
                   ).then_inc(S("winB"), 1)
            barrier(pe, 9)
            for w in range(NW):
                pe.wait_ge(S("upd"), w + 1)
                if w >= 2:
                    pe.wait_ge(S("u_out"), w - 1)
                tr(ps[:, w % 2, 0:P], pB_acc[:, w * VW:w * VW + OK]).then_inc(S("u_tr"), 1)
                pe.wait_ge(S("u_out"), w + 1)
                if w >= 2:
                    pe.wait_ge(S("u_add"), w - 1)
                mm(ps[:, 2 + w % 2, 0:D], pB_uT[w % 2], wout[:, :]).then_inc(S("u_mm"), 1)
            for r in range(2):
                pe.wait_ge(S("bn_in"), r + 1)
                mm(ps[:, 4, 0:D], ones[:, :], pB_n[:, 0:D]).then_inc(S("bn_mm"), 1)
            barrier(pe, 10)
            tr(ps[0:D, 6, 0:D], w3[:, :]).then_inc(S("w3_tr"), 1)
            x_transposes(3)
            pe.wait_ge(S("w3_out"), 1)
            for w in range(NW):
                if w >= 2:
                    pe.wait_ge(S("h_add"), w - 1)
                mm(ps[:, 4 + w % 2, 0:D], xT[:, w * P:(w + 1) * P], w3T[:, :]).then_inc(S("h_mm"), 1)
            pe.wait_ge(S("g_ready"), 1)
            for w in range(NW):
                pe.wait_ge(S(f"ld_adjb{w % 2}"), 16 * (w // 2 + 1))
                for g in range(7):
                    cols = min(512, N - g * 512)
                    last = mm(ps[0:D, g, 0:cols], t1[:, w, :], pD_adj[w % 2][:, g * 512:g * 512 + cols],
                              start=(w == 0), stop=(w == NW - 1))
                last.then_inc(S("out_mm"), 1)
            pe.wait_ge(S("oT"), 1)
            pe.wait_ge(S("oT_zero"), 1)
            for w in range(NW):
                if w >= 4:
                    pe.wait_ge(S("o_out"), w - 3)
                tr(ps[:, w % 4, 0:D], pD_oT[:, w * P:(w + 1) * P]).then_inc(S("o_tr"), 1)


_ROWS = ("dst", "src", "edge_type_8", "edge_weight")


def kernel(**inputs):
    import concourse.bacc as _bacc
    from concourse.bass_utils import run_bass_kernel_spmd as _run

    nc = _bacc.Bacc("TRN2", target_bir_lowering=False, num_devices=1)
    arrays, args = {}, {}
    given = {}
    for name, a in inputs.items():
        a = np.ascontiguousarray(a)
        if name in _ROWS:
            fill = NP if name == "dst" else 0
            rows = np.concatenate([a, np.full((NTR * P - E,), fill, a.dtype)]).reshape(NTR, P)
            given[name] = rows
            if name in ("dst", "src"):
                given[name + "_cols"] = np.ascontiguousarray(rows[0:NT].T)
        elif name.startswith("edge_attr"):
            a = np.concatenate([a, np.zeros((NT * P - E, a.shape[1]), a.dtype)])
            if name == "edge_attr_64":
                a = a.reshape(NT // U, U * P, D).transpose(0, 2, 1)
            else:
                a = a.reshape(NT, P, S9).transpose(1, 0, 2)
            given[name] = np.ascontiguousarray(a)
        else:
            given[name] = a
    for name, a in given.items():
        arrays["in_" + name] = a
        args[name] = nc.dram_tensor("in_" + name, a.shape, mybir.dt.from_np(a.dtype), kind="ExternalInput").ap()
    out = nc.dram_tensor("out", (N, D), mybir.dt.float32, kind="ExternalOutput").ap()
    build(nc, args, out)
    return _run(nc, [arrays], core_ids=[0]).results[0]["out"]
```

```python
from contextlib import ExitStack

import numpy as np

import concourse.bass as bass
from concourse import mybir

RMAX = bass.bass_isa.ReduceOp.max
RADD = bass.bass_isa.ReduceOp.add
P = 128
N = 3125
E = 100000
D = 64
R = 8
H1 = 4
S9 = 9
S10 = S9 + 1
OK = 128
H2 = 8
NW = -(-N // P)
NP = NW * P
LAST = N - (NW - 1) * P
REAL_TILES = -(-E // P)
G = 8
NT = -(-REAL_TILES // G) * G
NTR = NT + 4
NIT = NT // G
U = 4
NB = (REAL_TILES + NW - 1 + NW * (U - 1)) // U
NS = NB * U
NBLK = -(-NS // P)
NSP = NBLK * P
CENTRE = N // 2
BIG = 1.0e38
REC = 80
SCP = NT // 7
SCL = NT // SCP * P
VW = OK + H2
XC = 5
_ROWS = ("dst", "src", "edge_type_8", "edge_weight")


def build(nc, A, out_dram):
    f32, i32, bf16, f16 = mybir.dt.float32, mybir.dt.int32, mybir.dt.bfloat16, mybir.dt.float16
    ALU = mybir.AluOpType
    ACT = mybir.ActivationFunctionType
    AX = mybir.AxisListType
    ds = bass.ds
    ctx = ExitStack()
    with ctx:
        def sb(name, shape, dt=f32):
            return ctx.enter_context(nc.sbuf_tensor(name, shape, dt))

        def sem(name):
            return ctx.enter_context(nc.semaphore(name))

        def dram(name, shape, dt=f32):
            return nc.dram_tensor(name, shape, dt, kind="Internal").ap()

        d_tile = dram("d_slot_tile", (NSP,), i32)
        d_xw = dram("d_xw", (NP * R, D))
        d_adj = dram("d_adj", (NW, P, N))
        d_x = dram("d_x", (NP, D))
        d_q = dram("d_q", (NP, OK))
        d_v = dram("d_v", (P, NTR, OK))
        d_lg = dram("d_logits", (NT, H2, P))
        d_ex = dram("d_exps", (NT, H2, P))

        o_rows = {n: dram("o_" + n, (NTR, P), f32 if n == "edge_weight" else i32) for n in _ROWS}
        o_cols = {n: dram("o_" + n + "_cols", (P, NT), i32) for n in ("dst", "src")}
        o_a64 = dram("o_edge_attr_64", (NT // U, D, U * P))
        o_a9 = dram("o_edge_attr_9", (P, NT, S10))
        d_rec = dram("d_records", (NT * P, REC))

        ident = sb("ident", [P, P])
        ones = sb("ones", [P, P])
        iota128 = sb("iota128", [P, P])
        pcol = sb("pcol", [P, 1])
        realrow = sb("realrow", [P, 1])
        rel_t = sb("rel_t", [P, NSP])
        srcc_t = sb("srcc_t", [P, NSP])
        w_t = sb("w_t", [P, NSP])
        src_t = sb("src_t", [P, NT], i32)
        xwi_t = sb("xwi_t", [P, NSP], i32)
        dst_t = sb("dst_t", [P, NT], i32)
        blk_i = sb("blk_i", [P, NW + 1], i32)
        tile_row = sb("tile_row", [1, NSP], i32)
        x = sb("x", [P, NW, D])
        agg = sb("agg", [P, NW, D])
        t1 = sb("t1", [P, NW, D])
        t2 = sb("t2", [P, NW, D])
        st = sb("st", [P, 8, NW])
        xT = sb("xT", [D, NP])
        dinv = sb("dinv", [P, NW])
        deg = sb("deg", [P, NW])
        small = sb("small", [P, 64])

        f32r = mybir.dt.float32r
        xh = [sb(f"xh{i}", [P, XC * P], f32r) for i in range(2)]
        xl = [sb(f"xl{i}", [P, XC * P], f32r) for i in range(2)]
        c_a = sb("c_a", [P, XC * 2 * OK], f32r)
        c_b = sb("c_b", [P, XC * 2 * OK], f32r)
        b2r = sb("b2r", [64, 2 * OK], f32r)
        ones_r = sb("ones_r", [64, P], f32r)
        r_area = sb("r_area", [P, U * 4 * D + U * P], f32r)
        p3_mm = [r_area[:, i * 4 * D:(i + 1) * 4 * D] for i in range(U)]
        p3_oh = [r_area[:, U * 4 * D + i * P:U * 4 * D + (i + 1) * P] for i in range(U)]
        att_r = [r_area[:, i * U * P:(i + 1) * U * P] for i in range(2)]
        w2h = r_area[:, 2 * U * P:2 * U * P + 2 * OK]
        w2l = r_area[:, 2 * U * P + 2 * OK:2 * U * P + 4 * OK]
        w1h = sb("w1h", [P, P], f32r)
        w1l = sb("w1l", [D, P], f32r)
        hid_h = [sb(f"hid_h{i}", [P, U * P], f32r) for i in range(2)]
        hid_l = [sb(f"hid_l{i}", [P, U * P], f32r) for i in range(2)]

        w0 = sb("w0", [D, R, D])
        w1 = sb("w1", [D, 2, H1, D])
        w2n = sb("w2n", [D, OK + D])
        wout = sb("wout", [P, D])
        w3 = sb("w3", [D, D])
        w3T = sb("w3T", [D, D])
        gam = sb("gam", [P, 3, D])

        ps = ctx.enter_context(nc.psum_tensor("ps", [P, 8, 512], f32))
        psf = ps[:, :, :].rearrange("p b c -> p (b c)")

        phase = sem("phase")
        order_known = sem("order_known")
        order_made = sem("order_made")
        lk = {e: sem(f"chain_{e}") for e in ("dve", "act", "pool")}
        lkn = {"dve": 0, "act": 0, "pool": 0}

        def link(eng, name, ins):
            lkn[name] += 1
            ins.then_inc(lk[name], 1)
            eng.wait_ge(lk[name], lkn[name])

        def barrier(eng, n, ended=phase):
            eng.drain().then_inc(ended, 1)
            eng.wait_ge(ended, 5 * n)

        sems = {}

        def S(name):
            if name not in sems:
                sems[name] = sem(name)
            return sems[name]

        tick = sem("tick")


        def hold(eng):
            eng.sem_inc(tick, 1)

        AREA = 24576
        area = sb("area", [P, AREA])

        XW_AT, SC_AT, Q_AT, U_AT, H_AT = (i * NW for i in range(5))

        LD_C = 2 * S10 + 11

        class Cut:
            def __init__(self):
                self.at = 0

            def take(self, cols, rows=P, dt=f32):
                words = cols if dt in (f32, i32) else -(-cols // 2)
                v = area[0:rows, self.at:self.at + words]
                self.at += -(-words // 8) * 8
                assert self.at <= AREA, self.at
                return v if dt == f32 else v.bitcast(dt)[:, 0:cols]

        unsorted = sb("unsorted", [P, 1], i32)
        tri = sb("tri", [P, P])

        c = Cut()
        p0_i = [c.take(NT, dt=i32) for _ in range(2)]
        p0_f = [c.take(NT) for _ in range(2)]
        p0_m = c.take(1)
        p0_mm = c.take(1)
        p0_col = {n: c.take(NT, dt=(f32 if n == "edge_weight" else i32)) for n in _ROWS}
        p0_cum = c.take(NT)
        p0_pos = c.take(NT)
        p0_posi = c.take(NT, dt=i32)
        p0_cur = c.take(1)
        p0_base = c.take(1)
        p0_s = c.take(1)
        p0_sh = c.take(NT * S10)
        p0_at = c.take(P, rows=D)
        p0_rec = c.take(REC)
        p0_idx = c.take(1, dt=i32)
        p0_r2 = c.take(REC)
        p0_r2T = c.take(P, rows=D)
        p0_pad = {n: c.take(P, rows=NTR - NT, dt=(f32 if n == "edge_weight" else i32)) for n in _ROWS}

        def is_unsorted(eng):
            return eng.value_load(unsorted[0:1, 0:1], min_val=0, max_val=1) == 1

        c = Cut()
        p1_dst_i = c.take(NT, dt=i32)
        p1_k = c.take(NBLK)
        p1_ki = c.take(NBLK, dt=i32)
        p1_dst = c.take(NT)
        p1_lt = c.take(NT)
        p1_cnt = c.take(32)
        p1_bi = c.take(32, dt=i32)
        p1_te = c.take(32)
        p1_ts = c.take(32)
        p1_nb = c.take(32)
        p1_nbi = c.take(32, dt=i32)
        p1_cum = c.take(32)
        p1_sb = c.take(32)
        p1_off = c.take(32)
        p1_doff = c.take(32)
        p1_i = c.take(NBLK)
        p1_mask = c.take(NBLK * 24)
        p1_mo = c.take(NBLK * 24)
        p1_w = c.take(NBLK)
        p1_o = c.take(NBLK)
        p1_t = c.take(NBLK)
        p1_ti = c.take(NBLK, dt=i32)
        p1_g = {n: c.take(NSP, dt=(f32 if n == "wgt" else i32)) for n in ("dst", "src", "typ", "wgt")}
        p1_f = c.take(NSP)
        p1_a = c.take(NSP)
        p1_b = c.take(NSP)
        p1_rel = c.take(NSP)
        p1_s = c.take(NSP)
        p1_x = c.take(NSP)

        c = Cut()
        c.at = 20000
        p2_o = [c.take(R * D) for _ in range(2)]

        c = Cut()
        p3_idx = [c.take(U, dt=i32) for _ in range(2)]
        p3_msg = [c.take(D) for _ in range(2 * U)]
        p3_iota = c.take(N, dt=f16)
        p3_ohs = [c.take(N, dt=bf16) for _ in range(U)]
        p3_ohd = [c.take(P, dt=bf16) for _ in range(U)]
        p3_sum = c.take(NW * 2 * D)
        p3_z = c.take(512, dt=bf16)
        p3_ev = c.take(N)

        c = Cut()
        p5_hw = c.take(NW * H1 * D)
        p5_pr = [c.take(H1 * D) for _ in range(2)]
        p5_s = c.take(NW * H1)
        p5_e = c.take(NW * H1)
        p5_m = c.take(H1)
        p5_mm = c.take(H1)
        p5_z = c.take(H1)
        p5_zz = c.take(H1)
        p5_ri = c.take(H1)
        p5_zt = c.take(NW * D)
        p5_adj = [c.take(NP) for _ in range(2)]
        p5_at = c.take(NP)

        c = Cut()
        p8_qo = [c.take(OK + D) for _ in range(2)]
        self_o = t2
        p8_w1 = c.take(P)
        p8_b1 = c.take(1)
        p8_w2 = c.take(2 * OK)
        p8_b2 = c.take(2 * OK, rows=64)
        p8_xidx = [c.take(U, dt=i32) for _ in range(2)]
        p8_qidx = [c.take(U, dt=i32) for _ in range(2)]
        p8_att = [c.take(U * P) for _ in range(2)]
        p8_sh = c.take(NT * S10)
        p8_xg = [c.take(D) for _ in range(G)]
        p8_q = c.take(G * OK)
        p8_qg = [p8_q[:, j * OK:(j + 1) * OK] for j in range(G)]
        p8_xs = [c.take(XC * P) for _ in range(4)]
        p8_hid = [c.take(U * P) for _ in range(2)]
        p8_wk = [c.take(2 * OK) for _ in range(2)]
        lg = area[:, c.at:c.at + NT * H2]
        p8_c = c.take(XC * 2 * OK)
        c.at += NT * H2 - XC * 2 * OK
        p8_kv = c.take(G * 2 * OK)
        p8_pr = c.take(U * OK)
        NG = NT * H2 // P
        pA_row = [sb(f"scan_row{i}", [P, 512]) for i in range(2)]
        c = Cut()
        pS_a = c.take(H2 * SCL)
        pS_f = c.take(H2 * SCL)
        pS_dv = c.take(SCL)
        pS_di = c.take(SCL, dt=i32)
        pS_pm = c.take(SCL)
        pS_new = c.take(SCL)
        pS_v1 = c.take(SCL)
        pS_l = c.take(64)
        pS_tr = c.take(8 * P, rows=8)

        c = Cut()
        pB_ex = c.take(NTR * H2)
        pB_v = [c.take(U * OK) for _ in range(2)]
        pB_vx = c.take(U * VW).rearrange("p (k c) -> p k c", c=VW)
        pB_oh = c.take(U * P).rearrange("p (k c) -> p k c", c=P)
        pB_z = c.take(P)
        pB_acc = c.take(NW * VW)
        pB_r = c.take(NW * H2)
        pB_uT = [c.take(P) for _ in range(2)]
        pB_n = c.take(D * 4)

        c = Cut()
        pD_adj = [c.take(N) for _ in range(2)]
        pD_oT = c.take(NP, rows=D)

        block = ctx.enter_context(nc.Block())

        @block.sync
        def _(sp):
            flat = A["dst"].rearrange("t e -> (t e)")
            for j in range(2):
                sp.dma_start(p0_i[j], flat[j:j + NT * P].rearrange("(p c) -> p c", p=P)).then_inc(S("ld_order"), 16)
            barrier(sp, 1, order_known)
            with sp.If(is_unsorted(sp)):
                for n in _ROWS:
                    sp.dma_start(p0_col[n], A[n + "_cols"]).then_inc(S("so_ld"), 16)
                    sp.dma_start(p0_pad[n], A[n][NT:NTR, :]).then_inc(S("so_ld"), 16)
                sp.dma_start(p0_sh, A["edge_attr_9"].rearrange("p t s -> p (t s)")).then_inc(S("so_ld"), 16)
                sp.wait_ge(S("so_ld"), 16 * 9)
                for n in _ROWS:
                    sp.dma_start(o_rows[n][NT:NTR, :], p0_pad[n]).then_inc(S("so_st"), 16)
                sp.wait_ge(S("so_st"), 16 * 4)
                with sp.Fori(0, NT // U) as b:
                    for k in range(U):
                        sp.wait_ge(S("so_pe"), b * U + (k + NP + 1))
                        sp.dma_start(p0_at, A["edge_attr_64"][ds(b, 1), :, k * P:(k + 1) * P]
                                     .rearrange("o d e -> (o d) e")).then_inc(S("so_ld"), 16)
                sp.wait_ge(S("so_sc"), 16 * NT)
                with sp.Fori(0, NT // U) as b:
                    for k in range(U):
                        i = b * U + k
                        sp.dma_start(p0_r2, d_rec[ds(i * P, P), :]).then_inc(S("so_ld2"), 16)
                        sp.wait_ge(S("so_rec"), i + 2)
                        r2i = p0_r2.bitcast(i32)
                        sp.dma_start(o_a64[ds(b, 1), :, k * P:(k + 1) * P].rearrange("o d e -> (o d) e"), p0_r2T
                                     ).then_inc(S("so_st"), 16)
                        sp.dma_start(o_a9[:, ds(i, 1), :].rearrange("p o s -> p (o s)"), p0_r2[:, D:D + S10]
                                     ).then_inc(S("so_st"), 16)
                        with nc.allow_non_contiguous_dma(reason="single words, only where the edges come unsorted"):
                            for j, n in enumerate(_ROWS):
                                v = (p0_r2 if n == "edge_weight" else r2i)[:, D + S10 + j:D + S10 + j + 1]
                                sp.dma_start(o_rows[n][ds(i, 1), :].rearrange("o e -> e o"), v
                                             ).then_inc(S("so_st"), 16)
                                if n in o_cols:
                                    sp.dma_start(o_cols[n][:, ds(i, 1)], v).then_inc(S("so_st"), 16)
                        sp.wait_ge(S("so_st"), i * 128 + (16 * 4 + 128))
                        hold(sp)
                barrier(sp, 1, order_made)
            hold(sp)
            with sp.If(is_unsorted(sp)):
                sp.dma_start(p1_dst_i, o_cols["dst"]).then_inc(S("ld_dst"), 16)
                sp.dma_start(src_t[:, :], o_cols["src"]).then_inc(S("ld_w"), 16)
            with sp.Else():
                sp.dma_start(p1_dst_i, A["dst_cols"]).then_inc(S("ld_dst"), 16)
                sp.dma_start(src_t[:, :], A["src_cols"]).then_inc(S("ld_w"), 16)
            hold(sp)
            sp.wait_ge(S("x_zero"), 1)
            sp.dma_start(x[:, 0:NW - 1, :], A["x"][0:(NW - 1) * P, :].rearrange("(w p) d -> p w d", p=P)
                         ).then_inc(S("ld_x"), 16)
            sp.dma_start(x[0:LAST, NW - 1, :], A["x"][(NW - 1) * P:N, :]).then_inc(S("ld_x"), 16)
            sp.dma_start(w0[:, :, :], A["L0_gnn_W"].rearrange("r f o -> f r o")).then_inc(S("ld_w"), 16)
            sp.dma_start(w1[:, 0, :, :], A["L1_gnn_Wh"].rearrange("h d e -> d h e")).then_inc(S("ld_w"), 16)
            sp.dma_start(w1[:, 1, :, :], A["L1_gnn_weight"].rearrange("(h d) e -> d h e", h=H1)
                         ).then_inc(S("ld_w"), 16)
            sp.dma_start(w2n[:, 0:OK], A["L2_gnn_Wq"]).then_inc(S("ld_w"), 16)
            sp.dma_start(w2n[:, OK:OK + D], A["L2_gnn_W_self"]).then_inc(S("ld_w"), 16)
            sp.dma_start(wout[:, :], A["L2_gnn_W_out"]).then_inc(S("ld_w"), 16)
            sp.dma_start(w3[:, :], A["L3_gnn_W"]).then_inc(S("ld_w"), 16)
            for j, n in enumerate(("L2_gnn_gamma", "L2_gnn_beta", "L3_gnn_b")):
                sp.dma_start(gam[:, j, :], A[n].partition_broadcast(P)).then_inc(S("ld_w"), 16)
            sp.wait_ge(S("tiles_known"), 1)
            sp.dma_start(d_tile.rearrange("(b p) -> p b", p=P), p1_ti, allow_slow_non_contiguous=True).then_inc(S("st_tile"), 16)
            sp.wait_ge(S("st_tile"), 16)
            sp.dma_start(tile_row[0:1, :], d_tile.rearrange("(o n) -> o n", o=1)).then_inc(S("st_tile"), 16)
            sp.wait_ge(S("st_tile"), 32)
            sp.wait_ge(S("ld_w"), 176)
            barrier(sp, 1)
            xw_v = d_xw.rearrange("(w p r) o -> w p (r o)", p=P, r=R)
            for w in range(NW):
                sp.wait_ge(S("xw_out"), w + 1)
                sp.dma_start(xw_v[w], p2_o[w % 2]).then_inc(S(f"st_xw{w % 2}"), 16)
            sp.wait_ge(S("st_xw0"), 16 * 13)
            sp.wait_ge(S("st_xw1"), 16 * 12)
            barrier(sp, 2)
            with sp.Fori(0, NW) as w:
                sp.wait_ge(S("adj_out"), w * 3 + 5)
                sp.dma_start(d_adj[ds(w, 1), :, :].rearrange("o p c -> (o p) c"), p3_ev).then_inc(S("st_adj"), 16)
            sp.wait_ge(S("st_adj"), 16 * NW + 1)
            barrier(sp, 3)
            barrier(sp, 4)
            sp.wait_ge(S("adj_zero"), 1)
            for w in range(NW):
                if w >= 2:
                    sp.wait_ge(S("at_tr"), 7 * (w - 1))
                sp.dma_start(p5_adj[w % 2][:, 0:N], d_adj[w]).then_inc(S(f"ld_adj{w % 2}"), 16)
            barrier(sp, 5)
            sp.dma_start(d_x.rearrange("(w p) d -> p w d", p=P), x[:, :, :]).then_inc(S("st_x"), 16)
            q_v = d_q.rearrange("(w p) o -> w p o", p=P)
            for w in range(NW):
                sp.wait_ge(S("q_out"), w + 1)
                sp.dma_start(q_v[w], p8_qo[w % 2][:, 0:OK]).then_inc(S(f"st_xw{w % 2}"), 16)
            sp.wait_ge(S("st_x"), 16)
            sp.wait_ge(S("st_xw0"), 16 * 26)
            sp.wait_ge(S("st_xw1"), 16 * 24)
            for j, n in enumerate(("L2_gnn_Cqk", "L2_gnn_Cv")):
                for s in range(S9):
                    half = 64 * (s % 2)
                    at = (s // 2) * 2 * OK + j * OK
                    sp.dma_start(p8_c[half:half + D, at:at + OK], A[n][:, s, :]).then_inc(S("ld_c"), 16)
                sp.dma_start(p8_c[D:P, at:at + OK], A[n][:, S9 - 1, :]).then_inc(S("ld_c"), 16)
            sp.wait_ge(S("w2_zero"), 1)
            for j, n in enumerate(("k", "v")):
                for r in range(2):
                    sp.dma_start(p8_w1[r * D:(r + 1) * D, j * D:(j + 1) * D], A[f"L2_gnn_{n}_w1"]
                                 ).then_inc(S("ld_c"), 16)
                sp.dma_start(p8_b1[j * D:(j + 1) * D, :], A[f"L2_gnn_{n}_b1"].rearrange("(d o) -> d o", o=1)
                             ).then_inc(S("ld_c"), 16)
                sp.dma_start(p8_w2[j * D:(j + 1) * D, j * OK:(j + 1) * OK], A[f"L2_gnn_{n}_w2"]
                             ).then_inc(S("ld_c"), 16)
                sp.dma_start(p8_b2[:, j * OK:(j + 1) * OK], A[f"L2_gnn_{n}_b2"].partition_broadcast(64)
                             ).then_inc(S("ld_c"), 16)
            shuffled = is_unsorted(sp)
            with sp.If(shuffled):
                sp.dma_start(p8_sh, o_a9.rearrange("p t s -> p (t s)")).then_inc(S("ld_c"), 16)
            with sp.Else():
                sp.dma_start(p8_sh, A["edge_attr_9"].rearrange("p t s -> p (t s)")).then_inc(S("ld_c"), 16)
            sp.wait_ge(S("ld_c"), 16 * LD_C)
            barrier(sp, 6)
            def att_load(h, block):
                def both(table):
                    for r in range(2):
                        sp.dma_start(p8_att[h][r * D:(r + 1) * D, :],
                                     table[ds(block, 1), :, :].rearrange("o d e -> (o d) e")
                                     ).then_inc(S(f"ld_at{h}"), 16)
                with sp.If(shuffled):
                    both(o_a64)
                with sp.Else():
                    both(A["edge_attr_64"])

            def v_store(h, t, kvs):
                sp.wait_ge(S("kv_made"), kvs)
                sp.dma_start(d_v[:, t, :],
                             p8_kv3[:, h * U:(h + 1) * U, OK:2 * OK]).then_inc(S(f"st_v{h}"), 16)

            p8_kv3 = p8_kv.rearrange("p (j c) -> p j c", c=2 * OK)
            att_load(0, 0)
            att_load(1, 1)
            with sp.Fori(1, NIT) as it:
                for h in range(2):
                    sp.wait_ge(S("hid_mm"), it * 2 + h)
                    hold(sp)
                    att_load(h, it * 2 + h)
                    v_store(h, ds(it * G + (h * U - G), U), it * G + (h * U - G + U + 2))
            for h in range(2):
                v_store(h, slice(NT - G + h * U, NT - G + (h + 1) * U), NT - G + (h + 1) * U + 2)
            for h in range(2):
                sp.wait_ge(S(f"st_v{h}"), 16 * NIT)
            barrier(sp, 7)
            lg_v = d_lg.rearrange("s h e -> (s h) e")
            ex_v = d_ex.rearrange("s h e -> (s h) e")
            rows_g = [min(4, NG - 4 * g) for g in range(-(-NG // 4))]
            for g, n in enumerate(rows_g):
                sp.wait_ge(S("lg_row"), g + 1)
                sp.dma_start(lg_v[g * 4 * P:(g * 4 + n) * P, :].rearrange("(n p) e -> p n e", p=P),
                             pA_row[g % 2][:, 0:n * P].rearrange("p (n e) -> p n e", e=P)
                             ).then_inc(S(f"st_lg{g % 2}"), 16)
            for j in range(2):
                sp.wait_ge(S(f"st_lg{j}"), 16 * len(rows_g[j::2]))
            sp.wait_ge(S("lg_gone"), 1)
            lgs = d_lg.rearrange("(p s) h e -> p h s e", p=SCP)
            for h in range(H2):
                sp.dma_start(pS_a[0:SCP, h * SCL:(h + 1) * SCL].rearrange("p (s e) -> p s e", e=P), lgs[:, h, :, :]
                             ).then_inc(S("ld_scan"), 16)
            with sp.If(is_unsorted(sp)):
                sp.dma_start(pS_di[0:SCP, :], o_rows["dst"][0:NT, :].rearrange("(p s) e -> p (s e)", p=SCP)
                             ).then_inc(S("ld_scan"), 16)
            with sp.Else():
                sp.dma_start(pS_di[0:SCP, :], A["dst"][0:NT, :].rearrange("(p s) e -> p (s e)", p=SCP)
                             ).then_inc(S("ld_scan"), 16)
            exs = d_ex.rearrange("(p s) h e -> p h s e", p=SCP)
            sp.wait_ge(S("ex_done"), 1)
            for h in range(H2):
                sp.dma_start(exs[:, h, :, :], pS_a[0:SCP, h * SCL:(h + 1) * SCL].rearrange("p (s e) -> p s e", e=P)
                             ).then_inc(S("st_ex"), 16)
            sp.wait_ge(S("st_ex"), 16 * H2)
            for g, n in enumerate(rows_g):
                if g >= 2:
                    sp.wait_ge(S("ex_tr"), g - 1)
                sp.dma_start(pA_row[g % 2][:, 0:n * P].rearrange("p (n e) -> p n e", e=P),
                             ex_v[g * 4 * P:(g * 4 + n) * P, :].rearrange("(n p) e -> p n e", p=P)
                             ).then_inc(S(f"ld_ex{g % 2}"), 16)
            sp.wait_ge(S("v_zero"), 1)
            sp.dma_start(d_v[:, NT:NTR, :], pB_v[0].rearrange("p (t c) -> p t c", c=OK)).then_inc(S("st_v0"), 16)
            sp.wait_ge(S("st_v0"), 16 * (NIT + 1))
            barrier(sp, 8)
            with sp.Fori(0, NB // 2) as b2:
                for j in range(2):
                    t = sp.value_load(tile_row[0:1, ds(b2 * (2 * U) + j * U, 1)], min_val=0, max_val=NT)
                    sp.wait_ge(S("v_used"), b2 * U + (2 * j + 2))
                    sp.dma_start(pB_v[j], d_v[:, ds(t, U), :].rearrange("p t c -> p (t c)")).then_inc(S(f"ld_v{j}"), 16)
            barrier(sp, 9)
            barrier(sp, 10)
            for w in range(NW):
                if w >= 2:
                    sp.wait_ge(S("out_mm"), w - 1)
                sp.dma_start(pD_adj[w % 2], d_adj[w]).then_inc(S(f"ld_adj{w % 2}"), 16)
            sp.wait_ge(S("final"), 1)
            sp.dma_start(out_dram[0:(NW - 1) * P, :].rearrange("(w p) d -> p w d", p=P), x[:, 0:NW - 1, :]
                         ).then_inc(S("st_out"), 16)
            sp.dma_start(out_dram[(NW - 1) * P:N, :], x[0:LAST, NW - 1, :]).then_inc(S("st_out"), 16)
            sp.wait_ge(S("st_out"), 32)

        @block.gpsimd
        def _(pool):
            nc.gpsimd.memset(x[:, :, :], 0.0).then_inc(S("x_zero"), 1)
            nc.gpsimd.iota(iota128[:, :], [[1, P]], base=0, channel_multiplier=0,
                           allow_small_or_imprecise_dtypes=True)
            nc.gpsimd.iota(pcol[:, :], [[0, 1]], base=0, channel_multiplier=1, allow_small_or_imprecise_dtypes=True)
            nc.gpsimd.memset(ones[:, :], 1.0)
            link(pool, "pool", nc.gpsimd.memset(ident[:, :], 0.0))
            nc.gpsimd.affine_select(out=ident[:, :], in_=ident[:, :], compare_op=ALU.not_equal, fill=1.0, base=0,
                                    pattern=[[-1, P]], channel_multiplier=1).then_inc(S("consts"), 1)
            nc.gpsimd.affine_select(out=tri[:, :], in_=ones[:, :], compare_op=ALU.is_gt, fill=0.0, base=0,
                                    pattern=[[1, P]], channel_multiplier=-1).then_inc(S("consts0"), 1)
            pool.wait_ge(S("order_bad"), 1)
            nc.gpsimd.partition_all_reduce(p0_mm, p0_m, P, RMAX).then_inc(S("order_bad"), 1)
            barrier(pool, 1, order_known)
            with pool.If(is_unsorted(pool)):
                pool.wait_ge(S("so_posi"), 1)
                with pool.Fori(0, NT) as t:
                    pool.wait_ge(S("so_made"), t + 2)
                    hold(pool)
                    nc.gpsimd.tensor_copy(p0_idx, p0_posi[:, ds(t, 1)]).then_inc(S("so_idx"), 1)
                    pool.wait_ge(S("so_idx"), t + 1)
                    hold(pool)
                    pool.indirect_dma_start(out=d_rec, out_offset=bass.IndirectOffsetOnAxis(ap=p0_idx, axis=0),
                                            in_=p0_rec, in_offset=None).then_inc(S("so_sc"), 16)
                barrier(pool, 1, order_made)
            nc.gpsimd.iota(p1_i, [[P, NBLK]], base=0, channel_multiplier=1, allow_small_or_imprecise_dtypes=True)
            nc.gpsimd.iota(p1_k, [[0, NBLK]], base=0, channel_multiplier=1, allow_small_or_imprecise_dtypes=True
                           ).then_inc(S("consts1"), 1)
            pool.wait_ge(S("tiles_known"), 1)
            def row_gathers(table):
                for name, arr in (("dst", "dst"), ("src", "src"), ("typ", "edge_type_8"), ("wgt", "edge_weight")):
                    for j in range(NBLK):
                        pool.indirect_dma_start(out=p1_g[name][:, j * P:(j + 1) * P], out_offset=None, in_=table[arr],
                                                in_offset=bass.IndirectOffsetOnAxis(ap=p1_ti[:, j:j + 1], axis=0)
                                                ).then_inc(S(f"g_{name}"), 16)

            with pool.If(is_unsorted(pool)):
                row_gathers(o_rows)
            with pool.Else():
                row_gathers(A)
            pool.wait_ge(S("g_wgt"), 16 * NBLK)
            barrier(pool, 1)
            nc.gpsimd.iota(p3_iota, [[1, N]], base=-CENTRE, channel_multiplier=0,
                           allow_small_or_imprecise_dtypes=True)
            barrier(pool, 2)
            with pool.Fori(0, NB // 2) as b2:
                for j in range(2):
                    pool.wait_ge(S("oh3"), b2 * (2 * U) + (j + 1) * U)
                    hold(pool)
                    nc.gpsimd.tensor_copy(p3_idx[j], xwi_t[:, ds(b2 * (2 * U) + j * U, U)]).then_inc(S("idx3"), 1)
                    pool.wait_ge(S("idx3"), b2 * 2 + j + 1)
                    hold(pool)
                    for k in range(U):
                        pool.wait_ge(S("oh3"), b2 * (2 * U) + (j * U + k + 1))
                        hold(pool)
                        pool.indirect_dma_start(out=p3_msg[j * U + k], out_offset=None, in_=d_xw,
                                                in_offset=bass.IndirectOffsetOnAxis(ap=p3_idx[j][:, k:k + 1], axis=0)
                                                ).then_inc(S(f"g_x{j * U + k}"), 16)
            barrier(pool, 3)
            pool.wait_ge(S("sc_max"), 1)
            nc.gpsimd.partition_all_reduce(p5_mm, p5_m, P, RMAX).then_inc(S("sc_gmax"), 1)
            pool.wait_ge(S("sc_sum"), 1)
            nc.gpsimd.partition_all_reduce(p5_zz, p5_z, P, RADD).then_inc(S("sc_gsum"), 1)
            barrier(pool, 4)
            barrier(pool, 5)
            barrier(pool, 6)
            with pool.Fori(0, NIT) as it:
                for h in range(2):
                    pool.wait_ge(S("xs_made"), it * G + (h + 1) * U)
                    hold(pool)
                    nc.gpsimd.tensor_copy(p8_xidx[h], src_t[:, ds(it * G + h * U, U)]).then_inc(S("idx8"), 1)
                    pool.wait_ge(S("idx8"), it * 4 + (h * 2 + 1))
                    hold(pool)
                    for j in range(h * U, (h + 1) * U):
                        pool.indirect_dma_start(out=p8_xg[j], out_offset=None, in_=d_x,
                                                in_offset=bass.IndirectOffsetOnAxis(
                                                    ap=p8_xidx[h][:, j % U:j % U + 1], axis=0)
                                                ).then_inc(S(f"g_x{j}"), 16)
                    pool.wait_ge(S("q_used"), it * G + (h + 1) * U)
                    hold(pool)
                    nc.gpsimd.tensor_copy(p8_qidx[h], dst_t[:, ds(it * G + h * U, U)]).then_inc(S("idx8"), 1)
                    pool.wait_ge(S("idx8"), it * 4 + (h * 2 + 2))
                    hold(pool)
                    for j in range(h * U, (h + 1) * U):
                        pool.indirect_dma_start(out=p8_qg[j], out_offset=None, in_=d_q,
                                                in_offset=bass.IndirectOffsetOnAxis(
                                                    ap=p8_qidx[h][:, j % U:j % U + 1], axis=0)
                                                ).then_inc(S(f"g_q{j}"), 16)
            for n in range(7, 11):
                barrier(pool, n)

        @block.scalar
        def _(act):
            barrier(act, 1, order_known)
            with act.If(is_unsorted(act)):
                barrier(act, 1, order_made)
            hold(act)
            barrier(act, 1)
            for w in range(NW):
                act.wait_ge(S("node_mm"), XW_AT + w + 1)
                if w >= 2:
                    act.wait_ge(S(f"st_xw{w % 2}"), 16 * (w // 2))
                nc.scalar.activation(p2_o[w % 2], ps[:, 4 + w % 2, :], ACT.Copy).then_inc(S("xw_out"), 1)
            barrier(act, 2)
            act.sem_inc(S("adj_out"), 3)
            act.sem_inc(S("st_adj"), 1)
            with act.Fori(0, NW) as w:
                b0 = act.value_load(blk_i[0:1, ds(w, 1)], min_val=0, max_val=NB)
                b1 = act.value_load(blk_i[0:1, ds(w + 1, 1)], min_val=1, max_val=NB)
                with act.Fori(b0, b1) as b:
                    for k in range(U):
                        act.wait_ge(S("ohs3"), b * U + (k + 1))
                        hold(act)
                        nc.scalar.activation(p3_oh[k], p3_ohd[k], ACT.Copy).then_inc(S("ohr3"), 1)
                act.wait_ge(S("win3"), w + 1)
                act.wait_ge(S("st_adj"), w * 16 + 1)
                hold(act)
                nc.scalar.activation(p3_ev[:, 0:2048], psf[:, 0:2048], ACT.Copy).then_inc(S("adj_out"), 1)
                nc.scalar.activation(p3_ev[:, 2048:N], psf[:, 2048:N], ACT.Copy).then_inc(S("adj_out"), 1)
                nc.scalar.activation(p3_sum[:, ds(w * 2 * D, 2 * D)], ps[:, 7, 0:2 * D], ACT.Copy
                                     ).then_inc(S("adj_out"), 1)
            barrier(act, 3)
            act.wait_ge(S("ln_var"), 1)
            nc.scalar.activation(st[:, 4, :], st[:, 3, :], ACT.Sqrt).then_inc(S("ln_sd"), 1)
            for w in range(NW):
                act.wait_ge(S("node_mm"), SC_AT + w + 1)
                nc.scalar.activation(p5_hw[:, w * 256:(w + 1) * 256], ps[:, 6 + w % 2, 0:256], ACT.Copy
                                     ).then_inc(S("hw_out"), 1)
            act.wait_ge(S("sc_sub"), 1)
            nc.scalar.activation(p5_e, p5_e, ACT.Exp).then_inc(S("sc_exp"), 1)
            barrier(act, 4)
            for w in range(NW):
                for g in range(7):
                    cols = min(512, NP - g * 512)
                    act.wait_ge(S("at_tr"), 7 * w + g + 1)
                    if w >= 1:
                        act.wait_ge(S("z_mm"), 7 * (w - 1) + g + 1)
                        act.wait_ge(S("deg_red"), 7 * (w - 1) + g + 1)
                    nc.scalar.activation(p5_at[:, g * 512:g * 512 + cols], ps[:, (7 * w + g) % 4, 0:cols], ACT.Copy
                                         ).then_inc(S("at_out"), 1)
            act.wait_ge(S("elu_min"), 1)
            nc.scalar.activation(t1[:, :, :], t1[:, :, :], ACT.Exp).then_inc(S("elu_exp"), 1)
            act.wait_ge(S("ln_var"), 2)
            nc.scalar.activation(st[:, 4, :], st[:, 3, :], ACT.Sqrt).then_inc(S("ln_sd"), 1)
            barrier(act, 5)
            for w in range(NW):
                act.wait_ge(S("node_mm"), Q_AT + w + 1)
                if w >= 2:
                    act.wait_ge(S(f"st_xw{w % 2}"), 16 * (w // 2 + 13 - w % 2))
                nc.scalar.activation(p8_qo[w % 2][:, 0:OK], ps[:, 4 + w % 2, 0:OK], ACT.Copy).then_inc(S("q_out"), 1)
                nc.scalar.activation(self_o[:, w, :], ps[:, 4 + w % 2, OK:OK + D], ACT.Copy
                                     ).then_inc(S("self_out"), 1)
            barrier(act, 6)
            act.sem_inc(S("hid_out"), 1)
            act.sem_inc(S("w_out"), 1)

            def xs_out(j, i):
                act.wait_ge(S("xs_tr"), i + 5)
                act.wait_ge(S("tp_mm"), i + 1)
                nc.scalar.activation(xh[j % 2][:, :], psf[:, (j % 2) * 1024:(j % 2) * 1024 + XC * P], ACT.Copy
                                     ).then_inc(S("xt_out"), 1)

            def w_out(j, i):
                act.wait_ge(S("w_mm"), i + 1)
                act.wait_ge(S("kv_made"), i + 1)
                nc.scalar.activation(p8_wk[j % 2], ps[:, 4, 0:2 * OK], ACT.Copy).then_inc(S("w_out"), 1)

            def att_high(h, n, turn):
                act.wait_ge(S(f"ld_at{h}"), turn * 32 + 32)
                act.wait_ge(S("hid_mm"), n)
                nc.scalar.activation(att_r[h], p8_att[h], ACT.Copy).then_inc(S("att_high"), 1)

            def hid_out(h, n):
                act.wait_ge(S("hid_mm"), n + 2)
                nc.scalar.activation(p8_hid[h], ps[:, 5, :], ACT.Relu, bias=p8_b1)
                nc.scalar.activation(hid_h[h][:, :], ps[:, 5, :], ACT.Relu, bias=p8_b1).then_inc(S("hid_out"), 1)

            def act_tiles(it, last):
                for j in range(G):
                    if not (last and j == G - 1):
                        xs_out(j + 1, it * G + (j + 1))
                    if j == 0:
                        att_high(1, it * 2 + 1, it)
                    if j == 2:
                        act.wait_ge(S("w_mm"), it * G + 1)
                        hid_out(1, it * 2 + 1)
                    if j == 4 and not last:
                        att_high(0, it * 2 + 2, it + 1)
                    if j == 6 and not last:
                        act.wait_ge(S("w_mm"), it * G + U)
                        hid_out(0, it * 2 + 2)
                    w_out(j, it * G + j)

            xs_out(0, 0)
            act.wait_ge(S("ld_at0"), 32)
            nc.scalar.activation(att_r[0], p8_att[0], ACT.Copy).then_inc(S("att_high"), 1)
            hid_out(0, 0)
            with act.Fori(0, NIT - 1) as it:
                act_tiles(it, False)
            act_tiles(NIT - 1, True)
            barrier(act, 7)
            act.wait_ge(S("ex_sub"), 1)
            nc.scalar.activation(pS_a[0:SCP, :], pS_a[0:SCP, :], ACT.Exp).then_inc(S("ex_done"), 1)
            barrier(act, 8)
            act.sem_inc(S("accB"), 1)
            with act.Fori(0, NW) as w:
                act.wait_ge(S("winB"), w + 1)
                hold(act)
                nc.scalar.activation(pB_acc[:, ds(w * VW, VW)], ps[:, 0, 0:VW], ACT.Copy).then_inc(S("accB"), 1)
            barrier(act, 9)
            act.wait_ge(S("bn_var"), 1)
            nc.scalar.activation(pB_n[:, 0:D], pB_n[:, 0:D], ACT.Sqrt).then_inc(S("bn_sd"), 1)
            act.wait_ge(S("ln_var"), 3)
            nc.scalar.activation(st[:, 4, :], st[:, 3, :], ACT.Sqrt).then_inc(S("ln_sd"), 1)
            nc.scalar.activation(dinv[:, :], deg[:, :], ACT.Sqrt).then_inc(S("deg_sd"), 1)
            barrier(act, 10)
            act.wait_ge(S("out_mm"), NW)
            nc.scalar.activation(pD_oT[:, 0:N], psf[0:D, 0:N], ACT.Copy).then_inc(S("oT"), 1)
            act.wait_ge(S("ln_var"), 4)
            nc.scalar.activation(st[:, 4, :], st[:, 3, :], ACT.Sqrt).then_inc(S("ln_sd"), 1)

        @block.vector
        def _(dve):
            V = nc.vector

            def L(ins):
                link(dve, "dve", ins)

            def bw(a, n=D):
                return a.unsqueeze(2).to_broadcast([P, NW, n])

            def layer_norm(j):
                L(V.tensor_reduce(out=st[:, 0, :], in_=t1[:, :, :], axis=AX.X, op=ALU.add))
                L(V.tensor_scalar(st[:, 1, :], st[:, 0, :], 1.0 / D, None, ALU.mult))
                L(V.tensor_tensor(t1[:, :, :], t1[:, :, :], bw(st[:, 1, :]), ALU.subtract))
                L(V.tensor_tensor(agg[:, :, :], t1[:, :, :], t1[:, :, :], ALU.mult))
                L(V.tensor_reduce(out=st[:, 2, :], in_=agg[:, :, :], axis=AX.X, op=ALU.add))
                V.tensor_scalar(st[:, 3, :], st[:, 2, :], 1.0 / D, 1e-5, ALU.mult, ALU.add).then_inc(S("ln_var"), 1)
                dve.wait_ge(S("ln_sd"), j + 1)
                L(V.reciprocal(st[:, 5, :], st[:, 4, :]))
                L(V.tensor_tensor(x[:, :, :], t1[:, :, :], bw(st[:, 5, :]), ALU.mult))

            def x_transposes(tag):
                for w in range(NW):
                    dve.wait_ge(S("xT_tr"), tag * NW + w + 1)
                    V.tensor_copy(xT[:, w * P:(w + 1) * P], ps[0:D, w % 4, 0:P]).then_inc(S("xT_out"), 1)

            dve.wait_ge(S("ld_order"), 32)
            V.tensor_copy(p0_f[0], p0_i[0])
            L(V.tensor_copy(p0_f[1], p0_i[1]))
            L(V.tensor_tensor(p0_f[0], p0_f[0], p0_f[1], ALU.is_gt))
            V.tensor_reduce(out=p0_m, in_=p0_f[0], axis=AX.X, op=ALU.max).then_inc(S("order_bad"), 1)
            dve.wait_ge(S("order_bad"), 2)
            V.tensor_copy(unsorted[:, :], p0_mm)
            barrier(dve, 1, order_known)
            with dve.If(is_unsorted(dve)):
                dve.wait_ge(S("so_ld"), 16 * 9)
                dst_f, mask = p0_f
                V.memset(p0_rec, 0.0)
                V.memset(p0_pos, -1.0)
                V.memset(p0_cur, 0.0)
                V.memset(p0_base, 0.0)
                V.tensor_copy(dst_f, p0_col["dst"]).then_inc(S("so_dve"), 1)
                dve.wait_ge(S("so_dve"), 1)
                with dve.Fori(0, NP + 1) as n:
                    def step(ins, j):
                        ins.then_inc(S("so_dve"), 1)
                        dve.wait_ge(S("so_dve"), n * 7 + (j + 2))

                    step(V.tensor_scalar(mask, dst_f, p0_cur, None, ALU.is_equal), 0)
                    step(V.tensor_tensor_scan(p0_cum, mask, mask, 0.0, ALU.add, ALU.max), 1)
                    dve.wait_ge(S("so_pe"), n + 1)
                    step(V.tensor_tensor(p0_s, ps[:, 0, 0:1], p0_base, ALU.add), 2)
                    step(V.tensor_tensor(p0_base, ps[:, 0, 1:2], p0_base, ALU.add), 3)
                    step(V.tensor_scalar(p0_cur, p0_cur, 1.0, None, ALU.add), 4)
                    step(V.scalar_tensor_tensor(out=mask, in0=p0_cum, scalar=p0_s, in1=mask, op0=ALU.add,
                                                op1=ALU.mult), 5)
                    step(V.tensor_tensor(p0_pos, p0_pos, mask, ALU.add), 6)
                V.tensor_copy(p0_posi, p0_pos).then_inc(S("so_posi"), 1)
                dve.sem_inc(S("so_made"), 1)
                dve.sem_inc(S("so_rec"), 1)

                def records(t, first):
                    dve.wait_ge(S("so_pe"), t + (NP + 2))
                    if not first:
                        dve.wait_ge(S("so_sc"), t * 16)
                    hold(dve)
                    V.tensor_copy(p0_rec[:, 0:D], ps[:, 1, 0:D])
                    V.tensor_copy(p0_rec[:, D:D + S10], p0_sh[:, ds(t * S10, S10)])
                    for j, n in enumerate(_ROWS):
                        rec = p0_rec if n == "edge_weight" else p0_rec.bitcast(i32)
                        last = V.tensor_copy(rec[:, D + S10 + j:D + S10 + j + 1], p0_col[n][:, ds(t, 1)])
                    last.then_inc(S("so_made"), 1)

                records(0, True)
                with dve.Fori(1, NT) as t:
                    records(t, False)
                with dve.Fori(0, NT) as t:
                    dve.wait_ge(S("so_pe"), t + (NP + 2 + NT))
                    hold(dve)
                    V.tensor_copy(p0_r2T, ps[0:D, 2, 0:P]).then_inc(S("so_rec"), 1)
                barrier(dve, 1, order_made)
            V.memset(small[:, 3:4], 0.0)
            dve.wait_ge(S("ld_dst"), 16)
            L(V.memset(p1_cnt, 0.0))
            L(V.tensor_copy(p1_dst, p1_dst_i))
            L(V.tensor_scalar(p1_lt, p1_dst, float(NP - 1), None, ALU.min))
            L(V.tensor_copy(dst_t[:, :], p1_lt))
            for w in range(1, NW):
                L(V.tensor_scalar(p1_lt, p1_dst, float(P * w), None, ALU.is_lt))
                L(V.tensor_reduce(out=p1_cnt[:, w - 1:w], in_=p1_lt, axis=AX.X, op=ALU.add))
            V.memset(p1_ts, 0.0).then_inc(S("cnt"), 1)
            V.memset(p1_sb, 0.0)
            L(V.memset(p1_off, 0.0))
            dve.wait_ge(S("cnt_mm"), 1)
            L(V.tensor_copy(p1_bi, ps[:, 0, 0:32]))
            L(V.tensor_scalar(p1_bi, p1_bi, 7, None, ALU.arith_shift_right))
            L(V.tensor_copy(p1_te, p1_bi))
            L(V.memset(p1_te[:, NW - 1:NW], float(REAL_TILES - 1)))
            L(V.tensor_copy(p1_ts[:, 1:NW], p1_te[:, 0:NW - 1]))
            L(V.tensor_tensor(p1_nb[:, 0:NW], p1_te[:, 0:NW], p1_ts[:, 0:NW], ALU.subtract))
            L(V.tensor_scalar(p1_nb[:, 0:NW], p1_nb[:, 0:NW], float(U), None, ALU.add))
            L(V.tensor_copy(p1_nbi[:, 0:NW], p1_nb[:, 0:NW]))
            L(V.tensor_scalar(p1_nbi[:, 0:NW], p1_nbi[:, 0:NW], 2, None, ALU.arith_shift_right))
            L(V.tensor_copy(p1_nb[:, 0:NW], p1_nbi[:, 0:NW]))
            L(V.tensor_tensor_scan(p1_cum[:, 0:NW], ones[:, 0:NW], p1_nb[:, 0:NW], 0.0, ALU.mult, ALU.add))
            L(V.tensor_copy(p1_sb[:, 1:NW], p1_cum[:, 0:NW - 1]))
            L(V.memset(p1_sb[:, NW:NW + 1], float(NB)))
            L(V.tensor_copy(blk_i[:, :], p1_sb[:, 0:NW + 1]))
            L(V.tensor_scalar(p1_cum[:, 0:NW], p1_sb[:, 0:NW], float(U), None, ALU.mult))
            L(V.tensor_tensor(p1_off[:, 0:NW], p1_ts[:, 0:NW], p1_cum[:, 0:NW], ALU.subtract))
            L(V.tensor_tensor(p1_doff[:, 0:NW - 1], p1_off[:, 1:NW], p1_off[:, 0:NW - 1], ALU.subtract))
            m3 = p1_mask.rearrange("p (b w) -> p b w", w=24)
            o3 = p1_mo.rearrange("p (b w) -> p b w", w=24)
            dve.wait_ge(S("consts"), 1)
            dve.wait_ge(S("consts1"), 1)
            L(V.tensor_tensor(m3, p1_cum[:, 1:NW].unsqueeze(1).to_broadcast([P, NBLK, 24]),
                              p1_i.unsqueeze(2).to_broadcast([P, NBLK, 24]), ALU.is_le))
            L(V.tensor_tensor(o3, m3, p1_doff[:, 0:NW - 1].unsqueeze(1).to_broadcast([P, NBLK, 24]), ALU.mult))
            L(V.tensor_reduce(out=p1_w, in_=m3, axis=AX.X, op=ALU.add))
            L(V.tensor_reduce(out=p1_o, in_=o3, axis=AX.X, op=ALU.add))
            L(V.tensor_copy(p1_ki, p1_k))
            L(V.tensor_scalar(p1_ki, p1_ki, U - 1, None, ALU.bitwise_and))
            L(V.tensor_copy(p1_k, p1_ki))
            L(V.tensor_tensor(p1_t, p1_i, p1_o, ALU.add))
            L(V.tensor_tensor(p1_t, p1_t, p1_k, ALU.subtract))
            L(V.tensor_scalar(p1_t, p1_t, float(NT), None, ALU.min))
            L(V.tensor_tensor(p1_t, p1_t, p1_k, ALU.add))
            V.tensor_copy(p1_ti, p1_t).then_inc(S("tiles_known"), 1)
            L(V.tensor_scalar(p1_w, p1_w, float(P), None, ALU.mult))
            V.tensor_scalar(realrow[:, :], pcol[:, :], float(LAST), None, ALU.is_lt)
            dve.wait_ge(S("g_dst"), 16 * NBLK)
            L(V.tensor_copy(p1_f, p1_g["dst"]))
            L(V.tensor_tensor(p1_rel.rearrange("p (b e) -> p b e", e=P), p1_f.rearrange("p (b e) -> p b e", e=P),
                              p1_w.unsqueeze(2).to_broadcast([P, NBLK, P]), ALU.subtract))
            L(V.tensor_scalar(p1_a, p1_rel, 0.0, None, ALU.is_ge))
            L(V.tensor_scalar(p1_b, p1_rel, float(P), None, ALU.is_lt))
            L(V.tensor_tensor(p1_a, p1_a, p1_b, ALU.mult))
            L(V.tensor_scalar(p1_rel, p1_rel, 1.0, None, ALU.add))
            L(V.tensor_tensor(p1_rel, p1_rel, p1_a, ALU.mult))
            L(V.tensor_scalar(p1_rel, p1_rel, -1.0, None, ALU.add))
            dve.wait_ge(S("g_src"), 16 * NBLK)
            dve.wait_ge(S("g_typ"), 16 * NBLK)
            V.tensor_copy(p1_s, p1_g["src"])
            L(V.tensor_copy(p1_b, p1_g["typ"]))
            dve.wait_ge(S("g_wgt"), 16 * NBLK)
            V.scalar_tensor_tensor(out=p1_x, in0=p1_s, scalar=float(R), in1=p1_b, op0=ALU.mult, op1=ALU.add
                                   ).then_inc(S("tab_in"), 1)
            dve.wait_ge(S("tab_tr"), 1)
            for r, (dst_ap, srcps) in enumerate(((rel_t[:, :], 0), (xwi_t[:, :], 4), (w_t[:, :], 6))):
                V.tensor_copy(dst_ap, psf[:, srcps * 512:srcps * 512 + NSP])
            V.tensor_scalar(srcc_t[:, :], psf[:, 1024:1024 + NSP], float(-CENTRE), None, ALU.add
                            ).then_inc(S("tab_out"), 1)
            barrier(dve, 1)
            x_transposes(0)
            V.memset(p3_z, 0.0)
            for t in p3_mm:
                V.memset(t[:, 2 * D:4 * D].bitcast(f32), 0.0)
            barrier(dve, 2)
            dve.sem_inc(S("oh3"), 2 * U)
            with dve.Fori(0, NB // 2) as b2:
                for j in range(2 * U):
                    i = b2 * (2 * U) + j
                    k = j % U
                    dve.wait_ge(S("slot3_free"), i + 1)
                    V.tensor_scalar(p3_ohs[k], p3_iota, srcc_t[:, ds(i, 1)], None, ALU.is_equal)
                    V.tensor_scalar(p3_ohd[k], iota128[:, :], rel_t[:, ds(i, 1)], None, ALU.is_equal
                                    ).then_inc(S("ohs3"), 1)
                    dve.wait_ge(S(f"g_x{j}"), b2 * 16 + 16)
                    V.tensor_scalar(p3_mm[k][:, 0:D], p3_msg[j], w_t[:, ds(i, 1)], None, ALU.mult
                                    ).then_inc(S("mh3"), 1)
                    dve.wait_ge(S("mh3"), i + 1)
                    V.scalar_tensor_tensor(out=p3_mm[k][:, D:2 * D], in0=p3_msg[j], scalar=w_t[:, ds(i, 1)],
                                           in1=p3_mm[k][:, 0:D].bitcast(f32), op0=ALU.mult, op1=ALU.subtract
                                           ).then_inc(S("oh3"), 1)
            barrier(dve, 3)
            s4 = p3_sum.rearrange("p (w a d) -> p w a d", a=2, d=D)
            L(V.tensor_tensor(agg[:, :, :], s4[:, :, 0, :], s4[:, :, 1, :], ALU.add))
            L(V.tensor_tensor(t1[:, :, :], x[:, :, :], agg[:, :, :], ALU.add))
            layer_norm(0)
            V.memset(p5_adj[0][:, N:NP], 0.0).then_inc(S("x_ready"), 1)
            V.memset(p5_adj[1][:, N:NP], 0.0).then_inc(S("adj_zero"), 1)
            x_transposes(1)
            s3 = p5_s.rearrange("p (w h) -> p w h", h=H1)
            e3 = p5_e.rearrange("p (w h) -> p w h", h=H1)
            for w in range(NW):
                dve.wait_ge(S("node_mm"), SC_AT + w + 1)
                pr = p5_pr[w % 2].rearrange("p (h e) -> p h e", h=H1)
                L(V.tensor_tensor(pr, ps[:, 4 + w % 2, 0:256].rearrange("p (h e) -> p h e", h=H1),
                                  x[:, w, :].unsqueeze(1).to_broadcast([P, H1, D]), ALU.mult))
                V.tensor_reduce(out=s3[:, w, :], in_=pr, axis=AX.X, op=ALU.add).then_inc(S("sc_used"), 1)
            dve.wait_ge(S("sc_used"), NW)
            L(V.tensor_scalar(p5_s, p5_s, D ** -0.5, None, ALU.mult))
            L(V.tensor_scalar(small[:, 0:1], realrow[:, :], BIG, -BIG, ALU.mult, ALU.add))
            L(V.tensor_tensor(s3[:, NW - 1, :], s3[:, NW - 1, :], small[:, 0:1].to_broadcast([P, H1]), ALU.add))
            V.tensor_reduce(out=p5_m, in_=p5_s.rearrange("p (w h) -> p h w", h=H1), axis=AX.X, op=ALU.max
                            ).then_inc(S("sc_max"), 1)
            dve.wait_ge(S("sc_gmax"), 1)
            V.tensor_tensor(e3, s3, p5_mm.unsqueeze(1).to_broadcast([P, NW, H1]), ALU.subtract
                            ).then_inc(S("sc_sub"), 1)
            dve.wait_ge(S("sc_exp"), 1)
            V.tensor_reduce(out=p5_z, in_=p5_e.rearrange("p (w h) -> p h w", h=H1), axis=AX.X, op=ALU.add
                            ).then_inc(S("sc_sum"), 1)
            dve.wait_ge(S("sc_gsum"), 1)
            L(V.reciprocal(p5_ri, p5_zz))
            L(V.tensor_tensor(e3, e3, p5_ri.unsqueeze(1).to_broadcast([P, NW, H1]), ALU.mult))
            dve.wait_ge(S("hw_out"), NW)
            hw4 = p5_hw.rearrange("p (g e) -> p g e", e=D)
            L(V.tensor_tensor(hw4, hw4, p5_e.unsqueeze(2).to_broadcast([P, NW * H1, D]), ALU.mult))
            L(V.tensor_reduce(out=p5_zt.rearrange("p (w e) -> p w e", e=D),
                              in_=p5_hw.rearrange("p (w h e) -> p w e h", h=H1, e=D), axis=AX.X, op=ALU.add))
            V.memset(deg[:, :], 1.0)
            barrier(dve, 4)
            for w in range(NW):
                for g in range(7):
                    cols = min(512, NP - g * 512)
                    dve.wait_ge(S("at_out"), 7 * w + g + 1)
                    V.tensor_reduce(out=t1[:, w % 2, g * 4:g * 4 + cols // P],
                                    in_=p5_at[:, g * 512:g * 512 + cols].rearrange("p (c e) -> p c e", e=P), axis=AX.X, op=ALU.add
                                    ).then_inc(S("deg_red"), 1)
                dve.wait_ge(S("deg_red"), 7 * w + 7)
                L(V.tensor_tensor(deg[:, :], deg[:, :], t1[:, w % 2, 0:NW], ALU.add))
                dve.wait_ge(S("z_mm"), 7 * w + 7)
                V.tensor_copy(agg[:, w, :], ps[:, 4 + w % 2, 0:D]).then_inc(S("z_out"), 1)
            dve.wait_ge(S("z_out"), NW)
            V.tensor_scalar(t1[:, :, :], agg[:, :, :], 0.0, None, ALU.min).then_inc(S("elu_min"), 1)
            L(V.tensor_scalar(agg[:, :, :], agg[:, :, :], 0.0, -1.0, ALU.max, ALU.add))
            dve.wait_ge(S("elu_exp"), 1)
            L(V.tensor_tensor(agg[:, :, :], agg[:, :, :], t1[:, :, :], ALU.add))
            L(V.tensor_tensor(t1[:, :, :], x[:, :, :], agg[:, :, :], ALU.add))
            layer_norm(1)
            barrier(dve, 5)
            x_transposes(2)
            V.memset(p8_w2, 0.0)
            V.memset(ones_r[:, :].bitcast(f32), 1.0)
            V.memset(b2r[:, :].bitcast(f32), 0.0).then_inc(S("w2_zero"), 1)
            dve.wait_ge(S("ld_c"), 16 * LD_C)
            L(V.tensor_copy(c_a[:, :], p8_c))
            cut = (XC - 1) * 2 * OK
            ca = c_a[:, :].bitcast(f32)
            V.tensor_tensor(c_b[:, 0:cut], p8_c[:, 0:cut], ca[:, 0:cut], ALU.subtract)
            V.memset(c_b[:, cut:].bitcast(f32), 0.0)
            L(V.tensor_copy(b2r[0:1, :], p8_b2[0:1, :]))
            L(V.tensor_copy(c_b[0:D, cut:], p8_c[0:D, cut:]))
            L(V.tensor_tensor(c_a[D:P, cut:], p8_c[D:P, cut:], ca[D:P, cut:], ALU.subtract))
            V.tensor_copy(b2r[32:33, :], p8_b2[32:33, :])
            V.tensor_copy(w1h[:, :], p8_w1)
            L(V.tensor_copy(w2h, p8_w2))
            V.tensor_tensor(w1l[:, :], p8_w1[0:D, :], w1h[0:D, :].bitcast(f32), ALU.subtract)
            V.tensor_tensor(w2l, p8_w2, w2h.bitcast(f32), ALU.subtract)
            L(V.tensor_tensor(b2r[32:33, :], p8_b2[32:33, :], b2r[32:33, :].bitcast(f32), ALU.subtract))
            barrier(dve, 6)
            dve.sem_inc(S("xs_made"), G)
            dve.sem_inc(S("q_used"), G)
            dve.sem_inc(S("kv_made"), 2)
            dve.sem_inc(S("xl_made"), 2)

            def outer(j, i, it):
                dve.wait_ge(S(f"g_x{j}"), it * 16 + (16 * (NB // 2) + 16))
                dve.wait_ge(S("xs_tr"), i + 1)
                V.tensor_tensor(p8_xs[j % 4].rearrange("p (s d) -> p s d", d=D),
                                p8_xg[j].unsqueeze(1).to_broadcast([P, S10, D]),
                                p8_sh[:, ds(i * S10, S10)].unsqueeze(2).to_broadcast([P, S10, D]), ALU.mult
                                ).then_inc(S("xs_made"), 1)

            def low_part(j, i):
                dve.wait_ge(S("xt_out"), i + 1)
                dve.wait_ge(S("tp_mm"), i + 1)
                V.tensor_tensor(xl[j % 2][:, :], psf[:, (j % 2) * 1024:(j % 2) * 1024 + XC * P],
                                xh[j % 2][:, :].bitcast(f32), ALU.subtract).then_inc(S("xl_made"), 1)

            def products(j, i, it, first):
                dve.wait_ge(S("w_out"), i + 2)
                if not first:
                    dve.wait_ge(S(f"st_v{j // U}"), it * 16)
                dve.wait_ge(S("tp_mm"), i + 3)
                V.tensor_tensor(p8_kv[:, j * 2 * OK:(j + 1) * 2 * OK], ps[:, 6 + j % 2, 0:256], p8_wk[j % 2], ALU.mult
                                ).then_inc(S("kv_made"), 1)

            def q_times_k(h, i, it):
                for j in range(h * U, (h + 1) * U):
                    dve.wait_ge(S(f"g_q{j}"), it * 16 + 16)
                dve.wait_ge(S("kv_made"), i + (U + 2))
                V.tensor_tensor(p8_pr.rearrange("p (j c) -> p j c", c=OK),
                                p8_kv.rearrange("p (j c) -> p j c", c=2 * OK)[:, h * U:(h + 1) * U, 0:OK],
                                p8_q[:, h * U * OK:(h + 1) * U * OK].rearrange("p (j c) -> p j c", c=OK), ALU.mult
                                ).then_inc(S("q_used"), U)

            def head_sums(i):
                dve.wait_ge(S("q_used"), i + (G + U))
                hold(dve)
                V.tensor_reduce(out=lg[:, ds(i * H2, U * H2)], in_=p8_pr.rearrange("p (h c) -> p h c", c=OK // H2),
                                axis=AX.X, op=ALU.add).then_inc(S("lg_made"), U)

            def att_low(h, n):
                dve.wait_ge(S("att_high"), n + 1)
                V.tensor_tensor(att_r[h][D:P, :], p8_att[h][D:P, :], att_r[h][D:P, :].bitcast(f32), ALU.subtract
                                ).then_inc(S("att_low"), 1)

            def hid_low(h, n):
                dve.wait_ge(S("hid_out"), n + 2)
                V.tensor_tensor(hid_l[h][:, :], p8_hid[h], hid_h[h][:, :].bitcast(f32), ALU.subtract
                                ).then_inc(S("hid_low"), 1)

            def dve_tiles(it, first, last):
                for j in range(G):
                    i = it * G + j
                    if j < G - 2:
                        outer(j + 2, i + 2, it)
                    elif not last:
                        outer(j + 2 - G, i + 2, it + 1)
                    if not (last and j == G - 1):
                        low_part(j + 1, i + 1)
                    if j == U:
                        q_times_k(0, i - U, it)
                    elif j == 0 and not first:
                        q_times_k(1, i - U, it - 1)
                    if j == 1:
                        att_low(1, it * 2 + 1)
                    if j == 3:
                        hid_low(1, it * 2 + 1)
                    if j == 5 and not last:
                        att_low(0, it * 2 + 2)
                    if j == 7 and not last:
                        hid_low(0, it * 2 + 2)
                    products(j, i, it, first)
                    if not (first and j < U) and j % U == 1:
                        head_sums(i - (U + 1))

            outer(0, 0, 0)
            outer(1, 1, 0)
            low_part(0, 0)
            att_low(0, 0)
            hid_low(0, 0)
            dve_tiles(0, True, False)
            with dve.Fori(1, NIT - 1) as it:
                dve_tiles(it, False, False)
            dve_tiles(NIT - 1, False, True)
            q_times_k(1, NT - U, NIT - 1)
            head_sums(NT - U)
            dve.wait_ge(S("lg_made"), NT)
            barrier(dve, 7)
            rows_g = [min(4, NG - 4 * g) for g in range(-(-NG // 4))]
            for g, n in enumerate(rows_g):
                dve.wait_ge(S("lg_tr"), g + 1)
                if g >= 2:
                    dve.wait_ge(S(f"st_lg{g % 2}"), 16 * (g // 2))
                V.tensor_copy(pA_row[g % 2][:, 0:n * P], ps[:, g % 2, 0:n * P]).then_inc(S("lg_row"), 1)
            q = slice(0, SCP)
            dve.wait_ge(S("lg_row"), len(rows_g))
            V.memset(pS_l, 0.0).then_inc(S("lg_gone"), 1)
            dve.wait_ge(S("ld_scan"), 16 * (H2 + 1))
            L(V.tensor_copy(pS_dv[q, :], pS_di[q, :]))
            L(V.memset(pS_v1[q, :], 0.0))
            L(V.tensor_tensor_scan(pS_pm[q, :], pS_v1[q, :], pS_dv[q, :], -1.0, ALU.add, ALU.max))
            L(V.tensor_copy(pS_l[q, 0:8], pS_pm[q, SCL - 1:SCL].to_broadcast([SCP, 8])))
            V.tensor_copy(pS_l[q, 8:9], pS_l[q, 0:1]).then_inc(S("sc_in"), 1)
            T = [pS_tr[:, i * P:(i + 1) * P] for i in range(8)]
            dve.wait_ge(S("sc_tr"), 1)
            L(V.memset(pS_tr, 0.0))
            L(V.tensor_copy(T[0][:, 0:SCP], ps[0:8, 2, 0:SCP]))
            L(V.memset(T[2][:, 0:1], -1.0))
            L(V.tensor_tensor_scan(T[2][:, 1:SCP], T[1][:, 0:SCP - 1], T[0][:, 0:SCP - 1], -1.0, ALU.add, ALU.max))
            V.memset(T[3][:, 0:1], 0.0).then_inc(S("sc_back"), 1)
            dve.wait_ge(S("sc_bk"), 1)
            L(V.tensor_copy(pS_l[q, 16:24], ps[0:SCP, 3, 0:8]))
            L(V.tensor_scalar(pS_pm[q, :], pS_pm[q, :], pS_l[q, 16:17], None, ALU.max))
            L(V.tensor_tensor(pS_new[q, 1:SCL], pS_dv[q, 1:SCL], pS_pm[q, 0:SCL - 1], ALU.is_gt))
            L(V.tensor_tensor(pS_new[q, 0:1], pS_dv[q, 0:1], pS_l[q, 16:17], ALU.is_gt))
            L(V.tensor_scalar(pS_new[q, :], pS_new[q, :], -BIG, None, ALU.mult))
            L(V.tensor_reduce(out=pS_l[q, 24:25], in_=pS_new[q, :], axis=AX.X, op=ALU.min))
            L(V.tensor_reduce(out=pS_l[q, 25:26], in_=pS_new[q, 1:SCL], axis=AX.X, op=ALU.min))
            for h in range(H2):
                L(V.tensor_tensor_scan(pS_f[q, h * SCL:(h + 1) * SCL], pS_new[q, :], pS_a[q, h * SCL:(h + 1) * SCL],
                                       -BIG, ALU.add, ALU.max))
            f3 = pS_f[q, :].rearrange("p (h j) -> p h j", h=H2)
            L(V.tensor_copy(pS_l[q, 32:40], f3[:, :, SCL - 1]))
            V.tensor_copy(pS_l[q, 40:48], pS_l[q, 24:25].to_broadcast([SCP, 8])).then_inc(S("sc_in"), 1)
            dve.wait_ge(S("sc_tr"), 2)
            V.tensor_copy(T[0][:, 0:SCP], ps[0:8, 2, 0:SCP])
            L(V.tensor_copy(T[1][:, 0:SCP], ps[0:8, 2, P:P + SCP]))
            L(V.memset(T[2][:, 0:1], -BIG))
            L(V.tensor_tensor_scan(T[2][:, 1:SCP], T[1][:, 0:SCP - 1], T[0][:, 0:SCP - 1], -BIG, ALU.add, ALU.max))
            V.memset(T[3][:, 0:1], 0.0).then_inc(S("sc_back"), 1)
            dve.wait_ge(S("sc_bk"), 2)
            L(V.tensor_copy(pS_l[q, 48:56], ps[0:SCP, 3, 0:8]))
            for h in range(H2):
                L(V.tensor_tensor_scan(pS_f[q, h * SCL:(h + 1) * SCL], pS_new[q, :], pS_a[q, h * SCL:(h + 1) * SCL],
                                       pS_l[q, 48 + h:49 + h], ALU.add, ALU.max))
            L(V.memset(pS_v1[q, SCL - 1:SCL], 0.0))
            L(V.tensor_copy(pS_v1[q, 0:SCL - 1], pS_new[q, 1:SCL]))
            bwd = pS_pm
            for h in range(H2):
                L(V.tensor_tensor_scan(bwd[q, ::-1], pS_v1[q, ::-1], pS_f[q, h * SCL:(h + 1) * SCL][:, ::-1],
                                       -BIG, ALU.add, ALU.max))
                L(V.tensor_copy(pS_l[q, 32 + h:33 + h], bwd[q, 0:1]))
            V.tensor_copy(pS_l[q, 40:48], pS_l[q, 25:26].to_broadcast([SCP, 8]))
            L(V.tensor_copy(pS_l[q, 56:64], pS_new[q, 0:1].to_broadcast([SCP, 8])))
            V.memset(T[3][:, 0:1], 0.0).then_inc(S("sc_in"), 1)
            dve.wait_ge(S("sc_tr"), 3)
            V.tensor_copy(T[0][:, 0:SCP], ps[0:8, 2, 0:SCP])
            V.tensor_copy(T[1][:, 0:SCP], ps[0:8, 2, P:P + SCP])
            L(V.tensor_copy(T[4][:, 0:SCP], ps[0:8, 2, 2 * P:2 * P + SCP]))
            L(V.memset(T[5][:, 0:P], -BIG))
            L(V.tensor_copy(T[6][:, 0:SCP], T[1][:, 0:SCP]))
            L(V.tensor_tensor(T[6][:, 0:SCP - 1], T[1][:, 0:SCP - 1], T[4][:, 1:SCP], ALU.add))
            L(V.tensor_tensor_scan(T[5][:, 0:SCP][:, ::-1], T[6][:, 0:SCP][:, ::-1], T[0][:, 0:SCP][:, ::-1],
                                   -BIG, ALU.add, ALU.max))
            L(V.memset(T[2][:, 0:P], -BIG))
            L(V.tensor_tensor(T[2][:, 0:SCP - 1], T[5][:, 1:SCP], T[4][:, 1:SCP], ALU.add))
            V.memset(T[3][:, 0:1], 0.0).then_inc(S("sc_back"), 1)
            dve.wait_ge(S("sc_bk"), 3)
            L(V.tensor_copy(pS_l[q, 48:56], ps[0:SCP, 3, 0:8]))
            for h in range(H2):
                L(V.tensor_tensor_scan(bwd[q, ::-1], pS_v1[q, ::-1], pS_f[q, h * SCL:(h + 1) * SCL][:, ::-1],
                                       pS_l[q, 48 + h:49 + h], ALU.add, ALU.max))
                L(V.tensor_tensor(pS_a[q, h * SCL:(h + 1) * SCL], pS_a[q, h * SCL:(h + 1) * SCL], bwd[q, :],
                                  ALU.subtract))
            V.tensor_scalar(pS_a[q, :], pS_a[q, :], 0.0, None, ALU.min).then_inc(S("ex_sub"), 1)
            dve.wait_ge(S("st_ex"), 16 * H2)
            for g, n in enumerate(rows_g):
                dve.wait_ge(S("ex_tr"), g + 1)
                V.tensor_copy(pB_ex[:, g * 512:g * 512 + n * P], ps[:, g % 2, 0:n * P]).then_inc(S("ex_col"), 1)
            V.memset(pB_ex[:, NT * H2:NTR * H2], 0.0)
            V.memset(pB_z, 0.0)
            L(V.memset(pB_v[0], 0.0))
            V.memset(pB_r, 0.0).then_inc(S("v_zero"), 1)
            barrier(dve, 8)
            dve.sem_inc(S("v_used"), U)
            with dve.Fori(0, NB // 2) as b2:
                for j in range(2):
                    t = dve.value_load(tile_row[0:1, ds(b2 * (2 * U) + j * U, 1)], min_val=0, max_val=NT)
                    for k in range(0, U, 2):
                        i = b2 * (2 * U) + (j * U + k)
                        ex2 = pB_ex[:, ds(t * H2 + k * H2, 2 * H2)].rearrange("p (k h) -> p k h", k=2)
                        dve.wait_ge(S("slotB_free"), i + 2)
                        V.tensor_tensor(pB_oh[:, k:k + 2, :], iota128[:, :].unsqueeze(1).to_broadcast([P, 2, P]),
                                        rel_t[:, ds(i, 2)].unsqueeze(2).to_broadcast([P, 2, P]), ALU.is_equal)
                        V.tensor_copy(pB_vx[:, k:k + 2, OK:VW], ex2)
                        if k == 0:
                            dve.wait_ge(S(f"ld_v{j}"), b2 * 16 + 16)
                        V.tensor_tensor(pB_vx[:, k:k + 2, 0:OK].rearrange("p k (h c) -> p k h c", h=H2),
                                        pB_v[j][:, k * OK:(k + 2) * OK].rearrange("p (k h c) -> p k h c", k=2, h=H2),
                                        ex2.unsqueeze(3).to_broadcast([P, 2, H2, OK // H2]),
                                        ALU.mult).then_inc(S("v_used"), 1)
            barrier(dve, 9)
            dve.wait_ge(S("accB"), NW + 1)
            ac3 = pB_acc.rearrange("p (w c) -> p w c", c=VW)
            r3 = pB_r.rearrange("p (w h) -> p w h", h=H2)
            L(V.tensor_scalar(r3, ac3[:, :, OK:VW], 1e-16, None, ALU.add))
            L(V.reciprocal(r3, r3))
            for w in range(NW):
                u3 = ac3[:, w, 0:OK].rearrange("p (h c) -> p h c", h=H2)
                V.tensor_tensor(u3, u3, r3[:, w, :].unsqueeze(2).to_broadcast([P, H2, OK // H2]), ALU.mult
                                ).then_inc(S("upd"), 1)
            for w in range(NW):
                dve.wait_ge(S("u_tr"), w + 1)
                if w >= 2:
                    dve.wait_ge(S("node_mm"), U_AT + w - 1)
                V.tensor_copy(pB_uT[w % 2], ps[:, w % 2, 0:P]).then_inc(S("u_out"), 1)
                dve.wait_ge(S("node_mm"), U_AT + w + 1)
                V.tensor_tensor(t1[:, w, :], self_o[:, w, :], ps[:, 2 + w % 2, 0:D], ALU.add).then_inc(S("u_add"), 1)
            dve.wait_ge(S("u_add"), NW)
            V.tensor_reduce(out=pB_n[:, 0:D], in_=t1[:, :, :].rearrange("p w d -> p d w"), axis=AX.X, op=ALU.add
                            ).then_inc(S("bn_in"), 1)
            dve.wait_ge(S("bn_mm"), 1)
            L(V.tensor_scalar(pB_n[:, D:2 * D], ps[:, 4, 0:D], 1.0 / N, None, ALU.mult))
            L(V.tensor_tensor(t1[:, :, :], t1[:, :, :], pB_n[:, D:2 * D].unsqueeze(1).to_broadcast([P, NW, D]),
                              ALU.subtract))
            L(V.tensor_scalar(t1[:, NW - 1, :], t1[:, NW - 1, :], realrow[:, :], None, ALU.mult))
            L(V.tensor_tensor(agg[:, :, :], t1[:, :, :], t1[:, :, :], ALU.mult))
            V.tensor_reduce(out=pB_n[:, 0:D], in_=agg[:, :, :].rearrange("p w d -> p d w"), axis=AX.X, op=ALU.add
                            ).then_inc(S("bn_in"), 1)
            dve.wait_ge(S("bn_mm"), 2)
            V.tensor_scalar(pB_n[:, 0:D], ps[:, 4, 0:D], 1.0 / N, 1e-5, ALU.mult, ALU.add).then_inc(S("bn_var"), 1)
            dve.wait_ge(S("bn_sd"), 1)
            L(V.reciprocal(pB_n[:, 2 * D:3 * D], pB_n[:, 0:D]))
            L(V.tensor_tensor(pB_n[:, 2 * D:3 * D], pB_n[:, 2 * D:3 * D], gam[:, 0, :], ALU.mult))
            L(V.tensor_tensor(t1[:, :, :], t1[:, :, :], pB_n[:, 2 * D:3 * D].unsqueeze(1).to_broadcast([P, NW, D]),
                              ALU.mult))
            L(V.tensor_tensor(t1[:, :, :], t1[:, :, :], gam[:, 1, :].unsqueeze(1).to_broadcast([P, NW, D]), ALU.add))
            L(V.tensor_tensor(t1[:, :, :], t1[:, :, :], x[:, :, :], ALU.add))
            layer_norm(2)
            dve.wait_ge(S("deg_sd"), 1)
            L(V.reciprocal(dinv[:, :], dinv[:, :]))
            barrier(dve, 10)
            dve.wait_ge(S("w3_tr"), 1)
            V.tensor_copy(w3T[:, :], ps[0:D, 6, 0:D]).then_inc(S("w3_out"), 1)
            x_transposes(3)
            for w in range(NW):
                dve.wait_ge(S("node_mm"), H_AT + w + 1)
                V.tensor_tensor(t1[:, w, :], ps[:, 4 + w % 2, 0:D], gam[:, 2, :], ALU.add).then_inc(S("u_add"), 1)
            dve.wait_ge(S("u_add"), 2 * NW)
            V.tensor_tensor(t1[:, :, :], t1[:, :, :], bw(dinv[:, :]), ALU.mult).then_inc(S("g_ready"), 1)
            V.memset(pD_oT[:, N:NP], 0.0).then_inc(S("oT_zero"), 1)
            for w in range(NW):
                dve.wait_ge(S("u_tr"), NW + w + 1)
                V.tensor_copy(agg[:, w, :], ps[:, w % 4, 0:D]).then_inc(S("u_out"), 1)
            dve.wait_ge(S("u_out"), 2 * NW)
            L(V.tensor_tensor(t1[:, :, :], t1[:, :, :], agg[:, :, :], ALU.add))
            L(V.tensor_tensor(t1[:, :, :], t1[:, :, :], bw(dinv[:, :]), ALU.mult))
            L(V.tensor_tensor(t1[:, :, :], t1[:, :, :], x[:, :, :], ALU.add))
            layer_norm(3)
            V.memset(small[:, 2:3], 0.0).then_inc(S("final"), 1)

        @block.tensor
        def _(pe):
            def mm(out, lhsT, rhs, start=True, stop=True, **kw):
                return nc.tensor.matmul(out, lhsT, rhs, start=start, stop=stop, **kw)

            def tr(out, in_):
                k = in_.shape[0]
                return nc.tensor.transpose(out, in_, ident[0:k, 0:k])

            def x_transposes(tag):
                for w in range(NW):
                    if w >= 4:
                        pe.wait_ge(S("xT_out"), tag * NW + w - 3)
                    tr(ps[0:D, w % 4, 0:P], x[:, w, :]).then_inc(S("xT_tr"), 1)
                pe.wait_ge(S("xT_out"), tag * NW + NW)

            pe.wait_ge(S("consts"), 1)
            pe.wait_ge(S("consts0"), 1)
            barrier(pe, 1, order_known)
            with pe.If(is_unsorted(pe)):
                with pe.Fori(0, NP + 1) as n:
                    pe.wait_ge(S("so_dve"), n * 7 + 3)
                    mm(ps[:, 0, 0:1], tri[:, :], p0_cum[:, NT - 1:NT])
                    mm(ps[:, 0, 1:2], ones[:, :], p0_cum[:, NT - 1:NT]).then_inc(S("so_pe"), 1)
                with pe.Fori(0, NT) as t:
                    pe.wait_ge(S("so_ld"), t * 16 + 160)
                    pe.wait_ge(S("so_made"), t + 1)
                    hold(pe)
                    tr(ps[:, 1, 0:D], p0_at).then_inc(S("so_pe"), 1)
                with pe.Fori(0, NT) as t:
                    pe.wait_ge(S("so_ld2"), t * 16 + 16)
                    pe.wait_ge(S("so_rec"), t + 1)
                    hold(pe)
                    tr(ps[0:D, 2, 0:P], p0_r2[:, 0:D]).then_inc(S("so_pe"), 1)
                barrier(pe, 1, order_made)
            hold(pe)
            pe.wait_ge(S("cnt"), 1)
            pe.wait_ge(S("consts"), 1)
            mm(ps[:, 0, 0:32], ones[:, :], p1_cnt).then_inc(S("cnt_mm"), 1)
            pe.wait_ge(S("tab_in"), 1)
            for j, t in enumerate((p1_rel, p1_s, p1_x, p1_g["wgt"])):
                for c_ in range(NBLK):
                    last = tr(psf[:, j * 1024 + c_ * P:j * 1024 + (c_ + 1) * P], t[:, c_ * P:(c_ + 1) * P])
            last.then_inc(S("tab_tr"), 1)
            pe.wait_ge(S("ld_x"), 32)
            barrier(pe, 1)
            x_transposes(0)
            for w in range(NW):
                if w >= 2:
                    pe.wait_ge(S("xw_out"), w - 1)
                mm(ps[:, 4 + w % 2, :], xT[:, w * P:(w + 1) * P], w0[:, :, :].rearrange("f r o -> f (r o)")
                   ).then_inc(S("node_mm"), 1)
            barrier(pe, 2)
            pe.sem_inc(S("slot3_free"), U)
            with pe.Fori(0, NW) as w:
                for g in range(8):
                    if g in (0, 4, 7):
                        pe.wait_ge(S("adj_out"), w * 3 + {0: 1, 4: 2, 7: 3}[g])
                    cols = 512 if g < 7 else 4 * D
                    mm(ps[:, g, 0:cols], p3_z[:, 0:P], p3_z[:, 0:cols], start=True, stop=False,
                       skip_group_check=True)
                b0 = pe.value_load(blk_i[0:1, ds(w, 1)], min_val=0, max_val=NB)
                b1 = pe.value_load(blk_i[0:1, ds(w + 1, 1)], min_val=1, max_val=NB)
                with pe.Fori(b0, b1) as b:
                    for k in range(U):
                        pe.wait_ge(S("ohs3"), b * U + (k + 1))
                        for g in range(7):
                            cols = min(512, N - g * 512)
                            mm(ps[:, g, 0:cols], p3_ohd[k], p3_ohs[k][:, g * 512:g * 512 + cols],
                               start=False, stop=False, skip_group_check=True)
                        pe.wait_ge(S("oh3"), b * U + (2 * U + k + 1))
                        pe.wait_ge(S("ohr3"), b * U + (k + 1))
                        mm(ps[:, 7, 0:4 * D], p3_oh[k], p3_mm[k], start=False, stop=False, skip_group_check=True
                           ).then_inc(S("slot3_free"), 1)
                mm(ps[:, 7, 0:2], p3_z[:, 0:P], p3_z[:, 0:2], start=False, stop=True, skip_group_check=True
                   ).then_inc(S("win3"), 1)
            barrier(pe, 3)
            pe.wait_ge(S("x_ready"), 1)
            x_transposes(1)
            for w in range(NW):
                if w >= 2:
                    pe.wait_ge(S("sc_used"), w - 1)
                    pe.wait_ge(S("hw_out"), w - 1)
                for a in range(2):
                    last = mm(ps[:, 4 + 2 * a + w % 2, 0:H1 * D], xT[:, w * P:(w + 1) * P],
                              w1[:, a, :, :].rearrange("f h o -> f (h o)"))
                last.then_inc(S("node_mm"), 1)
            barrier(pe, 4)
            for w in range(NW):
                pe.wait_ge(S(f"ld_adj{w % 2}"), 16 * (w // 2 + 1))
                for g in range(9):
                    if g < 7:
                        n = 7 * w + g
                        if n >= 4:
                            pe.wait_ge(S("at_out"), n - 3)
                        for c_ in range(g * 4, min(g * 4 + 4, NW)):
                            last = tr(ps[:, n % 4, (c_ % 4) * P:(c_ % 4 + 1) * P],
                                      p5_adj[w % 2][:, c_ * P:(c_ + 1) * P])
                        last.then_inc(S("at_tr"), 1)
                    if g >= 2:
                        gg = g - 2
                        pe.wait_ge(S("at_out"), 7 * w + gg + 1)
                        if gg == 0 and w >= 2:
                            pe.wait_ge(S("z_out"), w - 1)
                        for c_ in range(gg * 4, min(gg * 4 + 4, NW)):
                            last = mm(ps[:, 4 + w % 2, 0:D], p5_at[:, c_ * P:(c_ + 1) * P],
                                      p5_zt[:, c_ * D:(c_ + 1) * D], start=(c_ == 0), stop=(c_ == NW - 1))
                        last.then_inc(S("z_mm"), 1)
            barrier(pe, 5)
            x_transposes(2)
            for w in range(NW):
                if w >= 2:
                    pe.wait_ge(S("self_out"), w - 1)
                mm(ps[:, 4 + w % 2, 0:OK + D], xT[:, w * P:(w + 1) * P], w2n[:, :]).then_inc(S("node_mm"), 1)
            barrier(pe, 6)
            pe.sem_inc(S("xs_tr"), 4)
            pe.sem_inc(S("tp_mm"), 2)
            pe.sem_inc(S("hid_mm"), 1)

            def xs_transpose(j, i):
                pe.wait_ge(S("xs_made"), i + (G + 1))
                pe.wait_ge(S("xl_made"), i + 1)
                o = (j % 2) * 1024
                for c_ in range(XC):
                    last = tr(psf[:, o + c_ * P:o + (c_ + 1) * P], p8_xs[j % 4][:, c_ * P:(c_ + 1) * P])
                last.then_inc(S("xs_tr"), 1)

            def hidden(h, n):
                pe.wait_ge(S("att_low"), n + 1)
                pe.wait_ge(S("hid_out"), n + 1)
                mm(ps[:, 5, :], w1h[:, :], att_r[h], stop=False)
                mm(ps[:, 5, :], w1l[:, :], att_r[h][0:D, :], start=False).then_inc(S("hid_mm"), 1)

            def weights(j):
                h, l = (t[j // U][:, (j % U) * P:(j % U + 1) * P] for t in (hid_h, hid_l))
                out = ps[:, 4, 0:2 * OK]
                mm(out, h, w2h, stop=False)
                mm(out, h, w2l, start=False, stop=False)
                mm(out, l, w2h, start=False, stop=False)
                mm(out, ones_r[:, :], b2r[:, :], start=False).then_inc(S("w_mm"), 1)

            def tensor_product(j, i):
                out = ps[:, 6 + j % 2, 0:2 * OK]
                n = 2 * OK
                high, low = ([t[j % 2][:, c_ * P:(c_ + 1) * P] for c_ in range(XC)] for t in (xh, xl))
                in_a, in_b = ([t[:, c_ * n:(c_ + 1) * n] for c_ in range(XC)] for t in (c_a, c_b))
                pe.wait_ge(S("xt_out"), i + 1)
                pe.wait_ge(S("kv_made"), i + 1)
                for c_ in range(XC):
                    mm(out, high[c_], in_a[c_], start=(c_ == 0), stop=False)
                    if c_ < XC - 1:
                        mm(out, high[c_], in_b[c_], start=False, stop=False)
                pe.wait_ge(S("xl_made"), i + 3)
                for c_ in range(XC - 1):
                    mm(out, low[c_], in_a[c_], start=False, stop=False)
                mm(out, low[XC - 1], in_b[XC - 1], start=False, stop=True).then_inc(S("tp_mm"), 1)

            def pe_tiles(it, last_turn):
                for j in range(G):
                    if not (last_turn and j == G - 1):
                        xs_transpose(j + 1, it * G + (j + 1))
                    if j == 2:
                        hidden(1, it * 2 + 1)
                    if j == 6 and not last_turn:
                        hidden(0, it * 2 + 2)
                    if j % U == 0:
                        pe.wait_ge(S("hid_low"), it * 2 + (j // U + 1))
                    pe.wait_ge(S("w_out"), it * G + j + 1)
                    weights(j)
                    tensor_product(j, it * G + j)

            xs_transpose(0, 0)
            hidden(0, 0)
            with pe.Fori(0, NIT - 1) as it:
                pe_tiles(it, False)
            pe_tiles(NIT - 1, True)
            barrier(pe, 7)
            rows_g = [min(4, NG - 4 * g) for g in range(-(-NG // 4))]
            for g, n in enumerate(rows_g):
                if g >= 2:
                    pe.wait_ge(S("lg_row"), g - 1)
                for c_ in range(n):
                    last = tr(ps[:, g % 2, c_ * P:(c_ + 1) * P], lg[:, (g * 4 + c_) * P:(g * 4 + c_ + 1) * P])
                last.then_inc(S("lg_tr"), 1)
            T = [pS_tr[:, i * P:(i + 1) * P] for i in range(8)]
            for r, cols in enumerate(((0,), (32, 40), (32, 40, 56))):
                pe.wait_ge(S("sc_in"), r + 1)
                for j, c_ in enumerate(cols):
                    last = tr(ps[0:8, 2, j * P:j * P + SCP], pS_l[0:SCP, c_:c_ + 8])
                last.then_inc(S("sc_tr"), 1)
                pe.wait_ge(S("sc_back"), r + 1)
                tr(ps[0:SCP, 3, 0:8], T[2][:, 0:SCP]).then_inc(S("sc_bk"), 1)
            for g, n in enumerate(rows_g):
                pe.wait_ge(S(f"ld_ex{g % 2}"), 16 * (g // 2 + 1))
                if g >= 2:
                    pe.wait_ge(S("ex_col"), g - 1)
                for c_ in range(n):
                    last = tr(ps[:, g % 2, c_ * P:(c_ + 1) * P], pA_row[g % 2][:, c_ * P:(c_ + 1) * P])
                last.then_inc(S("ex_tr"), 1)
            barrier(pe, 8)
            pe.sem_inc(S("slotB_free"), U)
            with pe.Fori(0, NW) as w:
                pe.wait_ge(S("accB"), w + 1)
                mm(ps[:, 0, 0:P], pB_z, pB_z, start=True, stop=False, skip_group_check=True)
                mm(ps[:, 0, P:VW], pB_z, pB_z[:, 0:H2], start=False, stop=False, skip_group_check=True)
                b0 = pe.value_load(blk_i[0:1, ds(w, 1)], min_val=0, max_val=NB)
                b1 = pe.value_load(blk_i[0:1, ds(w + 1, 1)], min_val=1, max_val=NB)
                with pe.Fori(b0, b1) as b:
                    for k in range(U):
                        if k % 2 == 0:
                            pe.wait_ge(S("v_used"), b * 2 + (U + k // 2 + 1))
                        mm(ps[:, 0, 0:VW], pB_oh[:, k, :], pB_vx[:, k, :], start=False, stop=False, skip_group_check=True
                           ).then_inc(S("slotB_free"), 1)
                mm(ps[:, 0, 0:2], pB_z, pB_z[:, 0:2], start=False, stop=True, skip_group_check=True
                   ).then_inc(S("winB"), 1)
            barrier(pe, 9)
            for w in range(NW):
                pe.wait_ge(S("upd"), w + 1)
                if w >= 2:
                    pe.wait_ge(S("u_out"), w - 1)
                tr(ps[:, w % 2, 0:P], pB_acc[:, w * VW:w * VW + OK]).then_inc(S("u_tr"), 1)
                pe.wait_ge(S("u_out"), w + 1)
                if w >= 2:
                    pe.wait_ge(S("u_add"), w - 1)
                mm(ps[:, 2 + w % 2, 0:D], pB_uT[w % 2], wout[:, :]).then_inc(S("node_mm"), 1)
            for r in range(2):
                pe.wait_ge(S("bn_in"), r + 1)
                mm(ps[:, 4, 0:D], ones[:, :], pB_n[:, 0:D]).then_inc(S("bn_mm"), 1)
            barrier(pe, 10)
            tr(ps[0:D, 6, 0:D], w3[:, :]).then_inc(S("w3_tr"), 1)
            x_transposes(3)
            pe.wait_ge(S("w3_out"), 1)
            for w in range(NW):
                if w >= 2:
                    pe.wait_ge(S("u_add"), NW + w - 1)
                mm(ps[:, 4 + w % 2, 0:D], xT[:, w * P:(w + 1) * P], w3T[:, :]).then_inc(S("node_mm"), 1)
            pe.wait_ge(S("g_ready"), 1)
            for w in range(NW):
                pe.wait_ge(S(f"ld_adj{w % 2}"), 16 * (w // 2 + 1 + 13 - w % 2))
                for g in range(7):
                    cols = min(512, N - g * 512)
                    last = mm(ps[0:D, g, 0:cols], t1[:, w, :], pD_adj[w % 2][:, g * 512:g * 512 + cols],
                              start=(w == 0), stop=(w == NW - 1))
                last.then_inc(S("out_mm"), 1)
            pe.wait_ge(S("oT"), 1)
            pe.wait_ge(S("oT_zero"), 1)
            for w in range(NW):
                if w >= 4:
                    pe.wait_ge(S("u_out"), NW + w - 3)
                tr(ps[:, w % 4, 0:D], pD_oT[:, w * P:(w + 1) * P]).then_inc(S("u_tr"), 1)


def kernel(**inputs):
    import concourse.bacc as _bacc
    from concourse.bass_utils import run_bass_kernel_spmd as _run

    nc = _bacc.Bacc("TRN2", target_bir_lowering=False, num_devices=1)
    arrays, args = {}, {}
    given = {}
    for name, a in inputs.items():
        a = np.ascontiguousarray(a)
        if name in _ROWS:
            fill = NP if name == "dst" else 0
            rows = np.concatenate([a, np.full((NTR * P - E,), fill, a.dtype)]).reshape(NTR, P)
            given[name] = rows
            given[name + "_cols"] = np.ascontiguousarray(rows[0:NT].T)
        elif name.startswith("edge_attr"):
            a = np.concatenate([a, np.zeros((NT * P - E, a.shape[1]), a.dtype)])
            if name == "edge_attr_64":
                a = a.reshape(NT // U, U * P, D).transpose(0, 2, 1)
            else:
                a = a.reshape(NT, P, S9).transpose(1, 0, 2)
                a = np.concatenate([a, a[:, :, S9 - 1:S9]], axis=2)
            given[name] = np.ascontiguousarray(a)
        else:
            given[name] = a
    for name, a in given.items():
        arrays["in_" + name] = a
        args[name] = nc.dram_tensor("in_" + name, a.shape, mybir.dt.from_np(a.dtype), kind="ExternalInput").ap()
    out = nc.dram_tensor("out", (N, D), mybir.dt.float32, kind="ExternalOutput").ap()
    build(nc, args, out)
    return _run(nc, [arrays], core_ids=[0]).results[0]["out"]
```
